# Optimizing a Trainium2 kernel written in Bass

```python
import numpy as np
import jax
import jax.numpy as jnp

def _softmax(x, axis=-1):
    return jax.nn.softmax(x, axis=axis)

def _gelu(x):
    return jax.nn.gelu(x, approximate=True)

def _silu(x):
    return jax.nn.silu(x)

def _sigmoid(x):
    return jax.nn.sigmoid(x)

def _layernorm(x, axis=-1, eps=1e-05):
    m = jnp.mean(x, axis=axis, keepdims=True)
    v = jnp.var(x, axis=axis, keepdims=True)
    return (x - m) / jnp.sqrt(v + eps)

def _scatter_add(tgt, idx, src, axis=0):
    return tgt.at[idx].add(src)

def _segment_sum(src, seg, n):
    return jax.ops.segment_sum(src, seg, n)
kernel_name = 'mk_vit_tower_d4_tok_img768_r4_2c067c'

def setup_inputs(seed: int=0):
    np.random.seed(seed)
    _w = jnp.asarray

    def _rec_inputs():
        import jax
        import jax.numpy as jnp
        _rk = jax.random.key(seed)
        x = -0.000596345 + 1.00056 * jax.random.normal(jax.random.fold_in(_rk, 1), (4, 3, 64, 64), jnp.float32)
        return x
    x = _rec_inputs()

    def _L0_tok_setup():
        import jax, jax.numpy as jnp
        import numpy as np
        B = 16
        IMG = 64
        CH = 3
        EMBED = 64
        GP = 16
        PRE = [1, 2, 4]
        N_LEVELS = 3
        FUSED = EMBED * N_LEVELS

        def hilbert_flat_indices(n):
            t = np.arange(n * n, dtype=np.int64)
            x = np.zeros(n * n, dtype=np.int64)
            y = np.zeros(n * n, dtype=np.int64)
            s = 1
            while s < n:
                rx = 1 & t // 2
                ry = 1 & (t ^ rx)
                swap = ry == 0
                flip = swap & (rx == 1)
                x = np.where(flip, s - 1 - x, x)
                y = np.where(flip, s - 1 - y, y)
                x2 = np.where(swap, y, x)
                y2 = np.where(swap, x, y)
                x, y = (x2, y2)
                x = x + s * rx
                y = y + s * ry
                t = t // 4
                s *= 2
            return y * n + x

        def _level(x, idx, W, b, p, gp):
            Bsz, C, H, _ = x.shape
            h = H // p
            t = x.reshape(Bsz, C, h, p, h, p).transpose(0, 2, 4, 3, 5, 1).reshape(Bsz, h * h, p * p * C)
            t = t[:, idx]
            t = t.reshape(Bsz, h * h // gp, gp * p * p * C)
            return t @ W.T + b

        def _interp_linear(x, n_out):
            L = x.shape[1]
            pos = (jnp.arange(n_out, dtype=jnp.float32) + 0.5) * (L / n_out) - 0.5
            pos = jnp.clip(pos, 0.0, L - 1)
            i0 = jnp.floor(pos).astype(jnp.int32)
            i1 = jnp.minimum(i0 + 1, L - 1)
            w = (pos - i0).astype(x.dtype)
            return x[:, i0] * (1.0 - w)[None, :, None] + x[:, i1] * w[None, :, None]
        key = jax.random.key(seed)
        ks = jax.random.split(key, 9)
        inp = {'x': jax.random.normal(ks[0], (B, CH, IMG, IMG), jnp.float32)}
        for i, p in enumerate(PRE):
            din = CH * p * p * GP
            inp[f'W{i}'] = jax.random.normal(ks[1 + 2 * i], (EMBED, din), jnp.float32) * din ** (-0.5)
            inp[f'b{i}'] = jax.random.normal(ks[2 + 2 * i], (EMBED,), jnp.float32) * 0.02
        inp['Wf'] = jax.random.normal(ks[7], (FUSED, FUSED), jnp.float32) * FUSED ** (-0.5)
        inp['bf'] = jax.random.normal(ks[8], (FUSED,), jnp.float32) * 0.02
        for i, p in enumerate(PRE):
            inp[f'idx{i}'] = jnp.asarray(hilbert_flat_indices(IMG // p), jnp.int32)
        return inp
    _L0_tok_all = _L0_tok_setup()
    _L0_tok_in = {k: v for k, v in _L0_tok_all.items() if k in ('W0', 'b0', 'W1', 'b1', 'W2', 'b2', 'Wf', 'bf', 'idx0', 'idx1', 'idx2')}
    del _L0_tok_all

    def _L0_attn_setup():
        import jax, jax.numpy as jnp
        import numpy as np
        from jax import lax
        H = 192
        I = 384
        N = 16
        R = 48
        K = 4
        NL = 16
        B, L = (2, 256)
        EPS = 1e-05

        def rmsnorm(x, w):
            return x * lax.rsqrt(jnp.mean(x * x, axis=-1, keepdims=True) + EPS) * w

        def causal_conv(u, w, b):
            uc = jnp.swapaxes(u, 1, 2)
            y = lax.conv_general_dilated(uc, w, (1,), [(K - 1, 0)], dimension_numbers=('NCH', 'OIH', 'NCH'), feature_group_count=I)
            return jnp.swapaxes(y + b[None, :, None], 1, 2)

        def selective_scan(u, dt, A, Bm, Cm, Dp):

            def step(h, inp):
                u_t, dt_t, B_t, C_t = inp
                dA = jnp.exp(dt_t[:, :, None] * A)
                h = dA * h + (dt_t * u_t)[:, :, None] * B_t[:, None, :]
                y = jnp.einsum('bin,bn->bi', h, C_t)
                return (h, y)
            inputs = tuple((jnp.moveaxis(a, 1, 0) for a in (u, dt, Bm, Cm)))
            h0 = jnp.zeros((u.shape[0],) + A.shape, u.dtype)
            _, ys = lax.scan(step, h0, inputs)
            return jnp.moveaxis(ys, 0, 1) + u * Dp

        def mamba_layer(x, p):
            in_w, cw, cb, xp_w, dtw, dtb, a_log, dp, ow, nw = p
            h = rmsnorm(x, nw)
            xz = jnp.einsum('blh,ch->blc', h, in_w)
            u, z = jnp.split(xz, 2, axis=-1)
            u = jax.nn.silu(causal_conv(u, cw, cb))
            proj = jnp.einsum('bli,ci->blc', u, xp_w)
            dt_r, Bm, Cm = (proj[..., :R], proj[..., R:R + N], proj[..., R + N:])
            dt = jax.nn.softplus(jnp.einsum('blr,ir->bli', dt_r, dtw) + dtb)
            A = -jnp.exp(a_log)
            y = selective_scan(u, dt, A, Bm, Cm, dp)
            y = y * jax.nn.silu(z)
            return x + jnp.einsum('bli,hi->blh', y, ow)
        key = jax.random.key(seed)
        ks = jax.random.split(key, 8)
        s = 0.02
        x = jax.random.normal(ks[0], (B, L, H), jnp.float32)
        in_proj_w = jax.random.normal(ks[1], (NL, 2 * I, H), jnp.float32) * s
        conv_w = jax.random.normal(ks[2], (NL, I, 1, K), jnp.float32) * 0.1
        conv_b = jnp.zeros((NL, I), jnp.float32)
        x_proj_w = jax.random.normal(ks[3], (NL, R + 2 * N, I), jnp.float32) * s
        dt_proj_w = jax.random.normal(ks[4], (NL, I, R), jnp.float32) * 0.01
        dt_proj_b = -4.0 + 0.1 * jax.random.normal(ks[5], (NL, I), jnp.float32)
        A_log = jnp.log(jnp.tile(jnp.arange(1, N + 1, dtype=jnp.float32), (NL, I, 1)))
        D = jnp.ones((NL, I), jnp.float32)
        out_proj_w = jax.random.normal(ks[6], (NL, H, I), jnp.float32) * s
        norm_w = jnp.ones((NL, H), jnp.float32)
        final_norm_w = jnp.ones((H,), jnp.float32)
        return {'x': x, 'in_proj_w': in_proj_w, 'conv_w': conv_w, 'conv_b': conv_b, 'x_proj_w': x_proj_w, 'dt_proj_w': dt_proj_w, 'dt_proj_b': dt_proj_b, 'A_log': A_log, 'D': D, 'out_proj_w': out_proj_w, 'norm_w': norm_w, 'final_norm_w': final_norm_w}
    _L0_attn_all = _L0_attn_setup()
    _L0_attn_in = {k: v for k, v in _L0_attn_all.items() if k in ('in_proj_w', 'conv_w', 'conv_b', 'x_proj_w', 'dt_proj_w', 'dt_proj_b', 'A_log', 'D', 'out_proj_w', 'norm_w', 'final_norm_w')}
    del _L0_attn_all

    def _L0_ffn_setup():
        import jax, jax.numpy as jnp
        import numpy as np
        D_MODEL = 192
        N_EXPERTS = 16
        TOP_K = 2
        D_FF = 4 * D_MODEL
        B, L = (4, 512)
        key = jax.random.key(seed)
        ks = jax.random.split(key, 6)
        s_in = 1.0 / np.sqrt(D_MODEL)
        s_ff = 1.0 / np.sqrt(D_FF)
        x = jax.random.normal(ks[0], (B, L, D_MODEL), dtype=jnp.float32)
        Wr = jax.random.uniform(ks[1], (N_EXPERTS, D_MODEL), jnp.float32, -s_in, s_in)
        W1 = jax.random.uniform(ks[2], (N_EXPERTS, D_MODEL, D_FF), jnp.float32, -s_in, s_in)
        b1 = jax.random.uniform(ks[3], (N_EXPERTS, D_FF), jnp.float32, -s_in, s_in)
        W2 = jax.random.uniform(ks[4], (N_EXPERTS, D_FF, D_MODEL), jnp.float32, -s_ff, s_ff)
        b2 = jax.random.uniform(ks[5], (N_EXPERTS, D_MODEL), jnp.float32, -s_ff, s_ff)
        return {'x': x, 'Wr': Wr, 'W1': W1, 'b1': b1, 'W2': W2, 'b2': b2}
    _L0_ffn_all = _L0_ffn_setup()
    _L0_ffn_in = {k: v for k, v in _L0_ffn_all.items() if k in ('Wr', 'W1', 'b1', 'W2', 'b2')}
    del _L0_ffn_all

    def _L1_attn_setup():
        import jax, jax.numpy as jnp
        import numpy as np
        D_MODEL = 192
        DT_RANK = D_MODEL // 16
        D_CONV = 4
        D_INNER = 2 * D_MODEL
        D_STATE = 16
        BATCH, SEQ_LEN = (1, 1024)

        def _silu(x):
            return x * jax.nn.sigmoid(x)
        key = jax.random.key(seed)
        ks = jax.random.split(key, 11)

        def n(k, shape, scale=0.02):
            return jax.random.normal(k, shape, dtype=jnp.float32) * scale
        return {'u': jax.random.normal(ks[0], (BATCH, SEQ_LEN, D_MODEL), dtype=jnp.float32), 'in_proj_w': n(ks[1], (2 * D_INNER, D_MODEL)), 'conv_w': n(ks[2], (D_INNER, 1, D_CONV)), 'conv_b': n(ks[3], (D_INNER,)), 'x_dt_w': n(ks[4], (DT_RANK, D_INNER)), 'x_b_w': n(ks[5], (D_STATE, D_INNER)), 'x_c_w': n(ks[6], (D_STATE, D_INNER)), 'dt_w': n(ks[7], (D_INNER, DT_RANK)), 'dt_b': n(ks[8], (D_INNER,)), 'A_log': jnp.log(jnp.tile(jnp.arange(1, D_STATE + 1, dtype=jnp.float32), (D_INNER, 1))), 'D_param': jnp.ones((D_INNER,), dtype=jnp.float32), 'out_proj_w': n(ks[9], (D_MODEL, D_INNER))}
    _L1_attn_all = _L1_attn_setup()
    _L1_attn_in = {k: v for k, v in _L1_attn_all.items() if k in ('in_proj_w', 'conv_w', 'conv_b', 'x_dt_w', 'x_b_w', 'x_c_w', 'dt_w', 'dt_b', 'A_log', 'D_param', 'out_proj_w')}
    del _L1_attn_all

    def _L1_ffn_setup():
        import jax, jax.numpy as jnp
        import numpy as np
        B, S, D = (2, 256, 192)
        I = 96
        E = 8
        G = 4
        TOPK_GROUPS = 2
        K = 2
        ROUTE_SCALE = 1.0
        ALPHA, LIMIT = (1.702, 7.0)

        def swiglu(h):
            xg = jnp.minimum(h[..., ::2], LIMIT)
            xl = jnp.clip(h[..., 1::2], -LIMIT, LIMIT)
            return xg * jax.nn.sigmoid(ALPHA * xg) * (xl + 1.0)

        def gate(x, gate_w, gate_b):
            scores = jax.nn.softmax(jnp.einsum('td,ed->te', x, gate_w).astype(jnp.float32), axis=-1)
            original_scores = scores
            s = scores + gate_b
            T = x.shape[0]
            sg = s.reshape(T, G, E // G)
            group_scores = jnp.sum(jax.lax.top_k(sg, 2)[0], axis=-1)
            _, gidx = jax.lax.top_k(group_scores, TOPK_GROUPS)
            keep = jnp.any(jax.nn.one_hot(gidx, G, dtype=jnp.bool_), axis=1)
            sg = jnp.where(keep[:, :, None], sg, -jnp.inf)
            s = sg.reshape(T, E)
            _, idx = jax.lax.top_k(s, K)
            w = jnp.take_along_axis(original_scores, idx, axis=1) * ROUTE_SCALE
            return (w.astype(x.dtype), idx)

        def expert_ffn(x, W1, B1, W3, B3, W2, B2):
            h1 = jnp.einsum('td,edh->teh', x, W1) + B1
            h3 = jnp.einsum('td,edh->teh', x, W3) + B3
            g = swiglu(h1 * h3)
            return jnp.einsum('tei,eid->ted', g, W2) + B2

        def shared_ffn(x, Ws1, Bs1, Ws3, Bs3, Ws2, Bs2):
            h = (x @ Ws1 + Bs1) * (x @ Ws3 + Bs3)
            return swiglu(h) @ Ws2 + Bs2
        key = jax.random.key(seed)
        ks = jax.random.split(key, 16)
        sc = 0.02
        inp = {'x': jax.random.normal(ks[0], (B, S, D), jnp.float32), 'gate_w': jax.random.normal(ks[1], (E, D), jnp.float32) * sc, 'gate_b': jax.random.normal(ks[2], (E,), jnp.float32) * sc, 'W1': jax.random.normal(ks[3], (E, D, 2 * I), jnp.float32) * sc, 'B1': jax.random.normal(ks[4], (E, 2 * I), jnp.float32) * sc, 'W3': jax.random.normal(ks[5], (E, D, 2 * I), jnp.float32) * sc, 'B3': jax.random.normal(ks[6], (E, 2 * I), jnp.float32) * sc, 'W2': jax.random.normal(ks[7], (E, I, D), jnp.float32) * sc, 'B2': jax.random.normal(ks[8], (E, D), jnp.float32) * sc, 'Ws1': jax.random.normal(ks[9], (D, 2 * I), jnp.float32) * sc, 'Bs1': jax.random.normal(ks[10], (2 * I,), jnp.float32) * sc, 'Ws3': jax.random.normal(ks[11], (D, 2 * I), jnp.float32) * sc, 'Bs3': jax.random.normal(ks[12], (2 * I,), jnp.float32) * sc, 'Ws2': jax.random.normal(ks[13], (I, D), jnp.float32) * sc, 'Bs2': jax.random.normal(ks[14], (D,), jnp.float32) * sc}
        return inp
    _L1_ffn_all = _L1_ffn_setup()
    _L1_ffn_in = {k: v for k, v in _L1_ffn_all.items() if k in ('gate_w', 'gate_b', 'W1', 'B1', 'W3', 'B3', 'W2', 'B2', 'Ws1', 'Bs1', 'Ws3', 'Bs3', 'Ws2', 'Bs2')}
    del _L1_ffn_all

    def _L2_attn_setup():
        import math
        import jax, jax.numpy as jnp
        import numpy as np
        D_MODEL = 192
        N_HEAD = 12
        HEAD_DIM = D_MODEL // N_HEAD
        ROPE_BASE = 10000.0
        EPS = 1e-06

        def rotary_cache(seq_len, head_dim, base=ROPE_BASE):
            half = head_dim // 2
            freq = 1.0 / base ** (jnp.arange(half, dtype=jnp.float32) / half)
            freqs = jnp.arange(seq_len, dtype=jnp.float32)[:, None] * freq[None, :]
            return (jnp.cos(freqs), jnp.sin(freqs))

        def apply_rope(x, cos, sin):
            cos = cos.astype(x.dtype)
            sin = sin.astype(x.dtype)
            x1 = x[..., ::2]
            x2 = x[..., 1::2]
            out = jnp.stack((x1 * cos - x2 * sin, x1 * sin + x2 * cos), axis=-1)
            return out.reshape(x.shape)
        key = jax.random.key(seed)
        kx, kq, kk, kv, kp = jax.random.split(key, 5)
        B, S, D = (2, 512, D_MODEL)
        x = jax.random.normal(kx, (B, S, D), dtype=jnp.float32)
        scale = 0.02
        Wq = jax.random.normal(kq, (D, D), dtype=jnp.float32) * scale
        Wk = jax.random.normal(kk, (D, D), dtype=jnp.float32) * scale
        Wv = jax.random.normal(kv, (D, D), dtype=jnp.float32) * scale
        Wproj = jax.random.normal(kp, (D, D), dtype=jnp.float32) * scale
        return {'x': x, 'Wq': Wq, 'Wk': Wk, 'Wv': Wv, 'Wproj': Wproj}
    _L2_attn_all = _L2_attn_setup()
    _L2_attn_in = {k: v for k, v in _L2_attn_all.items() if k in ('Wq', 'Wk', 'Wv', 'Wproj')}
    del _L2_attn_all

    def _L2_ffn_setup():
        import jax, jax.numpy as jnp
        import numpy as np
        B, S, D = (2, 256, 192)
        NF, NR, R, DS, K = (128, 128, 128, 64, 4)

        @jax.checkpoint
        def feature_fn(x, neurons, weights):
            all_h = jnp.einsum('bsd,ndr->bsnr', x, neurons)
            return jnp.einsum('bsnr,bsn->bsr', all_h, weights)

        @jax.checkpoint
        def restore_fn(h, neurons, weights):
            all_out = jnp.einsum('bsr,nrd->bsnd', h, neurons)
            return jnp.einsum('bsnd,bsn->bsd', all_out, weights)

        def topk_sparsify(weights, k):
            topk_vals, topk_idx = jax.lax.top_k(weights, k)
            N = weights.shape[-1]
            one_hot_mask = jax.nn.one_hot(topk_idx, N, dtype=weights.dtype)
            sparse = (one_hot_mask * topk_vals[..., jnp.newaxis]).sum(axis=-2)
            sparse = sparse / (sparse.sum(axis=-1, keepdims=True) + 1e-08)
            return (sparse, topk_idx)
        key = jax.random.key(seed)
        ks = jax.random.split(key, 8)
        x = jax.random.normal(ks[0], (B, S, D), jnp.float32)
        f_know = jax.random.normal(ks[1], (NF, D, R), jnp.float32) * 0.02
        r_know = jax.random.normal(ks[2], (NR, R, D), jnp.float32) * 0.02
        W_fk = jax.random.normal(ks[3], (D, DS), jnp.float32) * 0.02
        b_fk = jnp.zeros((DS,), jnp.float32)
        W_rk = jax.random.normal(ks[4], (D, DS), jnp.float32) * 0.02
        b_rk = jnp.zeros((DS,), jnp.float32)
        emb_fk = jax.random.normal(ks[5], (NF, DS), jnp.float32) * 0.02
        emb_rk = jax.random.normal(ks[6], (NR, DS), jnp.float32) * 0.02
        return {'x': x, 'f_know': f_know, 'r_know': r_know, 'W_fk': W_fk, 'b_fk': b_fk, 'W_rk': W_rk, 'b_rk': b_rk, 'emb_fk': emb_fk, 'emb_rk': emb_rk}
    _L2_ffn_all = _L2_ffn_setup()
    _L2_ffn_in = {k: v for k, v in _L2_ffn_all.items() if k in ('f_know', 'r_know', 'W_fk', 'b_fk', 'W_rk', 'b_rk', 'emb_fk', 'emb_rk')}
    del _L2_ffn_all

    def _L3_attn_setup():
        import jax, jax.numpy as jnp
        import numpy as np
        EMBED_DIM = 192
        MAX_LEN = 256
        ALPHA = 0.99
        BATCH = 16

        def _retention_mask(sl, alpha, dtype):
            i = jnp.arange(sl)[:, None]
            j = jnp.arange(sl)[None, :]
            causal = i >= j
            exponent = jnp.where(causal, (i - j).astype(dtype), 0.0)
            decay = jnp.asarray(alpha, dtype) ** exponent
            return jnp.where(causal, decay, jnp.zeros((), dtype))
        key = jax.random.key(seed)
        k1, k2, k3 = jax.random.split(key, 3)
        x = jax.random.normal(k1, (BATCH, MAX_LEN, EMBED_DIM), dtype=jnp.float32)
        scale = 1.0 / np.sqrt(EMBED_DIM)
        W_qkv = jax.random.uniform(k2, (EMBED_DIM, 3 * EMBED_DIM), dtype=jnp.float32, minval=-scale, maxval=scale)
        b_qkv = jax.random.uniform(k3, (3 * EMBED_DIM,), dtype=jnp.float32, minval=-scale, maxval=scale)
        return {'x': x, 'W_qkv': W_qkv, 'b_qkv': b_qkv}
    _L3_attn_all = _L3_attn_setup()
    _L3_attn_in = {k: v for k, v in _L3_attn_all.items() if k in ('W_qkv', 'b_qkv')}
    del _L3_attn_all

    def _L3_ffn_setup():
        import jax, jax.numpy as jnp
        import numpy as np
        B, N, D, E = (2, 512, 192, 8)
        H = 4 * D
        TARGET_SPARSITY = 0.6
        K_KEEP = int(N * (1.0 - TARGET_SPARSITY))
        V_MAX, FEAT_CLAMP, ETA = (3.0, 10.0, 1.0)

        def _bk_gii(v):
            dr, di = (v, jnp.full_like(v, -ETA))

            def cf(reverse):
                init = (jnp.full((v.shape[0],), 1e+18, v.dtype), jnp.zeros((v.shape[0],), v.dtype))

                def step(c, d):
                    ar, ai = c
                    drr, dii = d
                    den = ar * ar + ai * ai
                    out = (drr - ar / den, dii + ai / den)
                    return (out, out)
                _, (r, i) = jax.lax.scan(step, init, (dr.T, di.T), reverse=reverse)
                return (r.T, i.T)
            ar, ai = cf(False)
            br, bi = cf(True)
            cr, ci = (ar + br - dr, ai + bi - di)
            den = cr * cr + ci * ci
            return (cr / den, -ci / den)
        key = jax.random.key(seed)
        ks = jax.random.split(key, 8)
        s = 0.02
        return {'x': jax.random.normal(ks[0], (B, N, D), jnp.float32), 'Wg': jax.random.normal(ks[1], (D, E), jnp.float32) * s, 'bg': jnp.zeros((E,), jnp.float32), 'W1': jax.random.normal(ks[2], (E, D, H), jnp.float32) * s, 'b1': jnp.zeros((E, H), jnp.float32), 'W2': jax.random.normal(ks[3], (E, H, D), jnp.float32) * s, 'b2': jnp.zeros((E, D), jnp.float32), 'Wv': jax.random.normal(ks[4], (D,), jnp.float32) * s, 'bv': jnp.zeros((), jnp.float32), 'Wm': jax.random.normal(ks[5], (D,), jnp.float32) * s, 'bm': jnp.zeros((), jnp.float32), 'Wo': jax.random.normal(ks[6], (2, D), jnp.float32) * s, 'bo': jnp.zeros((D,), jnp.float32), 'bk_scale': jnp.ones((), jnp.float32)}
    _L3_ffn_all = _L3_ffn_setup()
    _L3_ffn_in = {k: v for k, v in _L3_ffn_all.items() if k in ('Wg', 'bg', 'W1', 'b1', 'W2', 'b2', 'Wv', 'bv', 'Wm', 'bm', 'Wo', 'bo', 'bk_scale')}
    del _L3_ffn_all
    return {'x': x, 'L0_tok_W0': _L0_tok_in['W0'], 'L0_tok_b0': _L0_tok_in['b0'], 'L0_tok_W1': _L0_tok_in['W1'], 'L0_tok_b1': _L0_tok_in['b1'], 'L0_tok_W2': _L0_tok_in['W2'], 'L0_tok_b2': _L0_tok_in['b2'], 'L0_tok_Wf': _L0_tok_in['Wf'], 'L0_tok_bf': _L0_tok_in['bf'], 'L0_tok_idx0': _L0_tok_in['idx0'], 'L0_tok_idx1': _L0_tok_in['idx1'], 'L0_tok_idx2': _L0_tok_in['idx2'], 'L0_attn_in_proj_w': _L0_attn_in['in_proj_w'], 'L0_attn_conv_w': _L0_attn_in['conv_w'], 'L0_attn_conv_b': _L0_attn_in['conv_b'], 'L0_attn_x_proj_w': _L0_attn_in['x_proj_w'], 'L0_attn_dt_proj_w': _L0_attn_in['dt_proj_w'], 'L0_attn_dt_proj_b': _L0_attn_in['dt_proj_b'], 'L0_attn_A_log': _L0_attn_in['A_log'], 'L0_attn_D': _L0_attn_in['D'], 'L0_attn_out_proj_w': _L0_attn_in['out_proj_w'], 'L0_attn_norm_w': _L0_attn_in['norm_w'], 'L0_attn_final_norm_w': _L0_attn_in['final_norm_w'], 'L0_ffn_Wr': _L0_ffn_in['Wr'], 'L0_ffn_W1': _L0_ffn_in['W1'], 'L0_ffn_b1': _L0_ffn_in['b1'], 'L0_ffn_W2': _L0_ffn_in['W2'], 'L0_ffn_b2': _L0_ffn_in['b2'], 'L1_attn_in_proj_w': _L1_attn_in['in_proj_w'], 'L1_attn_conv_w': _L1_attn_in['conv_w'], 'L1_attn_conv_b': _L1_attn_in['conv_b'], 'L1_attn_x_dt_w': _L1_attn_in['x_dt_w'], 'L1_attn_x_b_w': _L1_attn_in['x_b_w'], 'L1_attn_x_c_w': _L1_attn_in['x_c_w'], 'L1_attn_dt_w': _L1_attn_in['dt_w'], 'L1_attn_dt_b': _L1_attn_in['dt_b'], 'L1_attn_A_log': _L1_attn_in['A_log'], 'L1_attn_D_param': _L1_attn_in['D_param'], 'L1_attn_out_proj_w': _L1_attn_in['out_proj_w'], 'L1_ffn_gate_w': _L1_ffn_in['gate_w'], 'L1_ffn_gate_b': _L1_ffn_in['gate_b'], 'L1_ffn_W1': _L1_ffn_in['W1'], 'L1_ffn_B1': _L1_ffn_in['B1'], 'L1_ffn_W3': _L1_ffn_in['W3'], 'L1_ffn_B3': _L1_ffn_in['B3'], 'L1_ffn_W2': _L1_ffn_in['W2'], 'L1_ffn_B2': _L1_ffn_in['B2'], 'L1_ffn_Ws1': _L1_ffn_in['Ws1'], 'L1_ffn_Bs1': _L1_ffn_in['Bs1'], 'L1_ffn_Ws3': _L1_ffn_in['Ws3'], 'L1_ffn_Bs3': _L1_ffn_in['Bs3'], 'L1_ffn_Ws2': _L1_ffn_in['Ws2'], 'L1_ffn_Bs2': _L1_ffn_in['Bs2'], 'L2_attn_Wq': _L2_attn_in['Wq'], 'L2_attn_Wk': _L2_attn_in['Wk'], 'L2_attn_Wv': _L2_attn_in['Wv'], 'L2_attn_Wproj': _L2_attn_in['Wproj'], 'L2_ffn_f_know': _L2_ffn_in['f_know'], 'L2_ffn_r_know': _L2_ffn_in['r_know'], 'L2_ffn_W_fk': _L2_ffn_in['W_fk'], 'L2_ffn_b_fk': _L2_ffn_in['b_fk'], 'L2_ffn_W_rk': _L2_ffn_in['W_rk'], 'L2_ffn_b_rk': _L2_ffn_in['b_rk'], 'L2_ffn_emb_fk': _L2_ffn_in['emb_fk'], 'L2_ffn_emb_rk': _L2_ffn_in['emb_rk'], 'L3_attn_W_qkv': _L3_attn_in['W_qkv'], 'L3_attn_b_qkv': _L3_attn_in['b_qkv'], 'L3_ffn_Wg': _L3_ffn_in['Wg'], 'L3_ffn_bg': _L3_ffn_in['bg'], 'L3_ffn_W1': _L3_ffn_in['W1'], 'L3_ffn_b1': _L3_ffn_in['b1'], 'L3_ffn_W2': _L3_ffn_in['W2'], 'L3_ffn_b2': _L3_ffn_in['b2'], 'L3_ffn_Wv': _L3_ffn_in['Wv'], 'L3_ffn_bv': _L3_ffn_in['bv'], 'L3_ffn_Wm': _L3_ffn_in['Wm'], 'L3_ffn_bm': _L3_ffn_in['bm'], 'L3_ffn_Wo': _L3_ffn_in['Wo'], 'L3_ffn_bo': _L3_ffn_in['bo'], 'L3_ffn_bk_scale': _L3_ffn_in['bk_scale']}

def reference(x, L0_tok_W0, L0_tok_b0, L0_tok_W1, L0_tok_b1, L0_tok_W2, L0_tok_b2, L0_tok_Wf, L0_tok_bf, L0_tok_idx0, L0_tok_idx1, L0_tok_idx2, L0_attn_in_proj_w, L0_attn_conv_w, L0_attn_conv_b, L0_attn_x_proj_w, L0_attn_dt_proj_w, L0_attn_dt_proj_b, L0_attn_A_log, L0_attn_D, L0_attn_out_proj_w, L0_attn_norm_w, L0_attn_final_norm_w, L0_ffn_Wr, L0_ffn_W1, L0_ffn_b1, L0_ffn_W2, L0_ffn_b2, L1_attn_in_proj_w, L1_attn_conv_w, L1_attn_conv_b, L1_attn_x_dt_w, L1_attn_x_b_w, L1_attn_x_c_w, L1_attn_dt_w, L1_attn_dt_b, L1_attn_A_log, L1_attn_D_param, L1_attn_out_proj_w, L1_ffn_gate_w, L1_ffn_gate_b, L1_ffn_W1, L1_ffn_B1, L1_ffn_W3, L1_ffn_B3, L1_ffn_W2, L1_ffn_B2, L1_ffn_Ws1, L1_ffn_Bs1, L1_ffn_Ws3, L1_ffn_Bs3, L1_ffn_Ws2, L1_ffn_Bs2, L2_attn_Wq, L2_attn_Wk, L2_attn_Wv, L2_attn_Wproj, L2_ffn_f_know, L2_ffn_r_know, L2_ffn_W_fk, L2_ffn_b_fk, L2_ffn_W_rk, L2_ffn_b_rk, L2_ffn_emb_fk, L2_ffn_emb_rk, L3_attn_W_qkv, L3_attn_b_qkv, L3_ffn_Wg, L3_ffn_bg, L3_ffn_W1, L3_ffn_b1, L3_ffn_W2, L3_ffn_b2, L3_ffn_Wv, L3_ffn_bv, L3_ffn_Wm, L3_ffn_bm, L3_ffn_Wo, L3_ffn_bo, L3_ffn_bk_scale):
    import jax
    import jax.numpy as jnp

    def _L0_tok_ref(x, W0, b0, W1, b1, W2, b2, Wf, bf, idx0, idx1, idx2):
        import jax, jax.numpy as jnp
        import numpy as np
        B = 16
        IMG = 64
        CH = 3
        EMBED = 64
        GP = 16
        PRE = [1, 2, 4]
        N_LEVELS = 3
        FUSED = EMBED * N_LEVELS

        def hilbert_flat_indices(n):
            t = np.arange(n * n, dtype=np.int64)
            x = np.zeros(n * n, dtype=np.int64)
            y = np.zeros(n * n, dtype=np.int64)
            s = 1
            while s < n:
                rx = 1 & t // 2
                ry = 1 & (t ^ rx)
                swap = ry == 0
                flip = swap & (rx == 1)
                x = np.where(flip, s - 1 - x, x)
                y = np.where(flip, s - 1 - y, y)
                x2 = np.where(swap, y, x)
                y2 = np.where(swap, x, y)
                x, y = (x2, y2)
                x = x + s * rx
                y = y + s * ry
                t = t // 4
                s *= 2
            return y * n + x

        def _level(x, idx, W, b, p, gp):
            Bsz, C, H, _ = x.shape
            h = H // p
            t = x.reshape(Bsz, C, h, p, h, p).transpose(0, 2, 4, 3, 5, 1).reshape(Bsz, h * h, p * p * C)
            t = t[:, idx]
            t = t.reshape(Bsz, h * h // gp, gp * p * p * C)
            return t @ W.T + b

        def _interp_linear(x, n_out):
            L = x.shape[1]
            pos = (jnp.arange(n_out, dtype=jnp.float32) + 0.5) * (L / n_out) - 0.5
            pos = jnp.clip(pos, 0.0, L - 1)
            i0 = jnp.floor(pos).astype(jnp.int32)
            i1 = jnp.minimum(i0 + 1, L - 1)
            w = (pos - i0).astype(x.dtype)
            return x[:, i0] * (1.0 - w)[None, :, None] + x[:, i1] * w[None, :, None]
        Ws = [(idx0, W0, b0, PRE[0]), (idx1, W1, b1, PRE[1]), (idx2, W2, b2, PRE[2])]
        outs = [_level(x, idx, W, b, p, GP) for idx, W, b, p in Ws]
        n_tokens = outs[0].shape[1]
        outs = [outs[0]] + [_interp_linear(o, n_tokens) for o in outs[1:]]
        y = jnp.concatenate(outs, axis=-1)
        return y @ Wf.T + bf

    def _L0_attn_ref(x, in_proj_w, conv_w, conv_b, x_proj_w, dt_proj_w, dt_proj_b, A_log, D, out_proj_w, norm_w, final_norm_w):
        import jax, jax.numpy as jnp
        import numpy as np
        from jax import lax
        H = 192
        I = 384
        N = 16
        R = 48
        K = 4
        NL = 16
        B, L = (2, 256)
        EPS = 1e-05

        def rmsnorm(x, w):
            return x * lax.rsqrt(jnp.mean(x * x, axis=-1, keepdims=True) + EPS) * w

        def causal_conv(u, w, b):
            uc = jnp.swapaxes(u, 1, 2)
            y = lax.conv_general_dilated(uc, w, (1,), [(K - 1, 0)], dimension_numbers=('NCH', 'OIH', 'NCH'), feature_group_count=I)
            return jnp.swapaxes(y + b[None, :, None], 1, 2)

        def selective_scan(u, dt, A, Bm, Cm, Dp):

            def step(h, inp):
                u_t, dt_t, B_t, C_t = inp
                dA = jnp.exp(dt_t[:, :, None] * A)
                h = dA * h + (dt_t * u_t)[:, :, None] * B_t[:, None, :]
                y = jnp.einsum('bin,bn->bi', h, C_t)
                return (h, y)
            inputs = tuple((jnp.moveaxis(a, 1, 0) for a in (u, dt, Bm, Cm)))
            h0 = jnp.zeros((u.shape[0],) + A.shape, u.dtype)
            _, ys = lax.scan(step, h0, inputs)
            return jnp.moveaxis(ys, 0, 1) + u * Dp

        def mamba_layer(x, p):
            in_w, cw, cb, xp_w, dtw, dtb, a_log, dp, ow, nw = p
            h = rmsnorm(x, nw)
            xz = jnp.einsum('blh,ch->blc', h, in_w)
            u, z = jnp.split(xz, 2, axis=-1)
            u = jax.nn.silu(causal_conv(u, cw, cb))
            proj = jnp.einsum('bli,ci->blc', u, xp_w)
            dt_r, Bm, Cm = (proj[..., :R], proj[..., R:R + N], proj[..., R + N:])
            dt = jax.nn.softplus(jnp.einsum('blr,ir->bli', dt_r, dtw) + dtb)
            A = -jnp.exp(a_log)
            y = selective_scan(u, dt, A, Bm, Cm, dp)
            y = y * jax.nn.silu(z)
            return x + jnp.einsum('bli,hi->blh', y, ow)
        params = (in_proj_w, conv_w, conv_b, x_proj_w, dt_proj_w, dt_proj_b, A_log, D, out_proj_w, norm_w)

        def body(carry, p):
            return (mamba_layer(carry, p), None)
        out, _ = lax.scan(body, x, params)
        return rmsnorm(out, final_norm_w)

    def _L0_ffn_ref(x, Wr, W1, b1, W2, b2):
        import jax, jax.numpy as jnp
        import numpy as np
        D_MODEL = 192
        N_EXPERTS = 16
        TOP_K = 2
        D_FF = 4 * D_MODEL
        B, L = (4, 512)
        logits = jnp.einsum('bld,ed->ble', x, Wr)
        probs = jax.nn.softmax(logits, axis=-1)
        top_p, top_idx = jax.lax.top_k(probs, TOP_K)
        gating = jnp.sum(jax.nn.one_hot(top_idx, N_EXPERTS, dtype=probs.dtype) * top_p[..., None], axis=-2)
        gate_e = jnp.moveaxis(gating, -1, 0)

        def step(y, params):
            W1e, b1e, W2e, b2e, ge = params
            h = jax.nn.gelu(jnp.einsum('bld,df->blf', x, W1e) + b1e, approximate=False)
            out = jnp.einsum('blf,fd->bld', h, W2e) + b2e
            return (y + ge[..., None] * out, None)
        y0 = jnp.zeros_like(x)
        y, _ = jax.lax.scan(step, y0, (W1, b1, W2, b2, gate_e))
        return x + y

    def _L1_attn_ref(u, in_proj_w, conv_w, conv_b, x_dt_w, x_b_w, x_c_w, dt_w, dt_b, A_log, D_param, out_proj_w):
        import jax, jax.numpy as jnp
        import numpy as np
        D_MODEL = 192
        DT_RANK = D_MODEL // 16
        D_CONV = 4
        D_INNER = 2 * D_MODEL
        D_STATE = 16
        BATCH, SEQ_LEN = (1, 1024)

        def _silu(x):
            return x * jax.nn.sigmoid(x)
        batch = u.shape[0]
        xz = u @ in_proj_w.T
        x, z = jnp.split(xz, 2, axis=-1)
        x_ncl = jnp.transpose(x, (0, 2, 1))
        x_conv = jax.lax.conv_general_dilated(x_ncl, conv_w, window_strides=(1,), padding=[(D_CONV - 1, 0)], dimension_numbers=('NCH', 'OIH', 'NCH'), feature_group_count=D_INNER)
        x_conv = x_conv + conv_b[None, :, None]
        x_conv = _silu(jnp.transpose(x_conv, (0, 2, 1)))
        dt_rank = x_conv @ x_dt_w.T
        Bm = x_conv @ x_b_w.T
        Cm = x_conv @ x_c_w.T
        dt = jax.nn.softplus(dt_rank @ dt_w.T + dt_b)
        A = -jnp.exp(A_log)
        dA = jnp.exp(dt[..., None] * A)
        dB = dt[..., None] * Bm[:, :, None, :]

        def step(h, inp):
            dA_t, dB_t, x_t, C_t = inp
            h = h * dA_t + x_t[..., None] * dB_t
            y_t = jnp.sum(h * C_t[:, None, :], axis=-1) + D_param * x_t
            return (h, y_t)
        h0 = jnp.zeros((batch, D_INNER, D_STATE), dtype=u.dtype)
        scan_inputs = (jnp.moveaxis(dA, 1, 0), jnp.moveaxis(dB, 1, 0), jnp.moveaxis(x_conv, 1, 0), jnp.moveaxis(Cm, 1, 0))
        _, y_ssm = jax.lax.scan(step, h0, scan_inputs)
        y = jnp.moveaxis(y_ssm, 0, 1) * _silu(z)
        return y @ out_proj_w.T

    def _L1_ffn_ref(x, gate_w, gate_b, W1, B1, W3, B3, W2, B2, Ws1, Bs1, Ws3, Bs3, Ws2, Bs2):
        import jax, jax.numpy as jnp
        import numpy as np
        B, S, D = (2, 256, 192)
        I = 96
        E = 8
        G = 4
        TOPK_GROUPS = 2
        K = 2
        ROUTE_SCALE = 1.0
        ALPHA, LIMIT = (1.702, 7.0)

        def swiglu(h):
            xg = jnp.minimum(h[..., ::2], LIMIT)
            xl = jnp.clip(h[..., 1::2], -LIMIT, LIMIT)
            return xg * jax.nn.sigmoid(ALPHA * xg) * (xl + 1.0)

        def gate(x, gate_w, gate_b):
            scores = jax.nn.softmax(jnp.einsum('td,ed->te', x, gate_w).astype(jnp.float32), axis=-1)
            original_scores = scores
            s = scores + gate_b
            T = x.shape[0]
            sg = s.reshape(T, G, E // G)
            group_scores = jnp.sum(jax.lax.top_k(sg, 2)[0], axis=-1)
            _, gidx = jax.lax.top_k(group_scores, TOPK_GROUPS)
            keep = jnp.any(jax.nn.one_hot(gidx, G, dtype=jnp.bool_), axis=1)
            sg = jnp.where(keep[:, :, None], sg, -jnp.inf)
            s = sg.reshape(T, E)
            _, idx = jax.lax.top_k(s, K)
            w = jnp.take_along_axis(original_scores, idx, axis=1) * ROUTE_SCALE
            return (w.astype(x.dtype), idx)

        def expert_ffn(x, W1, B1, W3, B3, W2, B2):
            h1 = jnp.einsum('td,edh->teh', x, W1) + B1
            h3 = jnp.einsum('td,edh->teh', x, W3) + B3
            g = swiglu(h1 * h3)
            return jnp.einsum('tei,eid->ted', g, W2) + B2

        def shared_ffn(x, Ws1, Bs1, Ws3, Bs3, Ws2, Bs2):
            h = (x @ Ws1 + Bs1) * (x @ Ws3 + Bs3)
            return swiglu(h) @ Ws2 + Bs2
        inp_shape = x.shape
        xt = x.reshape(-1, D)
        w, idx = gate(xt, gate_w, gate_b)
        combine = jnp.einsum('tk,tke->te', w, jax.nn.one_hot(idx, E, dtype=w.dtype))
        per_expert = expert_ffn(xt, W1, B1, W3, B3, W2, B2)
        routed = jnp.einsum('ted,te->td', per_expert, combine)
        out = routed + shared_ffn(xt, Ws1, Bs1, Ws3, Bs3, Ws2, Bs2)
        return out.reshape(inp_shape)

    def _L2_attn_ref(x, Wq, Wk, Wv, Wproj):
        import math
        import jax, jax.numpy as jnp
        import numpy as np
        D_MODEL = 192
        N_HEAD = 12
        HEAD_DIM = D_MODEL // N_HEAD
        ROPE_BASE = 10000.0
        EPS = 1e-06

        def rotary_cache(seq_len, head_dim, base=ROPE_BASE):
            half = head_dim // 2
            freq = 1.0 / base ** (jnp.arange(half, dtype=jnp.float32) / half)
            freqs = jnp.arange(seq_len, dtype=jnp.float32)[:, None] * freq[None, :]
            return (jnp.cos(freqs), jnp.sin(freqs))

        def apply_rope(x, cos, sin):
            cos = cos.astype(x.dtype)
            sin = sin.astype(x.dtype)
            x1 = x[..., ::2]
            x2 = x[..., 1::2]
            out = jnp.stack((x1 * cos - x2 * sin, x1 * sin + x2 * cos), axis=-1)
            return out.reshape(x.shape)
        B, S, D = x.shape
        H, hd = (N_HEAD, HEAD_DIM)

        def heads(W):
            return (x @ W.T).reshape(B, S, H, hd).transpose(0, 2, 1, 3)
        q, k, v = (heads(Wq), heads(Wk), heads(Wv))
        cos, sin = rotary_cache(S, hd)
        cos = cos[None, None]
        sin = sin[None, None]
        q = apply_rope(q, cos, sin)
        k = apply_rope(k, cos, sin)
        scores = jnp.einsum('bhsd,bhtd->bhst', q.astype(jnp.float32), k.astype(jnp.float32))
        scores = scores / math.sqrt(hd)
        weights = jax.lax.erf(scores) + 1.0
        mask = jnp.tril(jnp.ones((S, S), dtype=bool))[None, None]
        weights = jnp.where(mask, weights, 0.0)
        denom = jnp.maximum(weights.sum(axis=-1, keepdims=True), EPS)
        y = jnp.einsum('bhst,bhtd->bhsd', weights, v.astype(jnp.float32)) / denom
        y = y.astype(v.dtype)
        y = y.transpose(0, 2, 1, 3).reshape(B, S, D)
        return y @ Wproj.T

    def _L2_ffn_ref(x, f_know, r_know, W_fk, b_fk, W_rk, b_rk, emb_fk, emb_rk):
        import jax, jax.numpy as jnp
        import numpy as np
        B, S, D = (2, 256, 192)
        NF, NR, R, DS, K = (128, 128, 128, 64, 4)

        @jax.checkpoint
        def feature_fn(x, neurons, weights):
            all_h = jnp.einsum('bsd,ndr->bsnr', x, neurons)
            return jnp.einsum('bsnr,bsn->bsr', all_h, weights)

        @jax.checkpoint
        def restore_fn(h, neurons, weights):
            all_out = jnp.einsum('bsr,nrd->bsnd', h, neurons)
            return jnp.einsum('bsnd,bsn->bsd', all_out, weights)

        def topk_sparsify(weights, k):
            topk_vals, topk_idx = jax.lax.top_k(weights, k)
            N = weights.shape[-1]
            one_hot_mask = jax.nn.one_hot(topk_idx, N, dtype=weights.dtype)
            sparse = (one_hot_mask * topk_vals[..., jnp.newaxis]).sum(axis=-2)
            sparse = sparse / (sparse.sum(axis=-1, keepdims=True) + 1e-08)
            return (sparse, topk_idx)
        emb_fk_n = emb_fk / (jnp.linalg.norm(emb_fk, axis=-1, keepdims=True) + 1e-08)
        emb_rk_n = emb_rk / (jnp.linalg.norm(emb_rk, axis=-1, keepdims=True) + 1e-08)
        logits_fk = jnp.einsum('bsd,nd->bsn', x @ W_fk + b_fk, emb_fk_n)
        logits_rk = jnp.einsum('bsd,nd->bsn', x @ W_rk + b_rk, emb_rk_n)
        w_fk, _ = topk_sparsify(jax.nn.softmax(logits_fk, axis=-1), K)
        w_rk, _ = topk_sparsify(jax.nn.softmax(logits_rk, axis=-1), K)
        h = feature_fn(x, f_know, w_fk)
        out = restore_fn(h, r_know, w_rk)
        return out

    def _L3_attn_ref(x, W_qkv, b_qkv):
        import jax, jax.numpy as jnp
        import numpy as np
        EMBED_DIM = 192
        MAX_LEN = 256
        ALPHA = 0.99
        BATCH = 16

        def _retention_mask(sl, alpha, dtype):
            i = jnp.arange(sl)[:, None]
            j = jnp.arange(sl)[None, :]
            causal = i >= j
            exponent = jnp.where(causal, (i - j).astype(dtype), 0.0)
            decay = jnp.asarray(alpha, dtype) ** exponent
            return jnp.where(causal, decay, jnp.zeros((), dtype))
        bs, sl, d = x.shape
        qkv = x @ W_qkv + b_qkv
        q, k, v = jnp.split(qkv, 3, axis=-1)
        M = _retention_mask(sl, ALPHA, x.dtype)
        scores = jnp.einsum('bsd,btd->bst', q, k) / jnp.sqrt(jnp.asarray(d, x.dtype))
        out = jnp.einsum('bst,btd->bsd', scores * M[None, :, :], v)
        return out

    def _L3_ffn_ref(x, Wg, bg, W1, b1, W2, b2, Wv, bv, Wm, bm, Wo, bo, bk_scale):
        import jax, jax.numpy as jnp
        import numpy as np
        B, N, D, E = (2, 512, 192, 8)
        H = 4 * D
        TARGET_SPARSITY = 0.6
        K_KEEP = int(N * (1.0 - TARGET_SPARSITY))
        V_MAX, FEAT_CLAMP, ETA = (3.0, 10.0, 1.0)

        def _bk_gii(v):
            dr, di = (v, jnp.full_like(v, -ETA))

            def cf(reverse):
                init = (jnp.full((v.shape[0],), 1e+18, v.dtype), jnp.zeros((v.shape[0],), v.dtype))

                def step(c, d):
                    ar, ai = c
                    drr, dii = d
                    den = ar * ar + ai * ai
                    out = (drr - ar / den, dii + ai / den)
                    return (out, out)
                _, (r, i) = jax.lax.scan(step, init, (dr.T, di.T), reverse=reverse)
                return (r.T, i.T)
            ar, ai = cf(False)
            br, bi = cf(True)
            cr, ci = (ar + br - dr, ai + bi - di)
            den = cr * cr + ci * ci
            return (cr / den, -ci / den)
        probs = jax.nn.softmax(x @ Wg + bg, axis=-1)
        top_p = jnp.max(probs, axis=-1)
        comb = jax.nn.one_hot(jnp.argmax(probs, -1), E, dtype=x.dtype) * top_p[..., None]
        h = jax.nn.gelu(jnp.einsum('bnd,edh->ebnh', x, W1) + b1[:, None, None, :])
        y = jnp.einsum('ebnh,ehd->ebnd', h, W2) + b2[:, None, None, :]
        ffn_out = jnp.einsum('ebnd,bne->bnd', y, comb)
        v = jnp.clip(ffn_out @ Wv + bv, -V_MAX, V_MAX)
        scores = jax.nn.sigmoid(x @ Wm + bm)
        thr = jax.lax.top_k(scores, K_KEEP)[0][:, -1]
        mask = (scores >= thr[:, None]).astype(x.dtype)
        gr, gi = _bk_gii(v)
        feats = jnp.clip(jnp.stack([gr, gi], -1) * mask[..., None], -FEAT_CLAMP, FEAT_CLAMP)
        return ffn_out + bk_scale * (feats @ Wo + bo)
    h = _L0_tok_ref(x, L0_tok_W0, L0_tok_b0, L0_tok_W1, L0_tok_b1, L0_tok_W2, L0_tok_b2, L0_tok_Wf, L0_tok_bf, L0_tok_idx0, L0_tok_idx1, L0_tok_idx2)
    h = h + _L0_attn_ref(_layernorm(h, axis=-1), L0_attn_in_proj_w, L0_attn_conv_w, L0_attn_conv_b, L0_attn_x_proj_w, L0_attn_dt_proj_w, L0_attn_dt_proj_b, L0_attn_A_log, L0_attn_D, L0_attn_out_proj_w, L0_attn_norm_w, L0_attn_final_norm_w)
    h = h + _L0_ffn_ref(_layernorm(h, axis=-1), L0_ffn_Wr, L0_ffn_W1, L0_ffn_b1, L0_ffn_W2, L0_ffn_b2)
    h = h + _L1_attn_ref(_layernorm(h, axis=-1), L1_attn_in_proj_w, L1_attn_conv_w, L1_attn_conv_b, L1_attn_x_dt_w, L1_attn_x_b_w, L1_attn_x_c_w, L1_attn_dt_w, L1_attn_dt_b, L1_attn_A_log, L1_attn_D_param, L1_attn_out_proj_w)
    h = h + _L1_ffn_ref(_layernorm(h, axis=-1), L1_ffn_gate_w, L1_ffn_gate_b, L1_ffn_W1, L1_ffn_B1, L1_ffn_W3, L1_ffn_B3, L1_ffn_W2, L1_ffn_B2, L1_ffn_Ws1, L1_ffn_Bs1, L1_ffn_Ws3, L1_ffn_Bs3, L1_ffn_Ws2, L1_ffn_Bs2)
    h = h + _L2_attn_ref(_layernorm(h, axis=-1), L2_attn_Wq, L2_attn_Wk, L2_attn_Wv, L2_attn_Wproj)
    h = h + _L2_ffn_ref(_layernorm(h, axis=-1), L2_ffn_f_know, L2_ffn_r_know, L2_ffn_W_fk, L2_ffn_b_fk, L2_ffn_W_rk, L2_ffn_b_rk, L2_ffn_emb_fk, L2_ffn_emb_rk)
    h = h + _L3_attn_ref(_layernorm(h, axis=-1), L3_attn_W_qkv, L3_attn_b_qkv)
    h = h + _L3_ffn_ref(_layernorm(h, axis=-1), L3_ffn_Wg, L3_ffn_bg, L3_ffn_W1, L3_ffn_b1, L3_ffn_W2, L3_ffn_b2, L3_ffn_Wv, L3_ffn_bv, L3_ffn_Wm, L3_ffn_bm, L3_ffn_Wo, L3_ffn_bo, L3_ffn_bk_scale)
    return h

_drawn_inputs = setup_inputs


def setup_inputs(seed=0):
    import zlib

    import numpy as np

    out = dict(_drawn_inputs(seed))
    spreads = {'L0_attn_conv_b': (0.0, 0.8),
     'L0_attn_D': (1.0, 0.6),
     'L0_attn_norm_w': (1.0, 0.6),
     'L0_attn_final_norm_w': (1.0, 0.2),
     'L1_attn_D_param': (1.0, 0.6),
     'L2_ffn_b_fk': (0.0, 0.8),
     'L2_ffn_b_rk': (0.0, 0.8),
     'L3_ffn_bg': (0.0, 0.8),
     'L3_ffn_b1': (0.0, 0.8),
     'L3_ffn_b2': (0.0, 2.0),
     'L3_ffn_bo': (0.0, 1.639)}
    factors = {'L0_tok_b0': 2.758,
     'L0_attn_in_proj_w': 5.491,
     'L0_attn_conv_w': 8.0,
     'L0_attn_x_proj_w': 8.0,
     'L0_attn_dt_proj_w': 8.0,
     'L0_attn_dt_proj_b': 8.0,
     'L0_attn_A_log': 8.0,
     'L0_attn_out_proj_w': 5.491,
     'L0_ffn_Wr': 3.804,
     'L0_ffn_W1': 3.853,
     'L0_ffn_b1': 8.0,
     'L0_ffn_W2': 3.548,
     'L0_ffn_b2': 8.0,
     'L1_attn_in_proj_w': 8.0,
     'L1_attn_conv_w': 8.0,
     'L1_attn_conv_b': 8.0,
     'L1_attn_x_dt_w': 8.0,
     'L1_attn_x_b_w': 8.0,
     'L1_attn_x_c_w': 8.0,
     'L1_attn_dt_w': 8.0,
     'L1_attn_dt_b': 8.0,
     'L1_attn_A_log': 8.0,
     'L1_attn_out_proj_w': 8.0,
     'L1_ffn_gate_w': 8.0,
     'L1_ffn_gate_b': 8.0,
     'L1_ffn_W1': 8.0,
     'L1_ffn_B1': 8.0,
     'L1_ffn_W3': 8.0,
     'L1_ffn_B3': 8.0,
     'L1_ffn_W2': 8.0,
     'L1_ffn_B2': 41.342,
     'L1_ffn_Ws1': 8.0,
     'L1_ffn_Bs1': 8.0,
     'L1_ffn_Ws3': 8.0,
     'L1_ffn_Bs3': 8.0,
     'L1_ffn_Ws2': 8.0,
     'L1_ffn_Bs2': 23.573,
     'L2_attn_Wq': 28.999,
     'L2_attn_Wk': 28.079,
     'L2_attn_Wv': 9.813,
     'L2_attn_Wproj': 10.099,
     'L2_ffn_f_know': 8.0,
     'L2_ffn_r_know': 8.0,
     'L2_ffn_W_fk': 8.0,
     'L2_ffn_W_rk': 8.0,
     'L2_ffn_emb_fk': 8.0,
     'L2_ffn_emb_rk': 8.0,
     'L3_ffn_Wg': 8.0,
     'L3_ffn_W1': 8.0,
     'L3_ffn_W2': 8.0,
     'L3_ffn_Wv': 200.0,
     'L3_ffn_Wm': 200.0,
     'L3_ffn_Wo': 189.531,
     'L3_attn_b_qkv': 3.313}
    for name, (base, spread) in spreads.items():
        noise = np.random.default_rng([zlib.crc32(name.encode()), seed]).standard_normal(out[name].shape)
        drawn = base * np.exp(spread * noise) if base else spread * noise
        out[name] = jnp.asarray(drawn.astype(out[name].dtype))
    for name, factor in factors.items():
        out[name] = (out[name] * factor).astype(out[name].dtype)
    return out
```

```python
from contextlib import ExitStack, contextmanager

import numpy as np
import concourse.bass as bass
from concourse import mybir

F32 = mybir.dt.float32
BF16 = mybir.dt.bfloat16
I32 = mybir.dt.int32
U32 = mybir.dt.uint32
ALU = mybir.AluOpType
ACT = mybir.ActivationFunctionType
AX = mybir.AxisListType

IMAGES, SEQ, D = 4, 256, 192
TOKENS = IMAGES * SEQ
P = 128
TILES = TOKENS // P
DH = D // 2
BANK = 512
EPS = 1e-5


class Own:

    def __init__(self, eng, done):
        self.eng, self.done = eng, done
        self.count, self.base = 0, 0

    def __call__(self, instruction):
        instruction.then_inc(self.done, 1)
        self.count += 1
        self.eng.wait_ge(self.done, self.base + self.count)

    @contextmanager
    def loop(self, rounds, steps):
        start = self.count
        if rounds == 1:
            yield 0
        else:
            with self.eng.Fori(0, rounds) as i:
                self.base = i * steps
                yield i
        assert self.count == start + steps, (self.count - start, steps)
        self.base, self.count = 0, start + rounds * steps


def one(ap):
    return ap.rearrange("o a b -> (o a) b")


def pick(ap, i):
    return one(ap[i:i + 1]) if isinstance(i, int) else one(ap[bass.ds(i, 1)])


def pick_of_two(ap, two, b):
    ap = ap[0:ap.shape[0] // 2 * 2]
    return pick(ap.rearrange("(o b) x y -> b o x y", b=2)[b], two)


class Chip:

    def __init__(self, nc, ctx):
        self.nc, self.ctx = nc, ctx
        self.stage_memory = None
        self.sems = {}
        self.mamba_layers = self.mamba_stacks = self.mamba_consts = 0
        self.experts = self.expert_stages = self.expert_consts = 0
        self.h = self.sb("h", [P, TILES, D], F32)
        self.xn = self.sb("xn", [P, TILES, D], F32)
        self.xnF = self.sb("xnF", [DH, 2, TOKENS], F32)
        self.ident = self.sb("ident", [P, P], F32)
        self.stats = self.sb("stats", [P, TILES, 6], F32)
        self.mean_var = self.sb("mean_var", [P, TILES, 2], F32)
        self.var = self.sb("var", [P, TILES], F32)
        self.std = self.sb("std", [P, TILES], F32)
        self.rstd = self.sb("rstd", [P, TILES], F32)
        self.ps = ctx.enter_context(nc.psum_tensor("ps", [P, 8, BANK], F32))
        self.ident_loaded = self.sem("ident_loaded")
        self.h_ready = self.sem("h_ready")
        self.ln_var_ready = self.sem("ln_var_ready")
        self.ln_std_ready = self.sem("ln_std_ready")
        self.xn_ready = self.sem("xn_ready")
        self.xnT_ready = self.sem("xnT_ready")
        self.xnF_ready = self.sem("xnF_ready")
        self.vector_own = self.sem("vector_own")
        self.scalar_own = self.sem("scalar_own")
        self.pool_own = self.sem("pool_own")
        self.tensor_own = self.sem("tensor_own")

    def sb(self, name, shape, dtype):
        return (self.stage_memory or self.ctx).enter_context(self.nc.sbuf_tensor(name, shape, dtype))

    def sem(self, name):
        if name not in self.sems:
            self.sems[name] = self.ctx.enter_context(self.nc.semaphore(name))
        return self.sems[name]

    def pair(self, n, rows=P):
        return self.ps[0:rows, 2 * n:2 * n + 2, :].rearrange("p a b -> p (a b)")

    def tok_psum(self, bank, width):
        return self.ps[:, bank:bank + 4, 0:2 * width].rearrange("p a (c d) -> p a c d", c=2)


def pairs_of(ap):
    return ap.rearrange("p (a c) n -> p a c n", c=2)



def norm_vector(k, v, own, n):
    v.wait_ge(k.h_ready, n)
    for j in range(TILES):
        last = v.bn_stats(k.stats[:, j, :], k.h[:, j, :])
    own(last)
    for j in range(TILES):
        last = v.bn_aggr(k.mean_var[:, j, :], k.stats[:, j, :])
    own(last)
    v.tensor_scalar(k.var[:, :], k.mean_var[:, :, 1], EPS, None, ALU.add).then_inc(k.ln_var_ready, 1)
    v.wait_ge(k.ln_std_ready, n)
    own(v.reciprocal(k.rstd[:, :], k.std[:, :]))
    for j in range(TILES):
        last = v.tensor_scalar(k.xn[:, j, :], k.h[:, j, :], k.mean_var[:, j, 0:1], k.rstd[:, j:j + 1],
                               ALU.subtract, ALU.mult)
    last.then_inc(k.xn_ready, 1)
    v.wait_ge(k.xnT_ready, n)
    v.tensor_copy(k.xnF[:, 1, :], k.pair(1, DH)).then_inc(k.xnF_ready, 1)


def norm_scalar(k, a, n):
    a.wait_ge(k.ln_var_ready, n)
    a.activation(k.std[:, :], k.var[:, :], ACT.Sqrt).then_inc(k.ln_std_ready, 1)
    a.wait_ge(k.xnT_ready, n)
    a.copy(k.xnF[:, 0, :], k.pair(0, DH)).then_inc(k.xnF_ready, 1)


def norm_tensor(k, pe, n):
    pe.wait_ge(k.xn_ready, n)
    transpose_tokens(k, pe, k.xn).then_inc(k.xnT_ready, 1)
    pe.wait_ge(k.xnF_ready, 2 * n)


def transpose_tokens(k, pe, x):
    for half in range(2):
        for j in range(TILES):
            last = pe.transpose(k.pair(half, DH)[:, P * j:P * (j + 1)], x[:, j, DH * half:DH * (half + 1)],
                                k.ident[:, :])
    return last



INNER, STATES, TAPS = 2 * D, 16, 4
BLOCKS = INNER // P
UNITS = BLOCKS * STATES
RING = 3
BC = 2 * STATES
PARAMS = TAPS + 3 + STATES


class Mamba:
    def __init__(self, k, name, norm, w, layers, rank):
        self.k, self.norm, self.w, self.layers, self.rank = k, norm, w, layers, rank
        self.own_norms = "norm_w" in w
        sb, sem = k.sb, k.sem
        self.w_in = sb(name + "_w_in", [DH, 2, 2 * INNER], F32)
        self.w_x = sb(name + "_w_x", [P, BLOCKS, 3 * BC + rank], F32)
        self.w_dt = sb(name + "_w_dt", [rank, INNER], F32)
        self.w_out = sb(name + "_w_out", [P, BLOCKS, D], F32)
        self.params = sb(name + "_mamba_params", [P, layers, BLOCKS, PARAMS], F32)
        self.par = sb(name + "_layer_params", [P, BLOCKS, PARAMS], F32)
        self.neg_a = sb(name + "_neg_a", [P, BLOCKS, STATES], F32)
        self.norms = sb(name + "_mamba_norms", [DH, layers, 2], F32)
        self.nw = sb(name + "_layer_norm_w", [DH, 2], F32)
        self.final_w = sb(name + "_final_w", [P, D], F32)
        self.x = sb(name + "_mamba_x", [P, TILES, D], F32)
        self.sel0 = sb(name + "_sel0", [3 * BC, BC], F32)
        self.sel = sb(name + "_sel", [3 * BC, BC, P], BF16)
        self.u = sb(name + "_u", [P, BLOCKS, TOKENS], F32)
        self.z = sb(name + "_z", [P, BLOCKS, TOKENS], F32)
        self.dt = sb(name + "_dt", [P, BLOCKS, TOKENS], F32)
        self.dtu = sb(name + "_dtu", [P, BLOCKS, TOKENS], F32)
        self.dtr = sb(name + "_dtr", [rank, TOKENS], F32)
        self.bc3 = sb(name + "_bc3", [3 * BC, TOKENS], BF16)
        self.b_row = sb(name + "_b_row", [P, 2, TOKENS], F32)
        self.c_row = sb(name + "_c_row", [P, 2, TOKENS], F32)
        self.da = sb(name + "_da", [P, RING, IMAGES, SEQ], F32)
        self.bu = sb(name + "_bu", [P, RING, TOKENS], F32)
        self.hs = sb(name + "_hs", [P, RING, TOKENS], F32)
        self.hc = sb(name + "_hc", [P, RING, TOKENS], F32)
        s = lambda x: sem("mamba_" + x)
        self.layer0, self.stack, self.consts0 = k.mamba_layers, k.mamba_stacks, k.mamba_consts
        self.consts = 64 if self.own_norms else 32
        k.mamba_layers, k.mamba_stacks, k.mamba_consts = self.layer0 + layers, self.stack + 1, self.consts0 + self.consts
        self.consts_loaded = s("consts_loaded")
        self.w_in_loaded, self.w_x_loaded = s("w_in_loaded"), s("w_x_loaded")
        self.w_dt_loaded, self.w_out_loaded = s("w_dt_loaded"), s("w_out_loaded")
        self.par_ready = s("par_ready")
        self.sel_ready = s("sel_ready")
        self.ms_ready, self.rms_ready, self.xs_ready = s("ms_ready"), s("rms_ready"), s("xs_ready")
        self.xsT_ready, self.xsF_ready = s("xsT_ready"), s("xsF_ready")
        self.in_ready = s("in_ready")
        self.tap_ready, self.conv_ready = s("tap_ready"), s("conv_ready")
        self.u_ready, self.z_ready = s("u_ready"), s("z_ready")
        self.bc_ready, self.bc3_ready = s("bc_ready"), s("bc3_ready")
        self.dtr_ready, self.dtr_copied = s("dtr_ready"), s("dtr_copied")
        self.dtp_ready = s("dtp_ready")
        self.e_ready, self.w1_ready, self.ln_ready = s("e_ready"), s("w1_ready"), s("ln_ready")
        self.dt_ready = s("dt_ready")
        self.row_ready, self.row_copied = s("row_ready"), s("row_copied")
        self.da_ready, self.bu_ready = s("da_ready"), s("bu_ready")
        self.scan_done, self.hc_ready, self.hc_used = s("scan_done"), s("hc_ready"), s("hc_used")
        self.y_ready, self.out_ready = s("y_ready"), s("out_ready")

    def sync(self, sp):
        k, w, n = self.k, self.w, self.layers
        sp.wait_ge(k.h_ready, self.norm)
        sp.dma_start(self.params[:, 0:n], w["params"].rearrange("n (b p) c -> p n b c", p=P)).then_inc(self.consts_loaded, 16)
        sp.dma_start(self.sel0[:, :], w["sel"]).then_inc(self.consts_loaded, 16)
        if self.own_norms:
            sp.dma_start(self.norms[:, :, :], w["norm_w"]).then_inc(self.consts_loaded, 16)
            sp.dma_start(self.final_w[:, :], w["final_w"].to_broadcast([P, D])).then_inc(self.consts_loaded, 16)

        def load(i):
            sp.dma_start(self.w_in[:, :, :], pick(w["in_T"], i).rearrange("(c p) m -> p c m", p=DH)).then_inc(self.w_in_loaded, 16)
            sp.dma_start(self.w_x[:, :, 0:3 * BC + self.rank], pick(w["x_T"], i).rearrange("(b p) m -> p b m", p=P)).then_inc(self.w_x_loaded, 16)
            sp.dma_start(self.w_dt[0:self.rank, :], pick(w["dt_T"], i)).then_inc(self.w_dt_loaded, 16)
            sp.dma_start(self.w_out[:, :, :], pick(w["out_T"], i).rearrange("(b p) m -> p b m", p=P)).then_inc(self.w_out_loaded, 16)

        load(0)
        if n > 1:
            with sp.Fori(1, n) as i:
                sp.wait_ge(self.in_ready, 6 * i)
                sp.dma_start(self.w_in[:, :, :], pick(w["in_T"], i).rearrange("(c p) m -> p c m", p=DH)).then_inc(self.w_in_loaded, 16)
                sp.wait_ge(self.dtr_ready, i)
                sp.dma_start(self.w_x[:, :, 0:3 * BC + self.rank], pick(w["x_T"], i).rearrange("(b p) m -> p b m", p=P)).then_inc(self.w_x_loaded, 16)
                sp.wait_ge(self.dtp_ready, 3 * i)
                sp.dma_start(self.w_dt[0:self.rank, :], pick(w["dt_T"], i)).then_inc(self.w_dt_loaded, 16)
                sp.wait_ge(self.out_ready, i)
                sp.dma_start(self.w_out[:, :, :], pick(w["out_T"], i).rearrange("(b p) m -> p b m", p=P)).then_inc(self.w_out_loaded, 16)

    def tensor(self, pe, own):
        k = self.k
        norm_tensor(k, pe, self.norm)
        pe.wait_ge(self.sel_ready, self.stack + 1)
        with own.loop(self.layers, 0) as layer:
            i = self.layer0 + layer
            if self.own_norms:
                pe.wait_ge(self.xs_ready, i + 1)
                transpose_tokens(k, pe, k.xn).then_inc(self.xsT_ready, 1)
                pe.wait_ge(self.xsF_ready, 2 * i + 2)
            pe.wait_ge(self.w_in_loaded, 16 * i + 16)
            for m in range(2 * BLOCKS):
                if m >= 4:
                    pe.wait_ge(self.conv_ready, 3 * i + m - 3)
                out = k.pair((m + 2) % 4)
                for c in range(2):
                    for t in range(2):
                        last = pe.matmul(out[:, BANK * t:BANK * (t + 1)], self.w_in[:, c, P * m:P * (m + 1)],
                                         k.xnF[:, c, BANK * t:BANK * (t + 1)], start=(c == 0), stop=(c == 1))
                last.then_inc(self.in_ready, 1)
            pe.wait_ge(self.w_x_loaded, 16 * i + 16)
            pe.wait_ge(self.u_ready, 3 * i + 3)
            for b in range(BLOCKS):
                for t in range(2):
                    last = pe.matmul(k.pair(0, 3 * BC)[:, BANK * t:BANK * (t + 1)], self.w_x[:, b, 0:3 * BC],
                                     self.u[:, b, BANK * t:BANK * (t + 1)], start=(b == 0), stop=(b == BLOCKS - 1))
            last.then_inc(self.bc_ready, 1)
            pe.wait_ge(self.z_ready, 3 * i + 1)
            for b in range(BLOCKS):
                for t in range(2):
                    last = pe.matmul(k.pair(1, self.rank)[:, BANK * t:BANK * (t + 1)],
                                     self.w_x[:, b, 3 * BC:3 * BC + self.rank],
                                     self.u[:, b, BANK * t:BANK * (t + 1)], start=(b == 0), stop=(b == BLOCKS - 1))
            last.then_inc(self.dtr_ready, 1)
            pe.wait_ge(self.w_dt_loaded, 16 * i + 16)
            pe.wait_ge(self.dtr_copied, i + 1)
            pe.wait_ge(self.z_ready, 3 * i + 3)
            for b in range(BLOCKS):
                for t in range(2):
                    last = pe.matmul(k.pair((2, 3, 1)[b])[:, BANK * t:BANK * (t + 1)],
                                     self.w_dt[0:self.rank, P * b:P * (b + 1)],
                                     self.dtr[0:self.rank, BANK * t:BANK * (t + 1)], start=True, stop=True)
                last.then_inc(self.dtp_ready, 1)
            pe.wait_ge(self.bc3_ready, i + 1)

            def row(r):
                if r >= 1:
                    pe.wait_ge(self.row_copied, BC * i + r)
                for t in range(2):
                    last = pe.matmul(k.pair(0)[:, BANK * t:BANK * (t + 1)], self.sel[:, (r % 2) * STATES + r // 2, :],
                                     self.bc3[:, BANK * t:BANK * (t + 1)], start=True, stop=True)
                last.then_inc(self.row_ready, 1)

            for r in range(4):
                row(r)
            for n in range(STATES):
                if n + 2 < STATES:
                    row(2 * n + 4)
                    row(2 * n + 5)
                for b in range(BLOCKS):
                    pe.wait_ge(self.hc_ready, UNITS * i + BLOCKS * n + b + 1)
                    slot = (BLOCKS * n + b) % RING
                    for t in range(2):
                        last = pe.matmul(k.pair(1 + b)[:, BANK * t:BANK * (t + 1)], k.ident[:, :],
                                         self.hc[:, slot, BANK * t:BANK * (t + 1)],
                                         start=(n == 0), stop=(n == STATES - 1))
                    last.then_inc(self.hc_used, 1)
            pe.wait_ge(self.w_out_loaded, 16 * i + 16)
            pe.wait_ge(self.y_ready, 3 * i + 3)
            for j in range(TILES):
                for b in range(BLOCKS):
                    last = pe.matmul(k.tok_psum(0, D)[:, j // 2, j % 2, :], self.u[:, b, P * j:P * (j + 1)],
                                     self.w_out[:, b, :], start=(b == 0), stop=(b == BLOCKS - 1))
            last.then_inc(self.out_ready, 1)

    def scalar(self, a, own):
        k = self.k
        norm_scalar(k, a, self.norm)
        with own.loop(self.layers, 5) as layer:
            i = self.layer0 + layer
            if self.own_norms:
                a.wait_ge(self.ms_ready, i + 1)
                a.activation(k.std[:, :], k.var[:, :], ACT.Sqrt).then_inc(self.rms_ready, 1)
                a.wait_ge(self.par_ready, i + 1)
                a.wait_ge(self.xsT_ready, i + 1)
                for half in range(2):
                    a.mul(k.xnF[:, half, :], k.pair(half, DH), self.nw[:, half:half + 1]).then_inc(self.xsF_ready, 1)
            a.wait_ge(self.par_ready, i + 1)
            for b in range(BLOCKS):
                a.wait_ge(self.in_ready, 6 * i + b + 1)
                a.activation(self.hs[:, b, :], k.pair((b + 2) % 4), ACT.Identity,
                             bias=self.par[:, b, TAPS:TAPS + 1], scale=self.par[:, b, TAPS - 1:TAPS]).then_inc(self.tap_ready, 1)
            for b in range(BLOCKS):
                a.wait_ge(self.conv_ready, 3 * i + b + 1)
                a.activation(self.u[:, b, :], self.hs[:, b, :], ACT.Silu).then_inc(self.u_ready, 1)
            for b in range(BLOCKS):
                a.wait_ge(self.in_ready, 6 * i + BLOCKS + b + 1)
                a.activation(self.z[:, b, :], k.pair((BLOCKS + b + 2) % 4), ACT.Silu).then_inc(self.z_ready, 1)
            a.wait_ge(self.dtr_ready, i + 1)
            a.copy(self.dtr[0:self.rank, :], k.pair(1, self.rank)).then_inc(self.dtr_copied, 1)
            own(a.activation(self.neg_a[:, :, :], self.par[:, :, TAPS + 3:PARAMS], ACT.Exp))
            own(a.mul(self.neg_a[:, :, :], self.neg_a[:, :, :], -1.0))
            for b in range(BLOCKS):
                a.wait_ge(self.dtp_ready, 3 * i + b + 1)
                a.activation(self.dt[:, b, :], k.pair((2, 3, 1)[b]), ACT.Identity,
                             bias=self.par[:, b, TAPS + 1:TAPS + 2])
                own(a.activation(self.bu[:, b, :], k.pair((2, 3, 1)[b]), ACT.Abs,
                                 bias=self.par[:, b, TAPS + 1:TAPS + 2]))
                a.activation(self.bu[:, b, :], self.bu[:, b, :], ACT.Exp, scale=-1.0).then_inc(self.e_ready, 1)
            a.wait_ge(self.bc3_ready, i + 1)
            for b in range(BLOCKS):
                a.wait_ge(self.w1_ready, 3 * i + b + 1)
                a.activation(self.hc[:, b, :], self.hs[:, b, :], ACT.Ln).then_inc(self.ln_ready, 1)

            def row_copy(r):
                n = r // 2
                a.wait_ge(self.row_ready, BC * i + r + 1)
                if n >= 2:
                    a.wait_ge(self.hc_ready if r % 2 else self.bu_ready, UNITS * i + BLOCKS * (n - 1))
                a.copy((self.c_row if r % 2 else self.b_row)[:, n % 2, :], k.pair(0)).then_inc(self.row_copied, 1)

            row_copy(0)
            row_copy(1)
            a.wait_ge(self.dt_ready, 3 * i + 3)
            for n in range(STATES):
                if n + 1 < STATES:
                    row_copy(2 * n + 2)
                for b in range(BLOCKS):
                    unit = BLOCKS * n + b
                    if unit >= RING:
                        a.wait_ge(self.scan_done, UNITS * i + unit - RING + 1)
                    a.activation(self.da[:, unit % RING, :, 1:SEQ],
                                 self.dt[:, b, :].rearrange("p (m t) -> p m t", m=IMAGES)[:, :, 1:SEQ], ACT.Exp,
                                 scale=self.neg_a[:, b, n:n + 1]).then_inc(self.da_ready, 1)
                if n + 1 < STATES:
                    row_copy(2 * n + 3)
        if self.own_norms:
            a.wait_ge(self.ms_ready, self.layers + 1)
            a.activation(k.std[:, :], k.var[:, :], ACT.Sqrt).then_inc(self.rms_ready, 1)

    def of_layer(self, t, i, blocks=True):
        row = t[:, i:i + 1] if isinstance(i, int) else t[:, bass.ds(i, 1)]
        return row.rearrange("p o b c -> p (o b) c") if blocks else row.rearrange("p o c -> p (o c)")

    def vector(self, v, own):
        k = self.k
        norm_vector(k, v, own, self.norm)
        v.wait_ge(self.consts_loaded, self.consts0 + self.consts)
        v.tensor_copy(self.sel[:, :, :], self.sel0[:, :].unsqueeze(2).to_broadcast([3 * BC, BC, P])).then_inc(self.sel_ready, 1)
        own(v.memset(self.da[:, :, :, 0], 0.0))
        if self.own_norms:
            own(v.tensor_copy(self.x[:, :, :], k.xn[:, :, :]))

        def rms():
            sq = self.bu[:, 0:2, :].rearrange("p a b -> p (a b)")[:, 0:TILES * D].rearrange("p (j d) -> p j d", d=D)
            own(v.tensor_tensor(sq, self.x[:, :, :], self.x[:, :, :], ALU.mult))
            own(v.tensor_reduce(k.var[:, :], sq, AX.X, ALU.add))
            v.tensor_scalar(k.var[:, :], k.var[:, :], 1.0 / D, EPS, ALU.mult, ALU.add).then_inc(self.ms_ready, 1)

        steps = 20 if self.own_norms else 15
        with own.loop(self.layers, steps) as layer:
            i = self.layer0 + layer
            own(v.tensor_copy(self.par[:, :, :], self.of_layer(self.params, layer)))
            if self.own_norms:
                own(v.tensor_copy(self.nw[:, :], self.of_layer(self.norms, layer, False)))
            v.sem_inc(self.par_ready, 1)
            if self.own_norms:
                rms()
                v.wait_ge(self.rms_ready, i + 1)
                own(v.reciprocal(k.rstd[:, :], k.std[:, :]))
                v.tensor_tensor(k.xn[:, :, :], self.x[:, :, :], k.rstd[:, :].unsqueeze(2).to_broadcast([P, TILES, D]),
                                ALU.mult).then_inc(self.xs_ready, 1)
            for b in range(BLOCKS):
                v.wait_ge(self.tap_ready, 3 * i + b + 1)
                x = k.pair((b + 2) % 4).rearrange("p (m t) -> p m t", m=IMAGES)
                acc = self.hs[:, b, :].rearrange("p (m t) -> p m t", m=IMAGES)
                for s in range(1, TAPS):
                    ins = v.scalar_tensor_tensor(out=acc[:, :, s:SEQ], in0=x[:, :, 0:SEQ - s],
                                                 scalar=self.par[:, b, TAPS - 1 - s:TAPS - s],
                                                 in1=acc[:, :, s:SEQ], op0=ALU.mult, op1=ALU.add)
                    if s < TAPS - 1:
                        own(ins)
                ins.then_inc(self.conv_ready, 1)
            v.wait_ge(self.bc_ready, i + 1)
            own(v.tensor_copy(self.bc3[:, :], k.pair(0, 3 * BC)))
            rest = self.hc[0:3 * BC, 0, :]
            own(v.tensor_tensor(rest, k.pair(0, 3 * BC), self.bc3[:, :], ALU.subtract))
            v.tensor_copy(self.bc3[BC:2 * BC, :], rest[BC:2 * BC, :])
            own(v.tensor_copy(self.bc3[2 * BC:, :], rest[2 * BC:, :]))
            own(v.tensor_tensor(rest[2 * BC:, :], rest[2 * BC:, :], self.bc3[2 * BC:, :], ALU.subtract))
            v.tensor_copy(self.bc3[2 * BC:, :], rest[2 * BC:, :]).then_inc(self.bc3_ready, 1)
            v.wait_ge(self.bc3_ready, i + 1)
            for b in range(BLOCKS):
                v.wait_ge(self.e_ready, 3 * i + b + 1)
                v.tensor_scalar(self.hs[:, b, :], self.bu[:, b, :], 1.0, None, ALU.add).then_inc(self.w1_ready, 1)
                v.wait_ge(self.w1_ready, 3 * i + b + 1)
                v.scalar_tensor_tensor(out=self.bu[:, b, :], in0=self.hs[:, b, :], scalar=1.0, in1=self.bu[:, b, :],
                                       op0=ALU.subtract, op1=ALU.subtract)
                v.wait_ge(self.ln_ready, 3 * i + b + 1)
                own(v.scalar_tensor_tensor(out=self.dt[:, b, :], in0=self.dt[:, b, :], scalar=0.0,
                                           in1=self.hc[:, b, :], op0=ALU.max, op1=ALU.add))
                v.tensor_tensor(self.dt[:, b, :], self.dt[:, b, :], self.bu[:, b, :], ALU.subtract).then_inc(self.dt_ready, 1)

            def weigh(unit):
                n = unit // BLOCKS
                v.wait_ge(self.scan_done, UNITS * i + unit + 1)
                v.wait_ge(self.row_copied, BC * i + 2 * n + 2)
                if unit >= RING:
                    v.wait_ge(self.hc_used, UNITS * i + unit - RING + 1)
                v.tensor_tensor(self.hc[:, unit % RING, :], self.hs[:, unit % RING, :], self.c_row[:, n % 2, :],
                                ALU.mult).then_inc(self.hc_ready, 1)

            for unit in range(UNITS):
                v.wait_ge(self.da_ready, UNITS * i + unit + 1)
                v.wait_ge(self.bu_ready, UNITS * i + unit + 1)
                if unit >= RING:
                    v.wait_ge(self.hc_ready, UNITS * i + unit - RING + 1)
                v.tensor_tensor_scan(self.hs[:, unit % RING, :],
                                     self.da[:, unit % RING, :, :].rearrange("p m t -> p (m t)"),
                                     self.bu[:, unit % RING, :], 0.0, ALU.mult, ALU.add).then_inc(self.scan_done, 1)
                if unit >= 1:
                    weigh(unit - 1)
            weigh(UNITS - 1)
            v.wait_ge(self.hc_used, UNITS * i + UNITS)
            for b in range(BLOCKS):
                ins = v.scalar_tensor_tensor(out=self.u[:, b, :], in0=self.u[:, b, :],
                                             scalar=self.par[:, b, TAPS + 2:TAPS + 3], in1=k.pair(1 + b),
                                             op0=ALU.mult, op1=ALU.add)
            own(ins)
            for b in range(BLOCKS):
                v.tensor_tensor(self.u[:, b, :], self.u[:, b, :], self.z[:, b, :], ALU.mult).then_inc(self.y_ready, 1)
            v.wait_ge(self.out_ready, i + 1)
            if self.own_norms:
                own(v.tensor_tensor(pairs_of(self.x[:, :, :]), pairs_of(self.x[:, :, :]), k.tok_psum(0, D), ALU.add))
            else:
                v.tensor_tensor(pairs_of(k.h[:, :, :]), pairs_of(k.h[:, :, :]), k.tok_psum(0, D),
                                ALU.add).then_inc(k.h_ready, 1)
        if self.own_norms:
            rms()
            v.wait_ge(self.rms_ready, self.layers + 1)
            own(v.reciprocal(k.rstd[:, :], k.std[:, :]))
            own(v.tensor_tensor(k.xn[:, :, :], self.x[:, :, :], k.rstd[:, :].unsqueeze(2).to_broadcast([P, TILES, D]), ALU.mult))
            own(v.tensor_tensor(k.xn[:, :, :], k.xn[:, :, :], self.final_w[:, :].unsqueeze(1).to_broadcast([P, TILES, D]), ALU.mult))
            v.tensor_tensor(k.h[:, :, :], k.h[:, :, :], k.xn[:, :, :], ALU.add).then_inc(k.h_ready, 1)

    def pool(self, g, own):
        with own.loop(self.layers, BLOCKS) as layer:
            i = self.layer0 + layer
            for b in range(BLOCKS):
                g.wait_ge(self.dt_ready, 3 * i + b + 1)
                own(g.tensor_tensor(self.dtu[:, b, :], self.dt[:, b, :], self.u[:, b, :], ALU.mult))
            for n in range(STATES):
                g.wait_ge(self.row_copied, BC * i + 2 * n + 1)
                for b in range(BLOCKS):
                    unit = BLOCKS * n + b
                    if unit >= RING:
                        g.wait_ge(self.scan_done, UNITS * i + unit - RING + 1)
                    g.tensor_tensor(self.bu[:, unit % RING, :], self.dtu[:, b, :], self.b_row[:, n % 2, :],
                                    ALU.mult).then_inc(self.bu_ready, 1)



SPAN = SEQ + P


def causal_parts():
    return ((0, 0, slice(0, SEQ)), (1, P, slice(SEQ, SPAN)))


class ErfAttention:
    HEADS, HEAD = 12, 16
    PAD = 32
    COLS = HEAD + 1
    FLOOR = 1e-6
    TURN = 2 ** 0.5 * HEAD ** -0.5
    TINY = 1e-20
    LEAST = 3 * 2.0 ** -24 - 1

    def __init__(self, k, name, norm, w):
        self.k, self.norm, self.w = k, norm, w
        sb, s = (lambda x, shape, t=F32: k.sb(name + "_" + x, shape, t)), (lambda x: k.sem(name + "_" + x))
        H, G = self.HEADS, 2 * self.HEADS
        self.w_qkv, self.w_proj = sb("w_qkv", [DH, 2, 3 * D]), sb("w_proj", [DH, 2, D])
        self.cos, self.sin, self.mask = sb("cos", [P, 2, 8]), sb("sin", [P, 2, 8]), sb("mask", [P, SPAN])
        self.qk = sb("qk", [P, TILES, G, self.PAD])
        self.t1, self.t2 = sb("t1", [P, IMAGES, G, 8]), sb("t2", [P, IMAGES, G, 8])
        self.v = sb("v", [P, TILES, H, self.COLS])
        self.qkT = sb("qkT", [P, 6, TOKENS])
        self.wts = sb("wts", [P, 2, 2, SPAN])
        self.gelu, self.ratio = sb("gelu", [P, 2, 2, SPAN]), sb("ratio", [P, 2, 2, SPAN])
        self.inv = sb("inv", [P, 2, 2, SPAN])
        self.den = sb("den", [P, TILES, H])
        self.y = sb("y", [P, TILES, D])
        self.consts_loaded, self.v_ready, self.qk_ready = s("consts_loaded"), s("v_ready"), s("qk_ready")
        self.rotated, self.qk_written, self.v_copied = s("rotated"), s("qk_written"), s("v_copied")
        self.qkT_ready, self.qkT_copied = s("qkT_ready"), s("qkT_copied")
        self.scores_ready, self.abs_done, self.wts_ready = s("scores_ready"), s("abs_done"), s("wts_ready")
        self.gelu_done, self.ratio_ready = s("gelu_done"), s("ratio_ready")
        self.av_ready, self.y_ready = s("av_ready"), s("y_ready")
        self.yT_ready, self.yT_copied, self.out_ready = s("yT_ready"), s("yT_copied"), s("out_ready")

    def sync(self, sp):
        w = self.w
        sp.wait_ge(self.k.h_ready, self.norm)
        for dst, src in ((self.w_qkv[:, :, :], w["qkv_T"].rearrange("(c p) m -> p c m", p=DH)),
                         (self.w_proj[:, :, :], w["proj_T"].rearrange("(c p) m -> p c m", p=DH)),
                         (self.cos[:, :, :], w["cos"]), (self.sin[:, :, :], w["sin"]), (self.mask[:, :], w["mask"])):
            sp.dma_start(dst, src).then_inc(self.consts_loaded, 16)

    def units(self):
        return [(6 * b + u, b, 2 * u) for b in range(IMAGES) for u in range(6)]

    def tensor(self, pe, own):
        k, H = self.k, self.HEADS
        norm_tensor(k, pe, self.norm)
        pe.wait_ge(self.consts_loaded, 80)
        for j in range(TILES):
            for c in range(2):
                last = pe.matmul(k.tok_psum(4, D)[:, j // 2, j % 2, :], k.xnF[:, c, P * j:P * (j + 1)],
                                 self.w_qkv[:, c, 2 * D:3 * D], start=(c == 0), stop=(c == 1))
        last.then_inc(self.v_ready, 1)
        for half in range(2):
            if half == 1:
                pe.wait_ge(self.rotated, 1)
            for b in range(IMAGES):
                for c in range(2):
                    last = pe.matmul(k.ps[:, b, 0:2 * D], k.xnF[:, c, P * (2 * b + half):P * (2 * b + half + 1)],
                                     self.w_qkv[:, c, 0:2 * D], start=(c == 0), stop=(c == 1))
            last.then_inc(self.qk_ready, 1)
        pe.wait_ge(self.qk_written, 4)
        pe.wait_ge(self.v_copied, 1)
        for g in range(6):
            if g >= 4:
                pe.wait_ge(self.qkT_copied, g - 3)
            for j in range(TILES):
                last = pe.transpose(k.pair(g % 4)[:, P * j:P * (j + 1)],
                                    self.qk[:, j, 4 * g:4 * g + 4, :].rearrange("p h d -> p (h d)"), k.ident[:, :])
            last.then_inc(self.qkT_ready, 1)
        pe.wait_ge(self.qkT_copied, 6)

        def scores(unit, b, head):
            if unit >= 2:
                pe.wait_ge(self.gelu_done, unit - 1)
            for i in range(2):
                rows = slice(self.PAD * ((head + i) % 4), self.PAD * ((head + i) % 4 + 1))
                g = (head + i) // 4
                for t, s0, cols in causal_parts():
                    key = SEQ * b + P * t
                    last = pe.matmul(k.ps[:, 2 * (unit % 2) + i, cols], self.qkT[rows, 3 + g, key:key + P],
                                     self.qkT[rows, g, SEQ * b + s0:SEQ * (b + 1)], start=True, stop=True)
            last.then_inc(self.scores_ready, 1)

        def weigh(unit, b, head):
            pe.wait_ge(self.wts_ready, unit + 1)
            for i in range(2):
                h = head + i
                wt = self.wts[:, unit % 2, i, :]
                out = k.tok_psum(4, H * self.COLS)[:, b, :, self.COLS * h:self.COLS * (h + 1)]
                pe.matmul(out[:, 0, :], wt[:, 0:P], self.v[:, 2 * b, h, :], start=True, stop=True)
                pe.matmul(out[:, 1, :], wt[:, P:SEQ], self.v[:, 2 * b, h, :], start=True, stop=False)
                last = pe.matmul(out[:, 1, :], wt[:, SEQ:SPAN], self.v[:, 2 * b + 1, h, :], start=False, stop=True)
            last.then_inc(self.av_ready, 1)

        units = self.units()
        scores(*units[0])
        for n, unit in enumerate(units):
            if n + 1 < len(units):
                scores(*units[n + 1])
            weigh(*unit)
        pe.wait_ge(self.y_ready, 1)
        transpose_tokens(k, pe, self.y).then_inc(self.yT_ready, 1)
        pe.wait_ge(self.yT_copied, 2)
        for j in range(TILES):
            for c in range(2):
                last = pe.matmul(k.tok_psum(4, D)[:, j // 2, j % 2, :], k.xnF[:, c, P * j:P * (j + 1)],
                                 self.w_proj[:, c, :], start=(c == 0), stop=(c == 1))
        last.then_inc(self.out_ready, 1)

    def scalar(self, a, own):
        k = self.k
        norm_scalar(k, a, self.norm)
        a.wait_ge(self.v_ready, 1)
        for half in range(2):
            last = a.copy(self.v[:, half::2, :, 0:self.HEAD],
                          k.tok_psum(4, D)[:, :, half, :].rearrange("p b (h d) -> p b h d", d=self.HEAD))
        last.then_inc(self.v_copied, 1)
        for g in range(6):
            a.wait_ge(self.qkT_ready, g + 1)
            a.copy(self.qkT[:, g, :], k.pair(g % 4)).then_inc(self.qkT_copied, 1)
        for unit in range(len(self.units())):
            a.wait_ge(self.scores_ready, unit + 1)
            if unit >= 2:
                a.wait_ge(self.ratio_ready, unit - 1)
            a.activation(self.inv[:, unit % 2, :, :], k.ps[:, 2 * (unit % 2):2 * (unit % 2) + 2, 0:SPAN],
                         ACT.Abs).then_inc(self.abs_done, 1)
            own(a.activation(self.gelu[:, unit % 2, :, :], k.ps[:, 2 * (unit % 2):2 * (unit % 2) + 2, 0:SPAN],
                             ACT.Gelu, scale=self.TURN))
            a.activation(self.gelu[:, unit % 2, :, :], self.gelu[:, unit % 2, :, :], ACT.Abs).then_inc(self.gelu_done, 1)
        a.wait_ge(self.yT_ready, 1)
        a.copy(k.xnF[:, 0, :], k.pair(0, DH)).then_inc(self.yT_copied, 1)

    def vector(self, v, own):
        k, H, G = self.k, self.HEADS, 2 * self.HEADS
        v.memset(self.qk[:, :, :, self.HEAD:], 0.0)
        v.memset(self.v[:, :, :, self.HEAD:], 1.0)
        norm_vector(k, v, own, self.norm)
        v.wait_ge(self.consts_loaded, 80)
        for half in range(2):
            v.wait_ge(self.qk_ready, half + 1)
            x = k.ps[:, 0:IMAGES, 0:2 * D].rearrange("p b (h d e) -> p b h d e", h=G, e=2)
            wide = [P, IMAGES, G, 8]
            for i, (first, second, op) in enumerate(((self.cos, self.sin, ALU.subtract), (self.sin, self.cos, ALU.add))):
                for b in range(IMAGES):
                    v.tensor_tensor(self.t1[:, b], x[:, b, :, :, 0], first[:, half, :].unsqueeze(1).to_broadcast(wide[0:1] + wide[2:]), ALU.mult)
                    last = v.tensor_tensor(self.t2[:, b], x[:, b, :, :, 1], second[:, half, :].unsqueeze(1).to_broadcast(wide[0:1] + wide[2:]), ALU.mult)
                if i == 0:
                    own(last)
                else:
                    last.then_inc(self.rotated, 1)
                    v.wait_ge(self.rotated, half + 1)
                v.tensor_tensor(self.qk[:, half::2, :, 8 * i:8 * i + 8], self.t1[:, :, :, :], self.t2[:, :, :, :],
                                op).then_inc(self.qk_written, 1)
                v.wait_ge(self.qk_written, 2 * half + i + 1)
        for unit in range(len(self.units())):
            v.wait_ge(self.abs_done, unit + 1)
            inv = self.inv[:, unit % 2, :, :]
            own(v.tensor_scalar(inv, inv, self.TINY, None, ALU.max))
            own(v.reciprocal(inv, inv))
            v.wait_ge(self.gelu_done, unit + 1)
            if unit >= 2:
                v.wait_ge(self.wts_ready, unit - 1)
            own(v.scalar_tensor_tensor(out=self.ratio[:, unit % 2, :, :], in0=self.gelu[:, unit % 2, :, :],
                                       scalar=self.TINY * self.TURN / 2, in1=inv, op0=ALU.max, op1=ALU.mult))
            ratio = self.ratio[:, unit % 2, :, :]
            own(v.tensor_scalar(ratio, ratio, 2 / self.TURN, -1.0, ALU.mult, ALU.add))
            v.tensor_scalar(ratio, ratio, self.LEAST, 1.0, ALU.max, ALU.add).then_inc(self.ratio_ready, 1)
            v.wait_ge(self.ratio_ready, unit + 1)
        v.wait_ge(self.av_ready, len(self.units()))
        sums = k.tok_psum(4, H * self.COLS).rearrange("p b t (h d) -> p b t h d", d=self.COLS)
        for half in range(2):
            last = v.tensor_scalar(self.den[:, half::2, :], sums[:, :, half, :, self.HEAD], self.FLOOR, None, ALU.max)
        own(last)
        own(v.reciprocal(self.den[:, :, :], self.den[:, :, :]))
        for half in range(2):
            last = v.tensor_tensor(self.y[:, half::2, :].rearrange("p b (h d) -> p b h d", d=self.HEAD),
                                   sums[:, :, half, :, 0:self.HEAD],
                                   self.den[:, half::2, :].unsqueeze(3).to_broadcast([P, IMAGES, H, self.HEAD]), ALU.mult)
        last.then_inc(self.y_ready, 1)
        v.wait_ge(self.yT_ready, 1)
        v.tensor_copy(k.xnF[:, 1, :], k.pair(1, DH)).then_inc(self.yT_copied, 1)
        v.wait_ge(self.out_ready, 1)
        v.tensor_tensor(pairs_of(k.h[:, :, :]), pairs_of(k.h[:, :, :]), k.tok_psum(4, D), ALU.add).then_inc(k.h_ready, 1)

    def pool(self, g, own):
        g.wait_ge(self.consts_loaded, 80)
        for unit in range(len(self.units())):
            g.wait_ge(self.ratio_ready, unit + 1)
            if unit >= 2:
                g.wait_ge(self.av_ready, unit - 1)
            g.tensor_tensor(self.wts[:, unit % 2, :, :], self.ratio[:, unit % 2, :, :],
                            self.mask[:, :].unsqueeze(1).to_broadcast([P, 2, SPAN]), ALU.mult).then_inc(self.wts_ready, 1)


class Retention:

    def __init__(self, k, name, norm, w):
        self.k, self.norm, self.w = k, norm, w
        sb, s = (lambda x, shape, t=F32: k.sb(name + "_" + x, shape, t)), (lambda x: k.sem(name + "_" + x))
        self.w_qkv, self.qk_b, self.v_b = sb("w_qkv", [DH, 2, 3 * D]), sb("qk_b", [DH, 4]), sb("v_b", [P, D])
        self.mask = sb("mask", [P, SPAN])
        self.qk = sb("qk", [DH, 4, TOKENS])
        self.v = sb("v", [P, TILES, D])
        self.wts = sb("wts", [P, IMAGES, SPAN])
        self.consts_loaded, self.qk_ready, self.qk_copied = s("consts_loaded"), s("qk_ready"), s("qk_copied")
        self.v_ready, self.v_copied = s("v_ready"), s("v_copied")
        self.scores_ready, self.wts_ready, self.out_ready = s("scores_ready"), s("wts_ready"), s("out_ready")

    def sync(self, sp):
        w = self.w
        sp.wait_ge(self.k.h_ready, self.norm)
        for dst, src in ((self.w_qkv[:, :, :], w["qkv"].rearrange("(c p) m -> p c m", p=DH)), (self.qk_b[:, :], w["qk_b"]),
                         (self.v_b[:, :], w["v_b"].to_broadcast([P, D])), (self.mask[:, :], w["mask"])):
            sp.dma_start(dst, src).then_inc(self.consts_loaded, 16)

    def tensor(self, pe, own):
        k = self.k
        norm_tensor(k, pe, self.norm)
        pe.wait_ge(self.consts_loaded, 64)
        for m in range(4):
            for c in range(2):
                for t in range(2):
                    last = pe.matmul(k.pair(m, DH)[:, BANK * t:BANK * (t + 1)], self.w_qkv[:, c, DH * m:DH * (m + 1)],
                                     k.xnF[:, c, BANK * t:BANK * (t + 1)], start=(c == 0), stop=(c == 1))
            last.then_inc(self.qk_ready, 1)
        pe.wait_ge(self.qk_copied, 2)
        for j in range(TILES):
            for c in range(2):
                last = pe.matmul(k.tok_psum(0, D)[:, j // 2, j % 2, :], k.xnF[:, c, P * j:P * (j + 1)],
                                 self.w_qkv[:, c, 2 * D:3 * D], start=(c == 0), stop=(c == 1))
        last.then_inc(self.v_ready, 1)
        pe.wait_ge(self.qk_copied, 4)
        for b in range(IMAGES):
            for t, s0, cols in causal_parts():
                key = SEQ * b + P * t
                for c in range(2):
                    last = pe.matmul(k.ps[:, 4 + b, cols], self.qk[:, 2 + c, key:key + P],
                                     self.qk[:, c, SEQ * b + s0:SEQ * (b + 1)], start=(c == 0), stop=(c == 1))
            last.then_inc(self.scores_ready, 1)
        pe.wait_ge(self.v_copied, 1)
        for b in range(IMAGES):
            pe.wait_ge(self.wts_ready, b + 1)
            out, wt = k.tok_psum(0, D)[:, b], self.wts[:, b, :]
            pe.matmul(out[:, 0, :], wt[:, 0:P], self.v[:, 2 * b, :], start=True, stop=True)
            pe.matmul(out[:, 1, :], wt[:, P:SEQ], self.v[:, 2 * b, :], start=True, stop=False)
            last = pe.matmul(out[:, 1, :], wt[:, SEQ:SPAN], self.v[:, 2 * b + 1, :], start=False, stop=True)
        last.then_inc(self.out_ready, 1)

    def scalar(self, a, own):
        k = self.k
        norm_scalar(k, a, self.norm)
        a.wait_ge(self.consts_loaded, 64)
        for m in range(4):
            a.wait_ge(self.qk_ready, m + 1)
            a.activation(self.qk[:, m, :], k.pair(m, DH), ACT.Identity, bias=self.qk_b[:, m:m + 1]).then_inc(self.qk_copied, 1)

    def vector(self, v, own):
        k = self.k
        norm_vector(k, v, own, self.norm)
        v.wait_ge(self.consts_loaded, 64)
        v.wait_ge(self.v_ready, 1)
        for half in range(2):
            last = v.tensor_tensor(self.v[:, half::2, :], k.tok_psum(0, D)[:, :, half, :],
                                   self.v_b[:, :].unsqueeze(1).to_broadcast([P, IMAGES, D]), ALU.add)
        last.then_inc(self.v_copied, 1)
        for b in range(IMAGES):
            v.wait_ge(self.scores_ready, b + 1)
            v.scalar_tensor_tensor(out=self.wts[:, b, :], in0=k.ps[:, 4 + b, 0:SPAN], scalar=D ** -0.5, in1=self.mask[:, :],
                                   op0=ALU.mult, op1=ALU.mult).then_inc(self.wts_ready, 1)
        v.wait_ge(self.out_ready, 1)
        v.tensor_tensor(pairs_of(k.h[:, :, :]), pairs_of(k.h[:, :, :]), k.tok_psum(0, D), ALU.add).then_inc(k.h_ready, 1)

    def pool(self, g, own):
        pass



class Resolvent:
    KEEP = int(512 * (1.0 - 0.6))
    V_MAX, CLAMP, START, Z_MIN = 3.0, 10.0, 1e18, -88.0
    ROWS, BACK, STEPS = 36, 32, 8

    def __init__(self, k, name, w, y):
        self.k, self.w, self.y = k, w, y
        sb, s = (lambda x, shape, t=F32: k.sb(name + "_" + x, shape, t)), (lambda x: k.sem(name + "_" + x))
        self.rows, self.scalars = sb("rows", [P, 5, D]), sb("scalars", [P, 3])
        self.turned, self.signs = sb("turned", [P, P]), sb("signs", [self.ROWS, SEQ])
        self.prod = sb("prod", [P, TILES, D])
        self.v, self.z, self.score = sb("v", [P, TILES]), sb("z", [P, TILES]), sb("score", [P, TILES])
        self.above, self.greater, self.mask = sb("above", [P, TILES]), sb("greater", [P, TILES, SEQ]), sb("mask", [P, TILES])
        self.d, self.hist = sb("d", [self.ROWS, SEQ, 2]), sb("hist", [self.ROWS, SEQ, 2])
        self.d_block, self.block = sb("d_block", [self.ROWS, self.STEPS, 2]), sb("block", [self.ROWS, self.STEPS, 2])
        self.sq, self.den = sb("sq", [self.ROWS, 2]), sb("den", [self.ROWS, 1])
        self.back = sb("back", [P, 16])
        self.c = sb("c", [P, 2, 2, IMAGES])
        self.c2 = sb("c2", [P, 2, 2, IMAGES])
        self.cd = sb("cd", [P, 2, IMAGES])
        self.feat = sb("feat", [P, 2, TILES])
        self.mix = sb("mix", [P, TILES, D])
        self.consts_loaded = s("consts_loaded")
        self.z_ready, self.z_exp, self.score_ready, self.scores_spread = s("z_ready"), s("z_exp"), s("score_ready"), s("scores_spread")
        self.v_ready, self.vT_ready, self.hist_ready = s("v_ready"), s("vT_ready"), s("hist_ready")
        self.fwd_ready, self.back_copied, self.back_ready = s("fwd_ready"), s("back_copied"), s("back_ready")

    def sync(self, sp):
        w = self.w
        for dst, src in ((self.rows[:, :, :].rearrange("p r d -> p (r d)"), w["rows"].to_broadcast([P, 5 * D])),
                         (self.scalars[:, :], w["scalars"].to_broadcast([P, 3])),
                         (self.turned[:, :], w["turned"]), (self.signs[:, :], w["signs"])):
            sp.dma_start(dst, src).then_inc(self.consts_loaded, 16)

    def tensor(self, pe, own):
        k = self.k
        pe.wait_ge(self.score_ready, 1)
        pe.wait_ge(self.consts_loaded, 64)
        for j in range(TILES):
            last = pe.matmul(k.pair(0)[:, P * j:P * (j + 1)], self.score[:, j:j + 1].to_broadcast([P, P]), k.ident[:, :],
                             start=True, stop=True)
        last.then_inc(self.scores_spread, 1)
        pe.wait_ge(self.v_ready, 1)
        for half in range(2):
            pe.matmul(k.ps[0:IMAGES, 2, P * half:P * (half + 1)], self.v[:, half::2], k.ident[:, :], start=True, stop=True)
            last = pe.matmul(k.ps[self.BACK:self.ROWS, 2, P * (1 - half):P * (2 - half)], self.v[:, half::2], self.turned[:, :],
                             start=True, stop=True)
        last.then_inc(self.vT_ready, 1)
        pe.wait_ge(self.hist_ready, 1)
        for part in range(2):
            for half in range(2):
                cols = slice(8 * part + 4 * half, 8 * part + 4 * half + 4)
                turned = slice(8 * part + 4 * (1 - half), 8 * part + 4 * (1 - half) + 4)
                pe.matmul(k.ps[:, 3, cols], self.hist[0:IMAGES, P * half:P * (half + 1), part], k.ident[0:IMAGES, 0:IMAGES],
                          start=True, stop=True)
                last = pe.matmul(k.ps[:, 4, turned], self.hist[self.BACK:self.ROWS, P * half:P * (half + 1), part],
                                 k.ident[self.BACK:self.ROWS, self.BACK:self.ROWS], start=True, stop=True)
        last.then_inc(self.fwd_ready, 1)
        pe.wait_ge(self.back_copied, 1)
        pe.matmul(k.ps[:, 5, 0:16], self.turned[:, :], self.back[:, :], start=True, stop=True).then_inc(self.back_ready, 1)

    def scalar(self, a, own):
        a.wait_ge(self.z_ready, 1)
        a.activation(self.z[:, :], self.z[:, :], ACT.Exp, scale=-1.0).then_inc(self.z_exp, 1)

    def vector(self, v, own):
        k = self.k
        v.wait_ge(self.consts_loaded, 64)
        for j in range(TILES):
            last = v.tensor_tensor_reduce(self.prod[:, j, :], k.xn[:, j, :], self.rows[:, 1, :], 1.0, 0.0, ALU.mult, ALU.add,
                                          self.z[:, j:j + 1])
        own(last)
        v.tensor_scalar(self.z[:, :], self.z[:, :], self.scalars[:, 1:2], self.Z_MIN, ALU.add, ALU.max).then_inc(self.z_ready, 1)
        for j in range(TILES):
            last = v.tensor_tensor_reduce(self.prod[:, j, :], self.y[:, j, :], self.rows[:, 0, :], 1.0, 0.0, ALU.mult, ALU.add,
                                          self.v[:, j:j + 1])
        own(last)
        own(v.tensor_scalar(self.v[:, :], self.v[:, :], self.scalars[:, 0:1], None, ALU.add))
        v.tensor_scalar(self.v[:, :], self.v[:, :], -self.V_MAX, self.V_MAX, ALU.max, ALU.min).then_inc(self.v_ready, 1)
        v.wait_ge(self.z_exp, 1)
        own(v.tensor_scalar(self.score[:, :], self.z[:, :], 1.0, None, ALU.add))
        v.reciprocal(self.score[:, :], self.score[:, :]).then_inc(self.score_ready, 1)
        v.wait_ge(self.scores_spread, 1)
        for j in range(TILES):
            b = j // 2
            last = v.tensor_scalar(self.greater[:, j, :], k.pair(0)[:, SEQ * b:SEQ * (b + 1)], self.score[:, j:j + 1], 0.0,
                                   ALU.is_gt, ALU.add, accum_out=self.above[:, j:j + 1])
        own(last)
        own(v.tensor_scalar(self.mask[:, :], self.above[:, :], self.KEEP - 0.5, None, ALU.is_lt))
        own(v.memset(self.d[:, :, :], 1.0))
        own(v.memset(self.block[:, :, :], 0.0))
        own(v.memset(self.block[:, self.STEPS - 1, 0:1], self.START))
        v.wait_ge(self.vT_ready, 1)
        for rows in (slice(0, IMAGES), slice(self.BACK, self.ROWS)):
            last = v.tensor_tensor(self.d[rows, :, 0], k.ps[rows, 2, 0:SEQ], self.signs[rows, :], ALU.mult)
        own(last)
        with own.loop(SEQ // self.STEPS, 3 * self.STEPS + 2) as i:
            at = bass.ds(i, 1)
            blocks = lambda t: t[:, :, :].rearrange("p (o s) c -> p o (s c)", s=self.STEPS)[:, at, :].rearrange("p o s -> p (o s)")
            flat = lambda t: t[:, :, :].rearrange("p s c -> p (s c)")
            own(v.tensor_copy(flat(self.d_block), blocks(self.d)))
            for s in range(self.STEPS):
                state = self.block[:, (s - 1) % self.STEPS, :]
                own(v.tensor_tensor_reduce(self.sq[:, :], state, state, 1.0, 0.0, ALU.mult, ALU.add, self.den[:, :]))
                own(v.reciprocal(self.den[:, :], self.den[:, :]))
                own(v.scalar_tensor_tensor(out=self.block[:, s, :], in0=state, scalar=self.den[:, :], in1=self.d_block[:, s, :],
                                           op0=ALU.mult, op1=ALU.subtract))
            own(v.tensor_copy(blocks(self.hist), flat(self.block)))
        v.scalar_tensor_tensor(out=self.hist[:, :, 0], in0=self.hist[:, :, 0], scalar=-1.0, in1=self.signs[:, :],
                               op0=ALU.mult, op1=ALU.mult).then_inc(self.hist_ready, 1)
        v.wait_ge(self.fwd_ready, 1)
        v.tensor_copy(self.back[:, :], k.ps[:, 4, 0:16]).then_inc(self.back_copied, 1)
        by_token = lambda t: t.rearrange("p (part half b) -> p part half b", part=2, half=2)
        own(v.tensor_copy(self.c[:, :, :, :], by_token(k.ps[:, 3, 0:16])))
        v.wait_ge(self.back_ready, 1)
        own(v.tensor_tensor(self.c[:, :, :, :], self.c[:, :, :, :], by_token(k.ps[:, 5, 0:16]), ALU.add))
        half_image = lambda t: t.rearrange("p (b half) -> p half b", half=2)
        v.tensor_tensor(self.c[:, 0], self.c[:, 0], half_image(self.v[:, :]), ALU.subtract)
        own(v.tensor_scalar(self.c[:, 1], self.c[:, 1], 1.0, None, ALU.add))
        own(v.tensor_tensor(self.c2[:, :, :, :], self.c[:, :, :, :], self.c[:, :, :, :], ALU.mult))
        own(v.tensor_tensor(self.cd[:, :, :], self.c2[:, 0], self.c2[:, 1], ALU.add))
        own(v.reciprocal(self.cd[:, :, :], self.cd[:, :, :]))
        v.tensor_tensor(self.c[:, 0], self.c[:, 0], self.cd[:, :, :], ALU.mult)
        own(v.scalar_tensor_tensor(out=self.c[:, 1], in0=self.c[:, 1], scalar=-1.0, in1=self.cd[:, :, :], op0=ALU.mult, op1=ALU.mult))
        for part in range(2):
            last = v.tensor_tensor(half_image(self.feat[:, part, :]), self.c[:, part], half_image(self.mask[:, :]), ALU.mult)
        own(last)
        own(v.tensor_scalar(self.feat[:, :, :], self.feat[:, :, :], -self.CLAMP, self.CLAMP, ALU.max, ALU.min))
        for step in range(2):
            for j in range(TILES):
                if step == 0:
                    last = v.scalar_tensor_tensor(out=self.mix[:, j, :], in0=self.rows[:, 2, :], scalar=self.feat[:, 0, j:j + 1],
                                                  in1=self.rows[:, 4, :], op0=ALU.mult, op1=ALU.add)
                else:
                    last = v.scalar_tensor_tensor(out=self.mix[:, j, :], in0=self.rows[:, 3, :], scalar=self.feat[:, 1, j:j + 1],
                                                  in1=self.mix[:, j, :], op0=ALU.mult, op1=ALU.add)
            own(last)
        own(v.scalar_tensor_tensor(out=self.y[:, :, :], in0=self.mix[:, :, :], scalar=self.scalars[:, 2:3], in1=self.y[:, :, :],
                                   op0=ALU.mult, op1=ALU.add))
        v.tensor_tensor(k.h[:, :, :], k.h[:, :, :], self.y[:, :, :], ALU.add).then_inc(k.h_ready, 1)

    def pool(self, g, own):
        pass



def softmax_vector(k, v, own, logits, exp_in, sums, max_ready, exp_ready, n=1):
    wide = list(exp_in.shape)
    own(v.tensor_reduce(sums, logits, AX.X, ALU.max))
    v.tensor_tensor(exp_in, logits, sums.unsqueeze(2).to_broadcast(wide), ALU.subtract).then_inc(max_ready, 1)
    v.wait_ge(exp_ready, n)
    own(v.tensor_reduce(sums, exp_in, AX.X, ALU.add))
    own(v.reciprocal(sums, sums))
    own(v.tensor_tensor(exp_in, exp_in, sums.unsqueeze(2).to_broadcast(wide), ALU.mult))


def top_vector(v, own, values, rounds, low, rev, best, hit, first, chosen):
    wide = list(values.shape)
    for r in range(rounds):
        own(v.tensor_reduce(best, values, AX.X, ALU.max))
        own(v.tensor_tensor(hit, values, best.unsqueeze(2).to_broadcast(wide), ALU.is_equal))
        own(v.tensor_tensor(hit, hit, rev.unsqueeze(1).to_broadcast(wide), ALU.mult))
        own(v.tensor_reduce(best, hit, AX.X, ALU.max))
        first_hit = chosen if r == 0 else first
        own(v.tensor_tensor(first_hit, hit, best.unsqueeze(2).to_broadcast(wide), ALU.is_equal))
        if r + 1 < rounds:
            own(v.scalar_tensor_tensor(out=values, in0=first_hit, scalar=low, in1=values, op0=ALU.mult, op1=ALU.add))
        if r > 0:
            own(v.tensor_tensor(chosen, chosen, first, ALU.add))



HIDDEN = 4 * D
CHUNKS = HIDDEN // P


class Experts:
    def __init__(self, k, name, norm, w, experts, top, gelu, keep_xn, tail=None):
        self.k, self.norm, self.w, self.n, self.top = k, norm, w, experts, top
        self.gelu, self.keep_xn, self.tail = gelu, keep_xn, tail
        sb = k.sb
        self.wr = sb(name + "_wr", [DH, 2, experts], F32)
        self.rb = sb(name + "_rb", [P, experts], F32)
        self.rev = sb(name + "_rev", [P, experts], F32)
        self.b1 = sb(name + "_b1", [P, experts // 2, 2 * CHUNKS], F32)
        self.b2 = sb(name + "_b2", [experts, D], F32)
        self.w1 = sb(name + "_w1", [DH, 2, 2, HIDDEN], F32)
        self.w2 = sb(name + "_w2", [P, 2, CHUNKS, D], F32)
        self.probs = sb(name + "_probs", [P, TILES, experts], F32)
        self.values = sb(name + "_values", [P, TILES, experts], F32)
        self.hit = sb(name + "_hit", [P, TILES, experts], F32)
        self.first = sb(name + "_first", [P, TILES, experts], F32)
        self.gates = sb(name + "_gates", [P, TILES, experts], F32)
        self.gates_T = sb(name + "_gates_T", [experts, TOKENS], F32)
        self.best = sb(name + "_best", [P, TILES], F32)
        self.hid = sb(name + "_hid", [P, 3, TOKENS], F32)
        self.y = sb(name + "_y", [P, TILES, D], F32)
        s = lambda x: k.sem("experts_" + x)
        self.before, self.turn, self.consts = k.experts, k.expert_stages, k.expert_consts
        self.consts += 16 * (5 if "router_b" in w else 4)
        k.experts, k.expert_stages, k.expert_consts = self.before + experts, self.turn + 1, self.consts
        self.consts_loaded = s("consts_loaded")
        self.w1_loaded = [s("w1_loaded0"), s("w1_loaded1")]
        self.w2_loaded = [s("w2_loaded0"), s("w2_loaded1")]
        self.logits_ready, self.max_ready, self.exp_ready = s("logits_ready"), s("max_ready"), s("exp_ready")
        self.gates_ready, self.gates_T_ready, self.gates_T_copied = s("gates_ready"), s("gates_T_ready"), s("gates_T_copied")
        self.b2_ready = s("b2_ready")
        self.hid_ready, self.gelu_done = s("hid_ready"), s("gelu_done")
        self.expert_ready = s("expert_ready")
        self.y_added = s("y_added")

    def each(self, eng, body):
        with eng.Fori(0, self.n // 2) as two:
            body(two, 0)
            body(two, 1)

    def sync(self, sp):
        w = self.w
        sp.wait_ge(self.k.h_ready, self.norm)
        loads = [(self.wr[:, :, :], w["router_T"].rearrange("(c p) e -> p c e", p=DH)),
                 (self.rev[:, :], w["rev"].to_broadcast([P, self.n])),
                 (self.b1[:, :, :], w["b1"]), (self.b2[:, :], w["b2"])]
        if "router_b" in w:
            loads.append((self.rb[:, :], w["router_b"].to_broadcast([P, self.n])))
        for dst, src in loads:
            sp.dma_start(dst, src).then_inc(self.consts_loaded, 16)

        def load(two, buf):
            sp.dma_start(self.w1[:, buf, :, :], pick_of_two(w["W1"], two, buf).rearrange("(c p) m -> p c m", p=DH)).then_inc(self.w1_loaded[buf], 16)
            sp.dma_start(self.w2[:, buf, :, :], pick_of_two(w["W2"], two, buf).rearrange("(c p) m -> p c m", p=P)).then_inc(self.w2_loaded[buf], 16)

        load(0, 0)
        load(0, 1)
        with sp.Fori(1, self.n // 2) as two:
            for buf in range(2):
                sp.wait_ge(self.expert_ready, self.before + 2 * two + buf - 1)
                load(two, buf)
        if self.tail:
            self.tail.sync(sp)

    def tensor(self, pe, own):
        k = self.k
        norm_tensor(k, pe, self.norm)
        pe.wait_ge(self.consts_loaded, self.consts)
        logits = k.ps[:, 4, 0:TILES * self.n].rearrange("p (j e) -> p j e", e=self.n)
        for j in range(TILES):
            for c in range(2):
                last = pe.matmul(logits[:, j, :], k.xnF[:, c, P * j:P * (j + 1)], self.wr[:, c, :],
                                 start=(c == 0), stop=(c == 1))
        last.then_inc(self.logits_ready, 1)
        pe.wait_ge(self.gates_ready, self.turn + 1)
        for j in range(TILES):
            last = pe.transpose(k.pair(0, self.n)[:, P * j:P * (j + 1)], self.gates[:, j, :], k.ident[:, :])
        last.then_inc(self.gates_T_ready, 1)
        pe.wait_ge(self.gates_T_copied, self.turn + 1)
        for j in range(TILES):
            last = pe.matmul(k.tok_psum(4, D)[:, j // 2, j % 2, :], self.gates_T[:, P * j:P * (j + 1)], self.b2[:, :],
                             start=True, stop=True)
        last.then_inc(self.b2_ready, 1)

        def expert(two, buf):
            e = self.before + 2 * two + buf

            def down(m):
                pe.wait_ge(self.gelu_done, 6 * e + m + 1)
                if m == 0:
                    pe.wait_ge(self.w2_loaded[buf], 8 * self.before + 16 * two + 16)
                    pe.wait_ge(self.y_added, self.turn + e + 1)
                for j in range(TILES):
                    last = pe.matmul(k.tok_psum(4, D)[:, j // 2, j % 2, :], self.hid[:, m % 3, P * j:P * (j + 1)],
                                     self.w2[:, buf, m, :], start=(m == 0 and j % 2 == 0), stop=(m == CHUNKS - 1),
                                     skip_group_check=True)
                return last

            pe.wait_ge(self.w1_loaded[buf], 8 * self.before + 16 * two + 16)
            for m in range(CHUNKS):
                if m >= 2:
                    pe.wait_ge(self.gelu_done, 6 * e + m - 1)
                for c in range(2):
                    for t in range(2):
                        last = pe.matmul(k.pair(m % 2)[:, BANK * t:BANK * (t + 1)], self.w1[:, buf, c, P * m:P * (m + 1)],
                                         k.xnF[:, c, BANK * t:BANK * (t + 1)], start=(c == 0), stop=(c == 1))
                last.then_inc(self.hid_ready, 1)
                if m >= 1:
                    down(m - 1)
            down(CHUNKS - 1).then_inc(self.expert_ready, 1)

        self.each(pe, expert)
        if self.tail:
            self.tail.tensor(pe, own)

    def scalar(self, a, own):
        k = self.k
        norm_scalar(k, a, self.norm)
        a.wait_ge(self.max_ready, self.turn + 1)
        a.activation(self.probs[:, :, :], self.probs[:, :, :], ACT.Exp).then_inc(self.exp_ready, 1)
        a.wait_ge(self.gates_T_ready, self.turn + 1)
        a.copy(self.gates_T[:, :], k.pair(0, self.n)).then_inc(self.gates_T_copied, 1)

        def expert(two, buf):
            e = self.before + 2 * two + buf
            for m in range(CHUNKS):
                a.wait_ge(self.hid_ready, 6 * e + m + 1)
                a.activation(self.hid[:, m % 3, :], k.pair(m % 2), self.gelu,
                             bias=column(self.b1, two, CHUNKS * buf + m)).then_inc(self.gelu_done, 1)

        self.each(a, expert)
        if self.tail:
            self.tail.scalar(a, own)

    def vector(self, v, own):
        k = self.k
        norm_vector(k, v, own, self.norm)
        v.wait_ge(self.logits_ready, self.turn + 1)
        logits = k.ps[:, 4, 0:TILES * self.n].rearrange("p (j e) -> p j e", e=self.n)
        if "router_b" in self.w:
            v.wait_ge(self.consts_loaded, self.consts)
            own(v.tensor_tensor(self.values[:, :, :], logits, self.rb[:, :].unsqueeze(1).to_broadcast([P, TILES, self.n]), ALU.add))
            logits = self.values[:, :, :]
        softmax_vector(k, v, own, logits, self.probs[:, :, :], self.best[:, :], self.max_ready, self.exp_ready, self.turn + 1)
        own(v.tensor_copy(self.values[:, :, :], self.probs[:, :, :]))
        top_vector(v, own, self.values[:, :, :], self.top, -4.0, self.rev[:, :], self.best[:, :], self.hit[:, :, :],
                   self.first[:, :, :], self.gates[:, :, :])
        v.tensor_tensor(self.gates[:, :, :], self.gates[:, :, :], self.probs[:, :, :], ALU.mult).then_inc(self.gates_ready, 1)
        v.wait_ge(self.gates_ready, self.turn + 1)
        v.wait_ge(self.b2_ready, self.turn + 1)
        y = pairs_of(self.y[:, :, :])
        if self.keep_xn:
            v.tensor_tensor(y, pairs_of(k.xn[:, :, :]), k.tok_psum(4, D), ALU.add).then_inc(self.y_added, 1)
        else:
            v.tensor_copy(y, k.tok_psum(4, D)).then_inc(self.y_added, 1)

        def expert(two, buf):
            e = self.before + 2 * two + buf
            v.wait_ge(self.expert_ready, e + 1)
            v.wait_ge(self.y_added, self.turn + e + 1)
            for j in range(TILES):
                last = v.scalar_tensor_tensor(out=self.y[:, j, :], in0=k.tok_psum(4, D)[:, j // 2, j % 2, :],
                                              scalar=column(self.gates[:, j, :].rearrange("p (e b) -> p e b", b=2), two, buf), in1=self.y[:, j, :],
                                              op0=ALU.mult, op1=ALU.add)
            last.then_inc(self.y_added, 1)

        self.each(v, expert)
        v.wait_ge(self.y_added, self.before + self.n + self.turn + 1)
        if self.tail:
            self.tail.vector(v, own)
        else:
            v.tensor_tensor(k.h[:, :, :], k.h[:, :, :], self.y[:, :, :], ALU.add).then_inc(k.h_ready, 1)

    def pool(self, g, own):
        if self.tail:
            self.tail.pool(g, own)


def column(t, i, j):
    s = [slice(x, x + 1) if isinstance(x, int) else bass.ds(x, 1) for x in (i, j)]
    return t[:, s[0], s[1]].rearrange("p a b -> p (a b)")



class GatedExperts:
    ROUTED, GROUPS, TOP_GROUPS, TOP, WIDTH = 8, 4, 2, 2, 96
    ALPHA, LIMIT = 1.702, 7.0
    MASKED = -1e30

    def __init__(self, k, name, norm, w):
        self.k, self.norm, self.w = k, norm, w
        n = self.n = self.ROUTED + 1
        sb, s = (lambda x, shape, t=F32: k.sb(name + "_" + x, shape, t)), (lambda x: k.sem(name + "_" + x))
        self.wr = sb("wr", [DH, 2, self.ROUTED])
        self.gate_b = sb("gate_b", [P, self.ROUTED])
        self.rev8, self.rev4 = sb("rev8", [P, 8]), sb("rev4", [P, 4])
        self.b1, self.b3 = sb("b1", [DH, n, 2]), sb("b3", [DH, n, 2])
        self.b2 = sb("b2", [n, D])
        self.w1, self.w3 = sb("w1", [DH, 2, 2, D]), sb("w3", [DH, 2, 2, D])
        self.w2 = sb("w2", [DH, 2, D])
        self.probs, self.scores = sb("probs", [P, TILES, 8]), sb("scores", [P, TILES, 8])
        self.hit, self.first, self.chosen = sb("hit", [P, TILES, 8]), sb("first", [P, TILES, 8]), sb("chosen", [P, TILES, 8])
        self.group, self.group_first = sb("group", [P, TILES, 4]), sb("group_first", [P, TILES, 4])
        self.group_hit, self.kept = sb("group_hit", [P, TILES, 4]), sb("kept", [P, TILES, 4])
        self.gates = sb("gates", [P, TILES, n])
        self.gates_T = sb("gates_T", [n, TOKENS])
        self.best = sb("best", [P, TILES])
        self.lin = sb("lin", [DH, 2, TOKENS])
        self.xg, self.xl = sb("xg", [DH, TOKENS]), sb("xl", [DH, TOKENS])
        self.sig = sb("sig", [DH, TOKENS])
        self.g = sb("g", [DH, 2, TOKENS])
        self.y = sb("y", [P, TILES, D])
        self.consts_loaded = s("consts_loaded")
        self.weights_loaded = [s("weights_loaded0"), s("weights_loaded1")]
        self.logits_ready, self.max_ready, self.exp_ready = s("logits_ready"), s("max_ready"), s("exp_ready")
        self.gates_ready, self.gates_T_ready, self.gates_T_copied = s("gates_ready"), s("gates_T_ready"), s("gates_T_copied")
        self.b2_ready = s("b2_ready")
        self.h1_ready, self.h3_ready = s("h1_ready"), s("h3_ready")
        self.lin_done, self.prod_done = s("lin_done"), s("prod_done")
        self.xg_ready, self.sig_ready, self.g_ready = s("xg_ready"), s("sig_ready"), s("g_ready")
        self.out_ready, self.y_added = s("out_ready"), s("y_added")

    def sync(self, sp):
        k, w = self.k, self.w
        sp.wait_ge(k.h_ready, self.norm)
        loads = [(self.wr[:, :, :], w["router_T"].rearrange("(c p) e -> p c e", p=DH)),
                 (self.gate_b[:, :], w["gate_b"].to_broadcast([P, 8])), (self.rev8[:, :], w["rev8"].to_broadcast([P, 8])),
                 (self.rev4[:, :], w["rev4"].to_broadcast([P, 4])), (self.b1[:, :, :], w["b1"]), (self.b3[:, :, :], w["b3"]),
                 (self.b2[:, :], w["b2"])]
        for dst, src in loads:
            sp.dma_start(dst, src).then_inc(self.consts_loaded, 16)

        def load(row, buf):
            for dst, src in ((self.w1[:, buf], row("W1").rearrange("(c p) m -> p c m", p=DH)),
                             (self.w3[:, buf], row("W3").rearrange("(c p) m -> p c m", p=DH)), (self.w2[:, buf], row("W2"))):
                sp.dma_start(dst, src).then_inc(self.weights_loaded[buf], 16)

        load(lambda x: pick(w[x], 0), 0)
        load(lambda x: pick(w[x], 1), 1)
        with sp.Fori(0, self.n // 2 - 1) as two:
            sp.wait_ge(self.out_ready, 2 * two + 1)
            load(lambda x: pick_of_two(w[x][1:], two, 1), 0)
            sp.wait_ge(self.out_ready, 2 * two + 2)
            load(lambda x: pick_of_two(w[x][3:], two, 0), 1)
        sp.wait_ge(self.out_ready, self.n - 2)
        load(lambda x: pick(w[x], self.n - 1), 0)

    def experts(self, eng, body):
        body(None, 0, 0, 0)
        with eng.Fori(0, self.n // 2) as two:
            body(two, 0, 2 * two + 1, 1)
            body(two, 1, 2 * two + 2, 0)

    def tensor(self, pe, own):
        k = self.k
        norm_tensor(k, pe, self.norm)
        pe.wait_ge(self.consts_loaded, 16 * 7)
        for j in range(TILES):
            for c in range(2):
                last = pe.matmul(k.ps[:, 4, 8 * j:8 * j + 8], k.xnF[:, c, P * j:P * (j + 1)], self.wr[:, c, :],
                                 start=(c == 0), stop=(c == 1))
        last.then_inc(self.logits_ready, 1)
        pe.wait_ge(self.gates_ready, 1)
        for j in range(TILES):
            last = pe.transpose(k.pair(0, self.n)[:, P * j:P * (j + 1)], self.gates[:, j, :], k.ident[:, :])
        last.then_inc(self.gates_T_ready, 1)
        pe.wait_ge(self.gates_T_copied, 1)
        for j in range(TILES):
            last = pe.matmul(k.tok_psum(4, D)[:, j // 2, j % 2, :], self.gates_T[:, P * j:P * (j + 1)], self.b2[:, :],
                             start=True, stop=True)
        last.then_inc(self.b2_ready, 1)

        def up(w, buf, odd, pair):
            for c in range(2):
                for t in range(2):
                    last = pe.matmul(k.pair(pair, DH)[:, BANK * t:BANK * (t + 1)], w[:, buf, c, DH * odd:DH * (odd + 1)],
                                     k.xnF[:, c, BANK * t:BANK * (t + 1)], start=(c == 0), stop=(c == 1))
            return last

        def down(e, buf):
            pe.wait_ge(self.g_ready, e + 1)
            pe.wait_ge(self.y_added, e + 1)
            for j in range(TILES):
                last = pe.matmul(k.tok_psum(4, D)[:, j // 2, j % 2, :], self.g[:, buf, P * j:P * (j + 1)],
                                 self.w2[:, buf, :], start=True, stop=True)
            last.then_inc(self.out_ready, 1)

        def expert(two, place, e, buf):
            loads = 48 if two is None else 48 * two + (48 if place == 0 else 96)
            pe.wait_ge(self.weights_loaded[buf], loads)
            if two is not None:
                pe.wait_ge(self.lin_done, 2 * e)
            up(self.w1, buf, 0, 0).then_inc(self.h1_ready, 1)
            if two is not None:
                pe.wait_ge(self.prod_done, 2 * e)
            up(self.w3, buf, 0, 1).then_inc(self.h3_ready, 1)
            pe.wait_ge(self.lin_done, 2 * e + 1)
            up(self.w1, buf, 1, 0).then_inc(self.h1_ready, 1)
            if two is not None:
                down(e - 1, 1 - buf)
            pe.wait_ge(self.prod_done, 2 * e + 1)
            up(self.w3, buf, 1, 1).then_inc(self.h3_ready, 1)

        self.experts(pe, expert)
        down(self.n - 1, 0)

    def scalar(self, a, own):
        k = self.k
        norm_scalar(k, a, self.norm)
        a.wait_ge(self.max_ready, 1)
        a.activation(self.probs[:, :, :], self.probs[:, :, :], ACT.Exp).then_inc(self.exp_ready, 1)
        a.wait_ge(self.gates_T_ready, 1)
        a.copy(self.gates_T[:, :], k.pair(0, self.n)).then_inc(self.gates_T_copied, 1)

        def bias(two, place, odd):
            if two is None:
                return self.b1[:, 0, odd:odd + 1]
            return column(self.b1[:, 1:, odd].rearrange("p (o b) -> p o b", b=2), two, place)

        def expert(two, place, e, buf):
            for odd in range(2):
                a.wait_ge(self.h1_ready, 2 * e + odd + 1)
                if two is not None:
                    a.wait_ge(self.prod_done, 2 * e + odd - 1)
                a.activation(self.lin[:, odd, :], k.pair(0, DH), ACT.Identity, bias=bias(two, place, odd)).then_inc(self.lin_done, 1)
                if odd == 0:
                    a.wait_ge(self.xg_ready, e + 1)
                    a.activation(self.sig[:, :], self.xg[:, :], ACT.Sigmoid, scale=self.ALPHA).then_inc(self.sig_ready, 1)

        self.experts(a, expert)

    def vector(self, v, own):
        k = self.k
        norm_vector(k, v, own, self.norm)
        wide = [P, TILES, 8]
        v.wait_ge(self.consts_loaded, 16 * 7)
        v.wait_ge(self.logits_ready, 1)
        logits = k.ps[:, 4, 0:64].rearrange("p (j e) -> p j e", e=8)
        softmax_vector(k, v, own, logits, self.probs[:, :, :], self.best[:, :], self.max_ready, self.exp_ready)
        own(v.tensor_tensor(self.scores[:, :, :], self.probs[:, :, :], self.gate_b[:, :].unsqueeze(1).to_broadcast(wide), ALU.add))
        own(v.tensor_reduce(self.group[:, :, :], self.scores[:, :, :].rearrange("p j (g i) -> p j g i", i=2), AX.X, ALU.add))
        top_vector(v, own, self.group[:, :, :], self.TOP_GROUPS, self.MASKED, self.rev4[:, :], self.best[:, :],
                   self.group_hit[:, :, :], self.group_first[:, :, :], self.kept[:, :, :])
        for i in range(2):
            half = self.scores[:, :, :].rearrange("p j (g i) -> p j g i", i=2)[:, :, :, i]
            own(v.tensor_tensor(half, half, self.kept[:, :, :], ALU.mult))
        own(v.tensor_scalar(self.group[:, :, :], self.kept[:, :, :], 1.0, -self.MASKED, ALU.subtract, ALU.mult))
        for i in range(2):
            half = self.scores[:, :, :].rearrange("p j (g i) -> p j g i", i=2)[:, :, :, i]
            own(v.tensor_tensor(half, half, self.group[:, :, :], ALU.add))
        top_vector(v, own, self.scores[:, :, :], self.TOP, self.MASKED, self.rev8[:, :], self.best[:, :],
                   self.hit[:, :, :], self.first[:, :, :], self.chosen[:, :, :])
        v.memset(self.gates[:, :, 8:9], 1.0)
        v.tensor_tensor(self.gates[:, :, 0:8], self.chosen[:, :, :], self.probs[:, :, :], ALU.mult).then_inc(self.gates_ready, 1)
        v.wait_ge(self.gates_ready, 1)
        v.wait_ge(self.b2_ready, 1)
        v.tensor_copy(pairs_of(self.y[:, :, :]), k.tok_psum(4, D)).then_inc(self.y_added, 1)

        def bias(two, place, odd):
            if two is None:
                return self.b3[:, 0, odd:odd + 1]
            return column(self.b3[:, 1:, odd].rearrange("p (o b) -> p o b", b=2), two, place)

        def gate(two, place, j):
            if two is None:
                return self.gates[:, j, self.n - 1:self.n]
            return column(self.gates[:, j, 0:self.n - 1].rearrange("p (o b) -> p o b", b=2), two, place)

        def add(two, place, e):
            v.wait_ge(self.out_ready, e + 1)
            v.wait_ge(self.y_added, e + 1)
            for j in range(TILES):
                last = v.scalar_tensor_tensor(out=self.y[:, j, :], in0=k.tok_psum(4, D)[:, j // 2, j % 2, :],
                                              scalar=gate(two, place, j), in1=self.y[:, j, :], op0=ALU.mult, op1=ALU.add)
            last.then_inc(self.y_added, 1)

        def expert(two, place, e, buf):
            for odd, out in ((0, self.xg), (1, self.xl)):
                v.wait_ge(self.lin_done, 2 * e + odd + 1)
                v.wait_ge(self.h3_ready, 2 * e + odd + 1)
                v.scalar_tensor_tensor(out=out[:, :], in0=k.pair(1, DH), scalar=bias(two, place, odd), in1=self.lin[:, odd, :],
                                       op0=ALU.add, op1=ALU.mult).then_inc(self.prod_done, 1)
                v.wait_ge(self.prod_done, 2 * e + odd + 1)
                if odd == 0:
                    v.tensor_scalar(self.xg[:, :], self.xg[:, :], self.LIMIT, None, ALU.min).then_inc(self.xg_ready, 1)
                    v.wait_ge(self.xg_ready, e + 1)
            own(v.tensor_scalar(self.xl[:, :], self.xl[:, :], self.LIMIT, -self.LIMIT, ALU.min, ALU.max))
            v.wait_ge(self.sig_ready, e + 1)
            own(v.tensor_tensor(self.xg[:, :], self.xg[:, :], self.sig[:, :], ALU.mult))
            v.scalar_tensor_tensor(out=self.g[:, buf, :], in0=self.xl[:, :], scalar=1.0, in1=self.xg[:, :],
                                   op0=ALU.add, op1=ALU.mult).then_inc(self.g_ready, 1)
            v.wait_ge(self.g_ready, e + 1)
            if two is not None:
                add(two, place, e - 1)

        expert(None, 0, 0, 0)
        with own.loop(self.n // 2, 4) as two:
            expert(two, 0, 2 * two + 1, 1)
            expert(two, 1, 2 * two + 2, 0)
        add(None, 0, self.n - 1)
        v.wait_ge(self.y_added, self.n + 1)
        v.tensor_tensor(k.h[:, :, :], k.h[:, :, :], self.y[:, :, :], ALU.add).then_inc(k.h_ready, 1)

    def pool(self, g, own):
        pass



class Neurons:
    N, RANK, KEY, TOP = 128, 128, 64, 4
    LISTS = 2 * TILES
    F_AT_ONCE, R_AT_ONCE = 4, 2
    SET = 4

    def __init__(self, k, name, norm, w):
        self.k, self.norm, self.w = k, norm, w
        sb, s = (lambda x, shape, t=F32: k.sb(name + "_" + x, shape, t)), (lambda x: k.sem(name + "_" + x))
        wide = [P, self.LISTS, self.N]
        self.key_w, self.key_b, self.rev = sb("key_w", [DH, 2, P]), sb("key_b", [P, 1]), sb("rev", [P, self.N])
        self.emb, self.emb_sq = sb("emb", [P, 2, self.KEY]), sb("emb_sq", [P, 2, self.KEY])
        self.norms = sb("norms", [P, 2])
        self.embT, self.keys = sb("embT", [P, self.N]), sb("keys", [P, TOKENS])
        self.probs, self.values, self.hit, self.first, self.chosen = (sb(x, wide) for x in ("probs", "values", "hit", "first", "chosen"))
        self.best = sb("best", [P, self.LISTS])
        self.F = sb("F", [DH, 2, 2, self.F_AT_ONCE * self.RANK])
        self.R = sb("R", [P, 2, self.R_AT_ONCE * D])
        self.feat, self.featT = sb("feat", [P, TILES, self.RANK]), sb("featT", [P, TOKENS])
        self.y = sb("y", [P, TILES, D])
        self.consts_loaded = s("consts_loaded")
        self.F_loaded, self.R_loaded = [s("F_loaded0"), s("F_loaded1")], [s("R_loaded0"), s("R_loaded1")]
        self.emb_ms_ready, self.emb_std_ready, self.emb_ready = s("emb_ms_ready"), s("emb_std_ready"), s("emb_ready")
        self.embT_ready, self.embT_copied = s("embT_ready"), s("embT_copied")
        self.keys_ready, self.keys_copied = s("keys_ready"), s("keys_copied")
        self.logits_ready, self.max_ready, self.exp_ready = s("logits_ready"), s("max_ready"), s("exp_ready")
        self.F_set, self.R_set = s("F_set"), s("R_set")
        self.F_added, self.R_added = s("F_added"), s("R_added")
        self.feat_ready, self.featT_ready, self.featT_copied = s("feat_ready"), s("featT_ready"), s("featT_copied")

    def sync(self, sp):
        w = self.w
        sp.wait_ge(self.k.h_ready, self.norm)
        for dst, src in ((self.key_w[:, :, :], w["key_w"].rearrange("(c p) m -> p c m", p=DH)), (self.key_b[:, :], w["key_b"]),
                         (self.rev[:, :], w["rev"].to_broadcast([P, self.N])), (self.emb[:, :, :], w["emb"])):
            sp.dma_start(dst, src).then_inc(self.consts_loaded, 16)
        for table, buffers, loaded, done in ((w["F"], self.F, self.F_loaded, self.F_set), (w["R"], self.R, self.R_loaded, self.R_set)):
            def load(two, buf):
                src = pick_of_two(table, two, buf)
                if table is w["F"]:
                    src = src.rearrange("(c p) m -> p c m", p=DH)
                sp.dma_start(buffers[:, buf], src).then_inc(loaded[buf], 16)
            load(0, 0)
            load(0, 1)
            with sp.Fori(1, table.shape[0] // 2) as two:
                for buf in range(2):
                    sp.wait_ge(done, 4 * two + 2 * buf - 2)
                    load(two, buf)

    def tensor(self, pe, own):
        k = self.k
        norm_tensor(k, pe, self.norm)
        pe.wait_ge(self.consts_loaded, 64)
        for c in range(2):
            for t in range(2):
                last = pe.matmul(k.pair(2)[:, BANK * t:BANK * (t + 1)], self.key_w[:, c, :], k.xnF[:, c, BANK * t:BANK * (t + 1)],
                                 start=(c == 0), stop=(c == 1))
        last.then_inc(self.keys_ready, 1)
        pe.wait_ge(self.emb_ready, 1)
        pe.transpose(k.ps[:, 6, 0:P], self.emb[:, :, :].rearrange("p a b -> p (a b)"), k.ident[:, :]).then_inc(self.embT_ready, 1)
        pe.wait_ge(self.keys_copied, 1)
        pe.wait_ge(self.embT_copied, 1)
        for a in range(2):
            rows = slice(self.KEY * a, self.KEY * (a + 1))
            for j in range(TILES):
                last = pe.matmul(k.pair(a)[:, P * j:P * (j + 1)], self.keys[rows, P * j:P * (j + 1)], self.embT[rows, :],
                                 start=True, stop=True)
        last.then_inc(self.logits_ready, 1)
        pe.wait_ge(self.max_ready, 1)

        def pool_of_maps(groups, loaded, ready, added, lhs, rhs, halves, width):
            with pe.Fori(0, groups // 2) as two:
                for buf in range(2):
                    pe.wait_ge(loaded[buf], 16 * two + 16)
                    for s in range(2):
                        pe.wait_ge(added, 4 * two + 2 * buf + s + 1)
                        for b in range(self.SET):
                            j = self.SET * s + b
                            for c in range(halves):
                                last = pe.matmul(k.ps[:, j, 0:width], lhs(c)[:, P * j:P * (j + 1)], rhs(buf, c),
                                                 start=(c == 0), stop=(c == halves - 1))
                        last.then_inc(ready, 1)

        pool_of_maps(self.N // self.F_AT_ONCE, self.F_loaded, self.F_set, self.F_added,
                     lambda c: k.xnF[:, c, :], lambda buf, c: self.F[:, buf, c, :], 2, self.F_AT_ONCE * self.RANK)
        pe.wait_ge(self.feat_ready, 1)
        for j in range(TILES):
            last = pe.transpose(k.pair(0)[:, P * j:P * (j + 1)], self.feat[:, j, :], k.ident[:, :])
        last.then_inc(self.featT_ready, 1)
        pe.wait_ge(self.featT_copied, 1)
        pool_of_maps(self.N // self.R_AT_ONCE, self.R_loaded, self.R_set, self.R_added,
                     lambda c: self.featT[:, :], lambda buf, c: self.R[:, buf, :], 1, self.R_AT_ONCE * D)

    def scalar(self, a, own):
        k = self.k
        a.wait_ge(self.emb_ms_ready, 1)
        a.activation(self.norms[:, :], self.norms[:, :], ACT.Sqrt).then_inc(self.emb_std_ready, 1)
        norm_scalar(k, a, self.norm)
        a.wait_ge(self.consts_loaded, 64)
        a.wait_ge(self.keys_ready, 1)
        a.activation(self.keys[:, :], k.pair(2), ACT.Identity, bias=self.key_b[:, 0:1]).then_inc(self.keys_copied, 1)
        a.wait_ge(self.embT_ready, 1)
        a.copy(self.embT[:, :], k.ps[:, 6, 0:P]).then_inc(self.embT_copied, 1)
        a.wait_ge(self.max_ready, 1)
        a.activation(self.probs[:, :, :], self.probs[:, :, :], ACT.Exp).then_inc(self.exp_ready, 1)
        a.wait_ge(self.featT_ready, 1)
        a.copy(self.featT[:, :], k.pair(0)).then_inc(self.featT_copied, 1)

    def vector(self, v, own):
        k = self.k
        v.memset(self.feat[:, :, :], 0.0)
        v.memset(self.y[:, :, :], 0.0)
        v.sem_inc(self.F_added, 2)
        v.sem_inc(self.R_added, 2)
        v.wait_ge(self.consts_loaded, 64)
        own(v.tensor_tensor(self.emb_sq[:, :, :], self.emb[:, :, :], self.emb[:, :, :], ALU.mult))
        v.tensor_reduce(self.norms[:, :], self.emb_sq[:, :, :], AX.X, ALU.add).then_inc(self.emb_ms_ready, 1)
        v.wait_ge(self.emb_std_ready, 1)
        own(v.tensor_scalar(self.norms[:, :], self.norms[:, :], 1e-8, None, ALU.add))
        own(v.reciprocal(self.norms[:, :], self.norms[:, :]))
        v.tensor_tensor(self.emb[:, :, :], self.emb[:, :, :], self.norms[:, :].unsqueeze(2).to_broadcast([P, 2, self.KEY]),
                        ALU.mult).then_inc(self.emb_ready, 1)
        norm_vector(k, v, own, self.norm)
        wide = [P, self.LISTS, self.N]
        v.wait_ge(self.logits_ready, 1)
        logits = k.ps[:, 0:4, :].rearrange("p a b -> p (a b)").rearrange("p (l n) -> p l n", n=self.N)
        softmax_vector(k, v, own, logits, self.probs[:, :, :], self.best[:, :], self.max_ready, self.exp_ready)
        own(v.tensor_copy(self.values[:, :, :], self.probs[:, :, :]))
        top_vector(v, own, self.values[:, :, :], self.TOP, -4.0, self.rev[:, :], self.best[:, :], self.hit[:, :, :],
                   self.first[:, :, :], self.chosen[:, :, :])
        w = self.probs
        own(v.tensor_tensor(w[:, :, :], w[:, :, :], self.chosen[:, :, :], ALU.mult))
        own(v.tensor_reduce(self.best[:, :], w[:, :, :], AX.X, ALU.add))
        own(v.tensor_scalar(self.best[:, :], self.best[:, :], 1e-8, None, ALU.add))
        own(v.reciprocal(self.best[:, :], self.best[:, :]))
        own(v.tensor_tensor(w[:, :, :], w[:, :, :], self.best[:, :].unsqueeze(2).to_broadcast(wide), ALU.mult))

        def add_up(groups, ready, added, out, width, each, row):
            with own.loop(groups // 2, 4 * each) as two:
                for buf in range(2):
                    for s in range(2):
                        v.wait_ge(ready, 4 * two + 2 * buf + s + 1)
                        for q in range(each):
                            for j in range(self.SET * s, self.SET * (s + 1)):
                                weights = w[:, row + j, :].rearrange("p (o m) -> p o m", m=2 * each)
                                last = v.scalar_tensor_tensor(
                                    out=out[:, j, :], in0=k.ps[:, j, width * q:width * (q + 1)],
                                    scalar=column(weights, two, each * buf + q), in1=out[:, j, :], op0=ALU.mult, op1=ALU.add)
                            own(last)
                        v.sem_inc(added, 1)

        add_up(self.N // self.F_AT_ONCE, self.F_set, self.F_added, self.feat, self.RANK, self.F_AT_ONCE, 0)
        v.sem_inc(self.feat_ready, 1)
        add_up(self.N // self.R_AT_ONCE, self.R_set, self.R_added, self.y, D, self.R_AT_ONCE, TILES)
        v.tensor_tensor(k.h[:, :, :], k.h[:, :, :], self.y[:, :, :], ALU.add).then_inc(k.h_ready, 1)

    def pool(self, g, own):
        pass



class Tokenizer:
    SIDE, LEVELS, GROUP, EMBED = 64, (1, 2, 4), 16, 64
    PLACES = (4096, 1024, 256)
    LENGTHS = (256, 64, 16)
    WIDTHS = (3, 12, 48)

    def __init__(self, k, name, norm, w):
        self.k, self.norm, self.w = k, norm, w
        sb, s = (lambda x, shape, t=F32: k.sb(name + "_" + x, shape, t)), (lambda x: k.sem(name + "_" + x))
        G, E = self.GROUP, self.EMBED
        self.rows = [P, self.LENGTHS[1], self.LENGTHS[2]]
        self.tiles = [2, 1, 1]
        self.raw = [sb("raw%d" % q, [self.rows[q], self.tiles[q], G], I32) for q in range(3)]
        self.pos = [sb("pos%d" % q, [self.rows[q], self.tiles[q], G]) for q in range(3)]
        self.neg = [sb("neg%d" % q, [self.rows[q], self.tiles[q], G]) for q in range(3)]
        self.idx = [sb("idx%d" % q, [self.rows[q], self.tiles[q], G], U32) for q in range(3)]
        self.got = [sb("got%d" % q, [self.rows[q], self.tiles[q], G, IMAGES * self.WIDTHS[q]]) for q in range(3)]
        self.byimage = [sb("byimage%d" % q, [self.rows[q], self.tiles[q], IMAGES, G * self.WIDTHS[q]]) for q in range(3)]
        self.byimage_ready = s("byimage_ready")
        self.gotT = [sb("gotT0", [G * 3, TOKENS]), sb("gotT1", [DH, 2, IMAGES, 64]), sb("gotT2", [DH, 8, IMAGES, 16])]
        self.W = [sb("W0", [G * 3, E]), sb("W1", [DH, 2, E]), sb("W2", [DH, 8, E])]
        self.b, self.fuse, self.fuse_b = sb("b", [E, 3]), sb("fuse", [E, 3, D]), sb("fuse_b", [P, D])
        self.stretch = [None, sb("stretch1", [64, SEQ]), sb("stretch2", [16, SEQ])]
        self.short = [None, sb("short1", [64, IMAGES, E]), sb("short2", [16, IMAGES, E])]
        self.e = sb("e", [E, 3, TOKENS])
        self.consts_loaded, self.idx_loaded, self.idx_ready = s("consts_loaded"), s("idx_loaded"), s("idx_ready")
        self.gathered = [s("gathered0"), s("gathered1"), s("gathered2")]
        self.gotT_ready, self.gotT_copied = s("gotT_ready"), s("gotT_copied")
        self.short_ready, self.short_copied = s("short_ready"), s("short_copied")
        self.e_ready, self.e_copied, self.out_ready = s("e_ready"), s("e_copied"), s("out_ready")

    def sync(self, sp):
        w = self.w
        for q in range(3):
            sp.dma_start(self.raw[q][:, :, :], w["idx%d" % q].rearrange("(t p g) -> p t g", p=self.rows[q], g=self.GROUP)).then_inc(self.idx_loaded, 16)
        for dst, src in ((self.W[0][:, :], w["W0_T"]), (self.W[1][:, :, :], w["W1_T"].rearrange("(c p) m -> p c m", p=DH)),
                         (self.W[2][:, :, :], w["W2_T"].rearrange("(c p) m -> p c m", p=DH)), (self.b[:, :], w["b"]),
                         (self.stretch[1][:, :], w["stretch1"]), (self.stretch[2][:, :], w["stretch2"]),
                         (self.fuse[:, :, :], w["fuse_T"].rearrange("(c p) m -> p c m", p=self.EMBED)),
                         (self.fuse_b[:, :], w["fuse_b"].to_broadcast([P, D]))):
            sp.dma_start(dst, src).then_inc(self.consts_loaded, 16)

    def pool(self, g, own):
        for q in (2, 1, 0):
            g.wait_ge(self.idx_ready, 3 - q)
            for t in range(self.tiles[q]):
                for i in range(self.GROUP):
                    g.indirect_dma_start(out=self.got[q][:, t, i, :], out_offset=None, in_=self.w["patches%d" % q],
                                         in_offset=bass.IndirectOffsetOnAxis(ap=self.idx[q][:, t, i:i + 1], axis=0)).then_inc(self.gathered[q], 16)

    def tensor(self, pe, own):
        k, G = self.k, self.GROUP
        pe.wait_ge(self.consts_loaded, 16 * 8)
        pe.wait_ge(self.byimage_ready, 1)
        for b in range(IMAGES):
            for c in range(8):
                last = pe.transpose(k.ps[0:DH, 4, 64 * c + 16 * b:64 * c + 16 * b + 16],
                                    self.byimage[2][:, 0, b, DH * c:DH * (c + 1)], k.ident[0:16, 0:16])
        last.then_inc(self.gotT_ready, 1)
        pe.wait_ge(self.byimage_ready, 2)
        for b in range(IMAGES):
            for c in range(2):
                last = pe.transpose(k.ps[0:DH, 2, 256 * c + 64 * b:256 * c + 64 * b + 64],
                                    self.byimage[1][:, 0, b, DH * c:DH * (c + 1)], k.ident[0:64, 0:64])
        last.then_inc(self.gotT_ready, 1)
        pe.wait_ge(self.gotT_copied, 1)
        for b in range(IMAGES):
            for c in range(8):
                last = pe.matmul(k.ps[0:16, 5, 64 * b:64 * b + 64], self.gotT[2][:, c, b, :], self.W[2][:, c, :],
                                 start=(c == 0), stop=(c == 7))
        last.then_inc(self.short_ready, 1)
        pe.wait_ge(self.gotT_copied, 2)
        for b in range(IMAGES):
            for c in range(2):
                last = pe.matmul(k.ps[0:64, 3, 64 * b:64 * b + 64], self.gotT[1][:, c, b, :], self.W[1][:, c, :],
                                 start=(c == 0), stop=(c == 1))
        last.then_inc(self.short_ready, 1)
        for n, (q, pair) in enumerate(((2, 2), (1, 1))):
            pe.wait_ge(self.short_copied, n + 1)
            if q == 1:
                pe.wait_ge(self.short_copied, 2)
            for b in range(IMAGES):
                last = pe.matmul(k.pair(pair, 64)[:, SEQ * b:SEQ * (b + 1)], self.short[q][:, b, :], self.stretch[q][:, :],
                                 start=True, stop=True)
            last.then_inc(self.e_ready, 1)
        pe.wait_ge(self.byimage_ready, 4)
        for j in range(TILES):
            last = pe.transpose(k.pair(0, 48)[:, P * j:P * (j + 1)], self.byimage[0][:, j % 2, j // 2, :],
                                k.ident[:, :])
        last.then_inc(self.gotT_ready, 1)
        pe.wait_ge(self.gotT_copied, 3)
        for t in range(2):
            last = pe.matmul(k.pair(0, 64)[:, BANK * t:BANK * (t + 1)], self.W[0][:, :], self.gotT[0][:, BANK * t:BANK * (t + 1)],
                             start=True, stop=True)
        last.then_inc(self.e_ready, 1)
        pe.wait_ge(self.e_copied, 3)
        for j in range(TILES):
            for q in range(3):
                last = pe.matmul(k.tok_psum(4, D)[:, j // 2, j % 2, :], self.e[:, q, P * j:P * (j + 1)], self.fuse[:, q, :],
                                 start=(q == 0), stop=(q == 2))
        last.then_inc(self.out_ready, 1)

    def scalar(self, a, own):
        k = self.k
        a.wait_ge(self.consts_loaded, 16 * 8)
        a.wait_ge(self.gotT_ready, 1)
        a.copy(self.gotT[2][:, :, :, :].rearrange("p c b l -> p (c b l)"), k.ps[0:DH, 4, :]).then_inc(self.gotT_copied, 1)
        a.wait_ge(self.gotT_ready, 2)
        a.copy(self.gotT[1][:, :, :, :].rearrange("p c b l -> p (c b l)"), k.ps[0:DH, 2, :]).then_inc(self.gotT_copied, 1)
        a.wait_ge(self.short_ready, 1)
        a.copy(self.short[2][:, :, :].rearrange("p b f -> p (b f)"), k.ps[0:16, 5, 0:256]).then_inc(self.short_copied, 1)
        a.wait_ge(self.short_ready, 2)
        a.copy(self.short[1][:, :, :].rearrange("p b f -> p (b f)"), k.ps[0:64, 3, 0:256]).then_inc(self.short_copied, 1)
        for n, (q, pair) in enumerate(((2, 2), (1, 1))):
            a.wait_ge(self.e_ready, n + 1)
            a.activation(self.e[:, q, :], k.pair(pair, 64), ACT.Identity, bias=self.b[:, q:q + 1]).then_inc(self.e_copied, 1)
        a.wait_ge(self.gotT_ready, 3)
        a.copy(self.gotT[0][:, :], k.pair(0, 48)).then_inc(self.gotT_copied, 1)
        a.wait_ge(self.e_ready, 3)
        a.activation(self.e[:, 0, :], k.pair(0, 64), ACT.Identity, bias=self.b[:, 0:1]).then_inc(self.e_copied, 1)

    def vector(self, v, own):
        k = self.k
        v.wait_ge(self.idx_loaded, 16 * 3)
        for q in (2, 1, 0):
            raw, pos, neg, n = self.raw[q][:, :, :], self.pos[q][:, :, :], self.neg[q][:, :, :], float(self.PLACES[q])
            own(v.tensor_copy(pos, raw))
            own(v.tensor_scalar(neg, pos, 0.0, n, ALU.is_lt, ALU.mult))
            own(v.tensor_tensor(pos, pos, neg, ALU.add))
            v.tensor_scalar(self.idx[q][:, :, :], pos, 0.0, n - 1, ALU.max, ALU.min).then_inc(self.idx_ready, 1)
        for q in (2, 1, 0):
            v.wait_ge(self.gathered[q], 16 * self.tiles[q] * self.GROUP)
            for t in range(self.tiles[q]):
                v.tensor_copy(self.byimage[q][:, t, :, :].rearrange("p b (g w) -> p b g w", g=self.GROUP),
                              self.got[q][:, t, :, :].rearrange("p g (b w) -> p b g w", b=IMAGES)).then_inc(self.byimage_ready, 1)
        v.wait_ge(self.consts_loaded, 16 * 8)
        v.wait_ge(self.out_ready, 1)
        for half in range(2):
            last = v.tensor_tensor(k.h[:, half::2, :], k.tok_psum(4, D)[:, :, half, :],
                                   self.fuse_b[:, :].unsqueeze(1).to_broadcast([P, IMAGES, D]), ALU.add)
        last.then_inc(k.h_ready, 1)



def build(nc, a, out):
    with ExitStack() as ctx:
        k = Chip(nc, ctx)
        stages = []
        for n, stage in enumerate(STAGES):
            with ExitStack() as k.stage_memory:
                stages.append(stage(k, a, n))
        out_stored = k.sem("out_stored")

        def start(eng, stage):
            if stage.norm > 0:
                eng.wait_ge(k.h_ready, stage.norm)
        block = ctx.enter_context(nc.Block())

        @block.sync
        def _(sp):
            sp.dma_start(k.ident[:, :], a["ident"]).then_inc(k.ident_loaded, 16)
            for stage in stages:
                stage.sync(sp)
            sp.wait_ge(k.h_ready, len(stages))
            sp.dma_start(out.rearrange("(j p) d -> p j d", p=P), k.h[:, :, :]).then_inc(out_stored, 16)
            sp.wait_ge(out_stored, 16)

        @block.tensor
        def _(pe):
            own = Own(pe, k.tensor_own)
            pe.wait_ge(k.ident_loaded, 16)
            for stage in stages:
                start(pe, stage)
                stage.tensor(pe, own)

        @block.scalar
        def _(act):
            own = Own(act, k.scalar_own)
            for stage in stages:
                start(act, stage)
                stage.scalar(act, own)

        @block.vector
        def _(dve):
            own = Own(dve, k.vector_own)
            for stage in stages:
                start(dve, stage)
                stage.vector(dve, own)

        @block.gpsimd
        def _(pool):
            own = Own(pool, k.pool_own)
            for stage in stages:
                start(pool, stage)
                stage.pool(pool, own)


def mamba_0(k, a, n):
    return Mamba(k, "l0", n, {x: a["m0_" + x] for x in ("in_T", "x_T", "dt_T", "out_T", "params", "norm_w", "final_w")}
                    | {"sel": a["row_sel"]}, 16, 48)


def mamba_1(k, a, n):
    return Mamba(k, "l1", n, {x: a["m1_" + x] for x in ("in_T", "x_T", "dt_T", "out_T", "params")} | {"sel": a["row_sel"]},
                 1, 12)


def experts_0(k, a, n):
    return Experts(k, "l0f", n, {x: a["e0_" + x] for x in ("router_T", "W1", "b1", "W2", "b2")} | {"rev": a["rev16"]},
                   16, 2, ACT.Gelu, True)


def experts_1(k, a, n):
    return GatedExperts(k, "l1f", n, {x: a["e1_" + x] for x in ("router_T", "gate_b", "W1", "W3", "W2", "b1", "b3", "b2")}
                        | {"rev8": a["rev8"], "rev4": a["rev4"]})


def attention_2(k, a, n):
    return ErfAttention(k, "l2a", n, {x: a["a2_" + x] for x in ("qkv_T", "proj_T", "cos", "sin", "mask")})


def attention_3(k, a, n):
    return Retention(k, "l3a", n, {x: a["a3_" + x] for x in ("qkv", "qk_b", "v_b", "mask")})


def neurons_2(k, a, n):
    return Neurons(k, "l2f", n, {x: a["n2_" + x] for x in ("key_w", "key_b", "emb", "F", "R")} | {"rev": a["rev128"]})


def tokenizer(k, a, n):
    return Tokenizer(k, "tok", n, {x: a["t_" + x] for x in ("patches0", "patches1", "patches2", "idx0", "idx1", "idx2", "W0_T", "W1_T",
                                                            "W2_T", "b", "stretch1", "stretch2", "fuse_T", "fuse_b")})


def experts_3(k, a, n):
    stage = Experts(k, "l3f", n, {x: a["e3_" + x] for x in ("router_T", "router_b", "W1", "b1", "W2", "b2")} | {"rev": a["rev8"]},
                    8, 1, ACT.Gelu_apprx_tanh, False)
    stage.tail = Resolvent(k, "bk", {x: a["r3_" + x] for x in ("rows", "scalars", "turned", "signs")}, stage.y)
    return stage


STAGES = (tokenizer, mamba_0, experts_0, mamba_1, experts_1, attention_2, neurons_2, attention_3, experts_3)



def stretch(short, long):
    at = np.clip((np.arange(long, dtype=np.float32) + np.float32(0.5)) * np.float32(short / long) - np.float32(0.5), 0, short - 1)
    low = np.floor(at).astype(np.int32)
    high = np.minimum(low + 1, short - 1)
    w = (at - low).astype(np.float32)
    m = np.zeros((short, long), np.float32)
    m[low, np.arange(long)] += 1 - w
    m[high, np.arange(long)] += w
    return m


def laid_out(x):
    a = {}
    c = np.ascontiguousarray
    a["ident"] = np.eye(P, dtype=np.float32)
    a["row_sel"] = c(np.tile(np.eye(BC, dtype=np.float32), (3, 1)))

    def mamba(p, in_w, conv_w, conv_b, dt_low, b_c, dt_w, dt_b, a_log, d, out_w):
        a[p + "in_T"] = c(in_w.transpose(0, 2, 1))
        a[p + "x_T"] = c(np.concatenate([b_c, b_c, b_c, dt_low], axis=1).transpose(0, 2, 1))
        a[p + "dt_T"] = c(dt_w.transpose(0, 2, 1))
        a[p + "out_T"] = c(out_w.transpose(0, 2, 1))
        a[p + "params"] = c(np.concatenate([conv_w[:, :, 0, :], conv_b[:, :, None], dt_b[:, :, None], d[:, :, None], a_log], axis=2))

    rank = 48
    mamba("m0_", x["L0_attn_in_proj_w"], x["L0_attn_conv_w"], x["L0_attn_conv_b"], x["L0_attn_x_proj_w"][:, :rank],
          x["L0_attn_x_proj_w"][:, rank:], x["L0_attn_dt_proj_w"], x["L0_attn_dt_proj_b"], x["L0_attn_A_log"],
          x["L0_attn_D"], x["L0_attn_out_proj_w"])
    a["m0_norm_w"] = c(x["L0_attn_norm_w"].reshape(-1, 2, DH).transpose(2, 0, 1))
    a["m0_final_w"] = x["L0_attn_final_norm_w"].reshape(1, D)
    mamba("m1_", *[x["L1_attn_" + y][None] for y in ("in_proj_w", "conv_w", "conv_b", "x_dt_w")],
          np.concatenate([x["L1_attn_x_b_w"], x["L1_attn_x_c_w"]], axis=0)[None],
          *[x["L1_attn_" + y][None] for y in ("dt_w", "dt_b", "A_log", "D_param", "out_proj_w")])

    for e in (4, 8, 16, 128):
        a["rev%d" % e] = np.arange(e, 0, -1, dtype=np.float32).reshape(1, e)
    for p, q, router in (("e0_", "L0_ffn_", x["L0_ffn_Wr"].T), ("e3_", "L3_ffn_", x["L3_ffn_Wg"])):
        a[p + "router_T"] = c(router)
        a[p + "W1"], a[p + "W2"], a[p + "b2"] = x[q + "W1"], x[q + "W2"], x[q + "b2"]
        a[p + "b1"] = c(x[q + "b1"].reshape(-1, 2 * CHUNKS, P).transpose(2, 0, 1))

    parted = lambda w: np.concatenate([w[..., ::2], w[..., 1::2]], axis=-1)
    q = "L1_ffn_"
    with_shared = lambda y, z: np.concatenate([x[q + y], x[q + z][None]], axis=0)
    a["e1_router_T"], a["e1_gate_b"] = c(x[q + "gate_w"].T), x[q + "gate_b"].reshape(1, -1)
    a["e1_W1"], a["e1_W3"] = c(parted(with_shared("W1", "Ws1"))), c(parted(with_shared("W3", "Ws3")))
    a["e1_W2"], a["e1_b2"] = with_shared("W2", "Ws2"), with_shared("B2", "Bs2")
    for y, z, t in (("b1", "B1", "Bs1"), ("b3", "B3", "Bs3")):
        a["e1_" + y] = c(with_shared(z, t).reshape(-1, DH, 2).transpose(1, 0, 2))

    a["a2_qkv_T"] = c(np.concatenate([x["L2_attn_W" + y].T for y in "qkv"], axis=1))
    a["a2_proj_T"] = c(x["L2_attn_Wproj"].T)
    half = 8
    freq = np.float32(1.0) / np.float32(10000.0) ** (np.arange(half, dtype=np.float32) / np.float32(half))
    angle = (np.arange(SEQ, dtype=np.float32)[:, None] * freq[None, :]).astype(np.float32)
    by_tile = lambda t: c(t.reshape(2, P, -1).transpose(1, 0, 2).astype(np.float32))
    a["a2_cos"], a["a2_sin"] = by_tile(np.cos(angle)), by_tile(np.sin(angle))
    query, key = np.arange(SEQ)[None, :], np.arange(SEQ)[:, None]
    spans = lambda t: c(np.concatenate([t[0:P], t[P:, P:]], axis=1).astype(np.float32))
    a["a2_mask"] = spans(query >= key)
    decay = np.float32(0.99) ** np.maximum(query - key, 0).astype(np.float32)
    a["a3_mask"] = spans(np.where(query >= key, decay, np.float32(0)))
    a["a3_qkv"] = x["L3_attn_W_qkv"]
    a["a3_qk_b"] = c(x["L3_attn_b_qkv"][:2 * D].reshape(4, DH).T)
    a["a3_v_b"] = x["L3_attn_b_qkv"][2 * D:].reshape(1, D)

    q = "L2_ffn_"
    a["n2_key_w"] = c(np.concatenate([x[q + "W_fk"], x[q + "W_rk"]], axis=1))
    a["n2_key_b"] = np.concatenate([x[q + "b_fk"], x[q + "b_rk"]]).reshape(-1, 1)
    a["n2_emb"] = c(np.stack([x[q + "emb_fk"], x[q + "emb_rk"]], axis=1))
    beside = lambda t, m: c(t.reshape(-1, m, *t.shape[1:]).transpose(0, 2, 1, 3).reshape(t.shape[0] // m, t.shape[1], -1))
    a["n2_F"], a["n2_R"] = beside(x[q + "f_know"], Neurons.F_AT_ONCE), beside(x[q + "r_know"], Neurons.R_AT_ONCE)

    images = x["x"]
    for q, p in enumerate(Tokenizer.LEVELS):
        side = Tokenizer.SIDE // p
        a["t_patches%d" % q] = c(images.reshape(IMAGES, 3, side, p, side, p).transpose(2, 4, 0, 3, 5, 1).reshape(side * side, -1))
        a["t_idx%d" % q] = x["L0_tok_idx%d" % q]
        a["t_W%d_T" % q] = c(x["L0_tok_W%d" % q].T)
        if q:
            a["t_stretch%d" % q] = stretch(Tokenizer.LENGTHS[q], SEQ)
    a["t_b"] = c(np.stack([x["L0_tok_b%d" % q] for q in range(3)], axis=1))
    a["t_fuse_T"], a["t_fuse_b"] = c(x["L0_tok_Wf"].T), x["L0_tok_bf"].reshape(1, D)
    q = "L3_ffn_"
    a["e3_router_b"] = x[q + "bg"].reshape(1, -1)
    a["r3_rows"] = np.concatenate([x[q + "Wv"], x[q + "Wm"], x[q + "Wo"].reshape(-1), x[q + "bo"]]).reshape(1, -1)
    a["r3_scalars"] = np.stack([x[q + "bv"], x[q + "bm"], x[q + "bk_scale"]]).reshape(1, 3)
    a["r3_turned"] = c(np.eye(P, dtype=np.float32)[:, ::-1])
    a["r3_signs"] = c(np.tile(np.where(np.arange(SEQ) % 2, -1.0, 1.0).astype(np.float32), (Resolvent.ROWS, 1)))
    return a


def kernel(**inputs):
    import concourse.bacc as bacc
    from concourse.bass_utils import run_bass_kernel_spmd

    x = {name: np.asarray(value) for name, value in inputs.items()}
    arrays = laid_out(x)
    nc = bacc.Bacc("TRN2", target_bir_lowering=False, num_devices=1)
    feeds, aps = {}, {}
    for name, value in arrays.items():
        value = np.ascontiguousarray(value)
        feeds["in_" + name] = value
        aps[name] = nc.dram_tensor("in_" + name, value.shape, mybir.dt.from_np(value.dtype), kind="ExternalInput").ap()
    out = nc.dram_tensor("out_0_dram", (TOKENS, D), F32, kind="ExternalOutput").ap()
    build(nc, aps, out)
    r = run_bass_kernel_spmd(nc, [feeds], core_ids=[0])
    return r.results[0]["out_0_dram"].reshape(IMAGES, SEQ, D)
```

```python
from contextlib import ExitStack, contextmanager

import numpy as np
import concourse.bass as bass
from concourse import mybir

F32 = mybir.dt.float32
BF16 = mybir.dt.bfloat16
I32 = mybir.dt.int32
U32 = mybir.dt.uint32
ALU = mybir.AluOpType
ACT = mybir.ActivationFunctionType
AX = mybir.AxisListType

IMAGES, SEQ, D = 4, 256, 192
TOKENS = IMAGES * SEQ
P = 128
TILES = TOKENS // P
DH = D // 2
HALF, HALF_TILES = TOKENS // 2, TILES // 2
BANK = 512
EPS = 1e-5


class Own:

    def __init__(self, eng, done):
        self.eng, self.done = eng, done
        self.count, self.base = 0, 0

    def __call__(self, instruction):
        instruction.then_inc(self.done, 1)
        self.count += 1
        self.eng.wait_ge(self.done, self.base + self.count)

    def mark(self, instruction):
        instruction.then_inc(self.done, 1)
        self.count += 1

    def wait_behind(self, steps):
        self.eng.wait_ge(self.done, self.base + self.count - steps)

    @contextmanager
    def loop(self, rounds, steps):
        start = self.count
        if rounds == 1:
            yield 0
        else:
            with self.eng.Fori(0, rounds) as i:
                self.base = i * steps
                yield i
        assert self.count == start + steps, (self.count - start, steps)
        self.base, self.count = 0, start + rounds * steps


def one(ap):
    return ap.rearrange("o a b -> (o a) b")


def pick(ap, i):
    return one(ap[i:i + 1]) if isinstance(i, int) else one(ap[bass.ds(i, 1)])


def pick_of_two(ap, two, b):
    ap = ap[0:ap.shape[0] // 2 * 2]
    return pick(ap.rearrange("(o b) x y -> b o x y", b=2)[b], two)


class Chip:

    def __init__(self, nc, ctx):
        self.nc, self.ctx = nc, ctx
        self.stage_memory = None
        self.sems = {}
        self.routers = self.gatings = 0
        self.mamba_layers = self.mamba_stacks = self.mamba_consts = 0
        self.experts = self.expert_stages = self.expert_consts = 0
        self.h = self.sb("h", [P, TILES, D], F32)
        self.xn = self.sb("xn", [P, TILES, D], F32)
        self.xnF = self.sb("xnF", [DH, 2, TOKENS], F32)
        self.ident = self.sb("ident", [P, P], F32)
        self.stats = self.sb("stats", [P, TILES, 6], F32)
        self.mean_var = self.sb("mean_var", [P, TILES, 2], F32)
        self.var = self.sb("var", [P, TILES], F32)
        self.std = self.sb("std", [P, TILES], F32)
        self.rstd = self.sb("rstd", [P, TILES], F32)
        self.ps = ctx.enter_context(nc.psum_tensor("ps", [P, 8, BANK], F32))
        self.ident_loaded = self.sem("ident_loaded")
        self.h_ready = self.sem("h_ready")
        self.ln_var_ready = self.sem("ln_var_ready")
        self.ln_std_ready = self.sem("ln_std_ready")
        self.xn_ready = self.sem("xn_ready")
        self.xnT_ready = self.sem("xnT_ready")
        self.xnF_ready = self.sem("xnF_ready")
        self.vector_own = self.sem("vector_own")
        self.scalar_own = self.sem("scalar_own")
        self.pool_own = self.sem("pool_own")
        self.tensor_own = self.sem("tensor_own")

    def sb(self, name, shape, dtype):
        return (self.stage_memory or self.ctx).enter_context(self.nc.sbuf_tensor(name, shape, dtype))

    def sem(self, name):
        if name not in self.sems:
            self.sems[name] = self.ctx.enter_context(self.nc.semaphore(name))
        return self.sems[name]

    def pair(self, n, rows=P):
        return self.ps[0:rows, 2 * n:2 * n + 2, :].rearrange("p a b -> p (a b)")

    def tok_psum(self, bank, width):
        return self.ps[:, bank:bank + 4, 0:2 * width].rearrange("p a (c d) -> p a c d", c=2)


def pairs_of(ap):
    return ap.rearrange("p (a c) n -> p a c n", c=2)



def norm_vector(k, v, own, n):
    v.wait_ge(k.h_ready, n)
    for j in range(TILES):
        last = v.bn_stats(k.stats[:, j, :], k.h[:, j, :])
    own(last)
    for j in range(TILES):
        last = v.bn_aggr(k.mean_var[:, j, :], k.stats[:, j, :])
    own(last)
    v.tensor_scalar(k.var[:, :], k.mean_var[:, :, 1], EPS, None, ALU.add).then_inc(k.ln_var_ready, 1)
    v.wait_ge(k.ln_std_ready, n)
    own(v.reciprocal(k.rstd[:, :], k.std[:, :]))
    for j in range(TILES):
        last = v.tensor_scalar(k.xn[:, j, :], k.h[:, j, :], k.mean_var[:, j, 0:1], k.rstd[:, j:j + 1],
                               ALU.subtract, ALU.mult)
    last.then_inc(k.xn_ready, 1)
    v.wait_ge(k.xnT_ready, n)
    v.tensor_copy(k.xnF[:, 1, :], k.pair(1, DH)).then_inc(k.xnF_ready, 1)


def norm_scalar(k, a, n):
    a.wait_ge(k.ln_var_ready, n)
    a.activation(k.std[:, :], k.var[:, :], ACT.Sqrt).then_inc(k.ln_std_ready, 1)
    a.wait_ge(k.xnT_ready, n)
    a.copy(k.xnF[:, 0, :], k.pair(0, DH)).then_inc(k.xnF_ready, 1)


def norm_tensor(k, pe, n):
    pe.wait_ge(k.xn_ready, n)
    transpose_tokens(k, pe, k.xn).then_inc(k.xnT_ready, 1)
    pe.wait_ge(k.xnF_ready, 2 * n)


def transpose_tokens(k, pe, x):
    for half in range(2):
        for j in range(TILES):
            last = pe.transpose(k.pair(half, DH)[:, P * j:P * (j + 1)], x[:, j, DH * half:DH * (half + 1)],
                                k.ident[:, :])
    return last



INNER, STATES, TAPS = 2 * D, 16, 4
BLOCKS = INNER // P
UNITS = BLOCKS * STATES
RING = 6
ROWS = 4
BC = 2 * STATES
BC_AT = 64
PARAMS = TAPS + 3 + STATES
HALF_IMAGES = IMAGES // 2
HC_RING, POOL_HC_RING = 5, 2
ROW_BANK, SIDE_BANK = 3, 5


def at_least(eng, semaphore, count):
    if not isinstance(count, int) or count > 0:
        eng.wait_ge(semaphore, count)


def by_pool(unit):
    return unit % 6 == 2


LATER = 5


def weighed_by_pool(unit):
    return (unit + 3) // 6


def weighed_by_vector(unit):
    return unit - weighed_by_pool(unit)


POOL_UNITS, VECTOR_UNITS = weighed_by_pool(UNITS), weighed_by_vector(UNITS)


class Mamba:
    PLANS = {"tensor": ((1, 4, 4, 4), (11, 13, 14, 14, 18, 18, 18, 19, 22, 22, 22, 24, 26, 27, 28, 29, 32, 34, 34, 42, 45)),
             "scalar": ((), (13, 16, 20, 23, 25, 28, 31, 33, 39, 40, 40, 43, 43, 44, 47, 47)),
             "vector": ((1, 1, 1, 1, 2, 2, 9), (11, 13, 19, 19, 21, 22, 23, 23, 25, 25, 25, 34, 35, 37, 42, 42, 42, 42, 42, 44, 44, 44, 45, 47, 47)),
             "pool": ((), (48, 48, 48))}

    def __init__(self, k, name, norm, w, layers, rank):
        self.k, self.norm, self.w, self.layers, self.rank = k, norm, w, layers, rank
        self.normed = "norm_w" in w
        sb = k.sb
        self.w_in = sb(name + "_w_in", [DH, 2, 2 * INNER], F32)
        self.w_x = sb(name + "_w_x", [P, BLOCKS, BC_AT + BC], F32)
        self.w_dt = sb(name + "_w_dt", [rank, INNER], F32)
        self.w_out = sb(name + "_w_out", [P, BLOCKS, D], F32)
        self.params = sb(name + "_params", [P, layers, BLOCKS, PARAMS], F32)
        self.par = sb(name + "_par", [P, 2, BLOCKS, PARAMS], F32)
        self.nw = sb(name + "_nw", [DH, 2, 2], F32)
        self.norms = sb(name + "_norms", [DH, layers, 2], F32)
        self.final_w = sb(name + "_final_w", [P, D], F32)
        self.x = sb(name + "_x", [P, TILES, D], F32)
        self.sel0 = sb(name + "_sel0", [3 * BC, BC], F32)
        self.sel = sb(name + "_sel", [3 * BC, BC, P], BF16)
        self.u = sb(name + "_u", [P, BLOCKS, TOKENS], F32)
        self.z = sb(name + "_z", [P, BLOCKS, TOKENS], F32)
        self.dt = sb(name + "_dt", [P, BLOCKS, TOKENS], F32)
        self.dtu = sb(name + "_dtu", [P, BLOCKS, TOKENS], F32)
        self.dtr = sb(name + "_dtr", [rank, HALF], F32)
        self.bc3 = sb(name + "_bc3", [3 * BC, 2, HALF], BF16)
        self.rest = sb(name + "_rest", [3 * BC, HALF], F32)
        self.part = sb(name + "_part", [3 * BC, HALF], BF16)
        self.conv = sb(name + "_conv", [P, BLOCKS, HALF], F32)
        self.one, self.eps = sb(name + "_one", [P, 1], F32), sb(name + "_eps", [P, 1], F32)
        self.e = sb(name + "_e", [P, BLOCKS, HALF], F32)
        self.w1 = sb(name + "_w1", [P, BLOCKS, HALF], F32)
        self.log = self.conv
        self.b_row = sb(name + "_b_row", [P, ROWS, HALF], F32)
        self.c_row = sb(name + "_c_row", [P, ROWS, HALF], F32)
        self.da = sb(name + "_da", [P, RING, HALF_IMAGES, SEQ], F32)
        self.bu = sb(name + "_bu", [P, RING, HALF], F32)
        self.hs = sb(name + "_hs", [P, RING, HALF], F32)
        self.pool_hc = sb(name + "_pool_hc", [P, POOL_HC_RING, HALF], F32)
        self.hc = sb(name + "_hc", [P, HC_RING, HALF], F32)
        self.own_vector = 2 * 18
        s = lambda x: k.sem("mamba_" + x)
        self.layer0, self.stack, self.consts = k.mamba_layers, k.mamba_stacks, k.mamba_consts
        self.consts += 64 if self.normed else 32
        k.mamba_layers, k.mamba_stacks, k.mamba_consts = self.layer0 + layers, self.stack + 1, self.consts
        self.consts_loaded = s("consts_loaded")
        self.w_in_loaded, self.w_x_loaded = s("w_in_loaded"), s("w_x_loaded")
        self.w_dt_loaded, self.w_out_loaded = s("w_dt_loaded"), s("w_out_loaded")
        self.sel_ready, self.neg_a_ready, self.par_ready = s("sel_ready"), s("neg_a_ready"), s("par_ready")
        self.x_ready, self.rms_ready = s("x_ready"), s("rms_ready")
        self.xs_ready, self.xsT_ready = s("xs_ready"), s("xsT_ready")
        self.xsF_ready = s("xsF_ready")
        self.in_ready = s("in_ready")
        self.tap_ready, self.conv_ready = s("tap_ready"), s("conv_ready")
        self.u_ready, self.z_ready = s("u_ready"), s("z_ready")
        self.xp_ready, self.dtr_copied = s("xp_ready"), s("dtr_copied")
        self.bc_read, self.bc3_ready = s("bc_read"), s("bc3_ready")
        self.dtp_ready = s("dtp_ready")
        self.e_ready, self.w1_ready, self.ln_ready = s("e_ready"), s("w1_ready"), s("ln_ready")
        self.dt_ready = s("dt_ready")
        self.row_ready, self.row_copied = s("row_ready"), s("row_copied")
        self.da_ready, self.bu_ready = s("da_ready"), s("bu_ready")
        self.scan_done, self.hc_ready, self.hc_used = s("scan_done"), s("hc_ready"), s("hc_used")
        self.pool_hc_ready, self.pool_hc_used = s("pool_hc_ready"), s("pool_hc_used")
        self.y_read, self.y_ready, self.out_ready = s("y_read"), s("y_ready"), s("out_ready")


    def steps(self, own, own_steps, engine, units, enter, leave):
        leave_plan, enter_plan = self.PLANS[engine]
        last = self.layers - 1

        def leave_and_enter(layer, half):
            yield from leave(layer, half)
            yield from enter(layer + 1, half)

        for _ in enter(0, 0):
            pass
        units(0, 0, Side(enter(0, 1), enter_plan))
        if last:
            with own.loop(last, own_steps) as i:
                units(i, 1, Side(leave_and_enter(i, 0), leave_plan + enter_plan))
                units(i + 1, 0, Side(leave_and_enter(i, 1), leave_plan + enter_plan))
        units(last, 1, Side(leave(last, 0), leave_plan))
        for _ in leave(last, 1):
            pass

    def step(self, layer, half):
        return 2 * (self.layer0 + layer) + half

    def tokens(self, half):
        return slice(HALF * half, HALF * (half + 1))

    def tiles(self, half):
        return slice(HALF_TILES * half, HALF_TILES * (half + 1))

    def of_layer(self, table, layer):
        row = table[:, layer:layer + 1] if isinstance(layer, int) else table[:, bass.ds(layer, 1)]
        return row.rearrange("p o b c -> p (o b) c") if len(table.shape) == 4 else row.rearrange("p o c -> p (o c)")

    def side_bank(self, b, rows=slice(0, P)):
        return self.k.ps[rows, SIDE_BANK + b, :]


    def sync(self, sp):
        w, n = self.w, self.layers
        sp.wait_ge(self.k.h_ready, self.norm)
        sp.dma_start(self.params[:, 0:n], w["params"].rearrange("n (b p) c -> p n b c", p=P)).then_inc(self.consts_loaded, 16)
        sp.dma_start(self.sel0[:, :], w["sel"]).then_inc(self.consts_loaded, 16)
        if self.normed:
            sp.dma_start(self.norms[:, :, :], w["norm_w"]).then_inc(self.consts_loaded, 16)
            sp.dma_start(self.final_w[:, :], w["final_w"].to_broadcast([P, D])).then_inc(self.consts_loaded, 16)

        def load(i):
            s = self.step(i, 0)
            at_least(sp, self.in_ready, 6 * s)
            sp.dma_start(self.w_in[:, :, :], pick(w["in_T"], i).rearrange("(c p) m -> p c m", p=DH)).then_inc(self.w_in_loaded, 16)
            at_least(sp, self.xp_ready, s)
            sp.dma_start(self.w_x[:, :, :], pick(w["x_T"], i).rearrange("(b p) m -> p b m", p=P)).then_inc(self.w_x_loaded, 16)
            at_least(sp, self.dtp_ready, 3 * s)
            sp.dma_start(self.w_dt[:, :], pick(w["dt_T"], i)).then_inc(self.w_dt_loaded, 16)
            at_least(sp, self.out_ready, s)
            sp.dma_start(self.w_out[:, :, :], pick(w["out_T"], i).rearrange("(b p) m -> p b m", p=P)).then_inc(self.w_out_loaded, 16)

        load(0)
        if n > 1:
            with sp.Fori(1, n) as i:
                load(i)


    def tensor(self, pe, own):
        k = self.k
        norm_tensor(k, pe, self.norm)
        pe.wait_ge(self.sel_ready, self.stack + 1)

        def loaded(semaphore, layer):
            pe.wait_ge(semaphore, 16 * (self.layer0 + layer) + 16)

        def row(s, half, r):
            at_least(pe, self.row_copied, BC * s + r - 1)
            pe.matmul(k.ps[:, ROW_BANK + r % 2, :], self.sel[:, (r % 2) * STATES + r // 2, :], self.bc3[:, half, :],
                      start=True, stop=True).then_inc(self.row_ready, 1)

        def enter(layer, half):
            s, t = self.step(layer, half), self.tokens(half)
            at_least(pe, self.e_ready, BLOCKS * s)
            if self.normed:
                pe.wait_ge(self.xs_ready, s + 1)
                for c, b in enumerate((2, 1)):
                    for j in range(HALF_TILES):
                        last = pe.transpose(self.side_bank(b, slice(0, DH))[:, P * j:P * (j + 1)],
                                            k.xn[:, HALF_TILES * half + j, DH * c:DH * (c + 1)], k.ident[:, :])
                last.then_inc(self.xsT_ready, 1)
            yield
            if self.normed:
                pe.wait_ge(self.xsF_ready, 2 * s + 2)
            loaded(self.w_in_loaded, layer)
            for m in range(2 * BLOCKS):
                if m >= BLOCKS:
                    pe.wait_ge(self.conv_ready, BLOCKS * s + m - BLOCKS + 1)
                for c in range(2):
                    last = pe.matmul(self.side_bank(m % BLOCKS), self.w_in[:, c, P * m:P * (m + 1)], k.xnF[:, c, t],
                                     start=(c == 0), stop=(c == 1))
                    if c == 0:
                        yield
                last.then_inc(self.in_ready, 1)
                yield
            loaded(self.w_x_loaded, layer)
            pe.wait_ge(self.u_ready, BLOCKS * s + BLOCKS)
            pe.wait_ge(self.z_ready, BLOCKS * s + 1)
            for b in range(BLOCKS):
                if b:
                    yield
                last = pe.matmul(self.side_bank(0, slice(0, BC_AT + BC)), self.w_x[:, b, :], self.u[:, b, t],
                                 start=(b == 0), stop=(b == BLOCKS - 1))
            last.then_inc(self.xp_ready, 1)
            yield
            loaded(self.w_dt_loaded, layer)
            pe.wait_ge(self.dtr_copied, s + 1)
            pe.wait_ge(self.z_ready, BLOCKS * s + BLOCKS)
            for b in range(BLOCKS):
                if b:
                    yield
                if b == BLOCKS - 1:
                    pe.wait_ge(self.bc_read, s + 1)
                pe.matmul(self.side_bank((b + 1) % BLOCKS), self.w_dt[:, P * b:P * (b + 1)], self.dtr[:, :],
                          start=True, stop=True).then_inc(self.dtp_ready, 1)
            yield
            pe.wait_ge(self.bc3_ready, s + 1)
            row(s, half, 0)
            row(s, half, 1)
            yield
            row(s, half, 2)
            row(s, half, 3)

        def add_pools(s, unit):
            at = weighed_by_pool(unit)
            pe.wait_ge(self.pool_hc_ready, POOL_UNITS * s + at + 1)
            pe.matmul(k.ps[:, unit % BLOCKS, :], k.ident[:, :], self.pool_hc[:, at % POOL_HC_RING, :], start=False,
                      stop=(at == POOL_UNITS - 1)).then_inc(self.pool_hc_used, 1)

        def units(layer, half, side):
            s = self.step(layer, half)
            row(s, half, 4)
            row(s, half, 5)
            for n in range(STATES):
                if n + 3 < STATES:
                    row(s, half, 2 * n + 6)
                    row(s, half, 2 * n + 7)
                for b in range(BLOCKS):
                    unit = BLOCKS * n + b
                    side.before(unit)
                    if unit == 0:
                        at_least(pe, self.y_read, s)
                    if not by_pool(unit):
                        at = weighed_by_vector(unit)
                        pe.wait_ge(self.hc_ready, VECTOR_UNITS * s + at + 1)
                        pe.matmul(k.ps[:, b, :], k.ident[:, :], self.hc[:, at % HC_RING, :],
                                  start=(unit in (0, 1, 5)), stop=(unit in (45, 46))).then_inc(self.hc_used, 1)
                    if by_pool(unit - LATER) and unit >= LATER:
                        add_pools(s, unit - LATER)
            add_pools(s, UNITS - 4)
            side.finish()

        def leave(layer, half):
            s = self.step(layer, half)
            loaded(self.w_out_loaded, layer)
            entered = min(s + 2, 2 * (self.layer0 + self.layers)) if isinstance(s, int) else s + 2
            pe.wait_ge(self.e_ready, BLOCKS * entered)
            pe.wait_ge(self.y_ready, s + 1)
            for j in range(HALF_TILES):
                at = HALF * half + P * j
                for b in range(BLOCKS):
                    last = pe.matmul(self.side_bank(j // 2)[:, D * (j % 2):D * (j % 2 + 1)], self.u[:, b, at:at + P],
                                     self.w_out[:, b, :], start=(b == 0), stop=(b == BLOCKS - 1))
                if j == HALF_TILES - 1:
                    last.then_inc(self.out_ready, 1)
                yield

        self.steps(own, 0, "tensor", units, enter, leave)


    def root_mean_square(self, a, own, half):
        for j in range(HALF_TILES * half, HALF_TILES * (half + 1)):
            at = j % HALF_TILES
            last = a.activation(self.w1[:, :, :].rearrange("p b t -> p (b t)")[:, D * at:D * (at + 1)], self.x[:, j, :], ACT.Square, accum_out=self.k.var[:, j:j + 1])
        own(last)
        return a.activation(self.k.std[:, self.tiles(half)], self.k.var[:, self.tiles(half)], ACT.Sqrt, bias=self.eps[:, :],
                            scale=1.0 / D)

    def scalar(self, a, own):
        k = self.k
        norm_scalar(k, a, self.norm)
        a.wait_ge(self.consts_loaded, self.consts)
        for i in range(self.layers):
            last = a.activation(self.params[:, i, :, TAPS + 3:PARAMS], self.params[:, i, :, TAPS + 3:PARAMS], ACT.Exp)
        own(last)
        for i in range(self.layers):
            last = a.mul(self.params[:, i, :, TAPS + 3:PARAMS], self.params[:, i, :, TAPS + 3:PARAMS], -1.0)
        last.then_inc(self.neg_a_ready, 1)

        def row_copy(s, r):
            n = r // 2
            a.wait_ge(self.row_ready, BC * s + r + 1)
            before = BLOCKS * (n + 1 - ROWS)
            if r % 2:
                at_least(a, self.hc_ready, VECTOR_UNITS * s + weighed_by_vector(before))
                at_least(a, self.pool_hc_ready, POOL_UNITS * s + weighed_by_pool(before))
            else:
                at_least(a, self.bu_ready, UNITS * s + before)
            a.copy((self.c_row if r % 2 else self.b_row)[:, n % ROWS, :], k.ps[:, ROW_BANK + r % 2, :]).then_inc(self.row_copied, 1)

        def enter(layer, half):
            s, t = self.step(layer, half), self.tokens(half)
            a.wait_ge(self.par_ready, s + 1)
            if self.normed:
                a.wait_ge(self.x_ready, s + 1)
                self.root_mean_square(a, own, half).then_inc(self.rms_ready, 1)
                yield
                a.wait_ge(self.xsT_ready, s + 1)
                for c, b in enumerate((2, 1)):
                    a.mul(k.xnF[:, c, t], self.side_bank(b, slice(0, DH)), self.nw[:, half, c:c + 1]).then_inc(self.xsF_ready, 1)
                yield
            else:
                yield
                yield
            at_least(a, self.u_ready, BLOCKS * s)
            for b in range(BLOCKS):
                a.wait_ge(self.in_ready, 2 * BLOCKS * s + b + 1)
                a.activation(self.conv[:, b, :], self.side_bank(b), ACT.Identity, bias=self.par[:, half, b, TAPS:TAPS + 1],
                             scale=self.par[:, half, b, TAPS - 1:TAPS]).then_inc(self.tap_ready, 1)
                yield
            for b in range(BLOCKS):
                a.wait_ge(self.conv_ready, BLOCKS * s + b + 1)
                a.activation(self.u[:, b, t], self.conv[:, b, :], ACT.Silu).then_inc(self.u_ready, 1)
            yield
            for b in range(BLOCKS):
                a.wait_ge(self.in_ready, 2 * BLOCKS * s + BLOCKS + b + 1)
                a.activation(self.z[:, b, t], self.side_bank(b), ACT.Silu).then_inc(self.z_ready, 1)
            yield
            a.wait_ge(self.xp_ready, s + 1)
            a.copy(self.dtr[:, :], self.side_bank(0, slice(0, self.rank))).then_inc(self.dtr_copied, 1)
            yield
            at_least(a, self.da_ready, UNITS * (s - 1))
            at_least(a, self.dt_ready, BLOCKS * s)
            for b in range(BLOCKS):
                a.wait_ge(self.dtp_ready, BLOCKS * s + b + 1)
                a.activation(self.dt[:, b, t], self.side_bank((b + 1) % BLOCKS), ACT.Identity,
                             bias=self.par[:, half, b, TAPS + 1:TAPS + 2])
                own.mark(a.activation(self.e[:, b, :], self.side_bank((b + 1) % BLOCKS), ACT.Abs,
                                      bias=self.par[:, half, b, TAPS + 1:TAPS + 2]))
                yield
                own.wait_behind(0)
                a.activation(self.e[:, b, :], self.e[:, b, :], ACT.Exp, scale=-1.0).then_inc(self.e_ready, 1)
            yield
            for b in range(BLOCKS):
                a.wait_ge(self.e_ready, BLOCKS * s + b + 1)
                a.activation(self.w1[:, b, :], self.e[:, b, :], ACT.Identity, bias=self.one[:, :]).then_inc(self.w1_ready, 1)
            yield
            a.wait_ge(self.u_ready, BLOCKS * s + BLOCKS)
            for b in range(BLOCKS):
                a.wait_ge(self.w1_ready, BLOCKS * s + b + 1)
                a.activation(self.log[:, b, :], self.w1[:, b, :], ACT.Ln).then_inc(self.ln_ready, 1)
            yield
            row_copy(s, 0)
            row_copy(s, 1)
            yield
            row_copy(s, 2)
            row_copy(s, 3)

        def units(layer, half, side):
            s = self.step(layer, half)
            a.wait_ge(self.dt_ready, BLOCKS * s + BLOCKS)
            for n in range(STATES):
                for b in range(BLOCKS):
                    unit = BLOCKS * n + b
                    side.before(unit)
                    at_least(a, self.scan_done, UNITS * s + unit - RING + 1)
                    a.activation(self.da[:, unit % RING, :, 1:SEQ],
                                 self.dt[:, b, self.tokens(half)].rearrange("p (m t) -> p m t", t=SEQ)[:, :, 1:SEQ], ACT.Exp,
                                 scale=self.par[:, half, b, TAPS + 3 + n:TAPS + 4 + n]).then_inc(self.da_ready, 1)
                if n + 2 < STATES:
                    row_copy(s, 2 * n + 4)
                    row_copy(s, 2 * n + 5)
            side.finish()

        def leave(layer, half):
            return iter(())

        self.steps(own, 2 * 4, "scalar", units, enter, leave)
        if self.normed:
            a.wait_ge(self.x_ready, 2 * (self.layer0 + self.layers) + 2)
            for half in range(2):
                self.root_mean_square(a, own, half).then_inc(self.rms_ready, 1)


    def vector(self, v, own):
        k = self.k
        norm_vector(k, v, own, self.norm)
        v.wait_ge(self.consts_loaded, self.consts)
        v.wait_ge(self.neg_a_ready, self.stack + 1)
        v.tensor_copy(self.sel[:, :, :], self.sel0[:, :].unsqueeze(2).to_broadcast([3 * BC, BC, P])).then_inc(self.sel_ready, 1)
        v.memset(self.one[:, :], 1.0)
        v.memset(self.eps[:, :], EPS)
        own(v.memset(self.da[:, :, :, 0], 0.0))
        if self.normed:
            own(v.tensor_copy(self.x[:, :, :], k.xn[:, :, :]))
            v.sem_inc(self.x_ready, 2)

        def scaled(tiles, n):
            own(v.reciprocal(k.rstd[:, tiles], k.std[:, tiles]))
            return v.tensor_tensor(k.xn[:, tiles, :], self.x[:, tiles, :],
                                   k.rstd[:, tiles].unsqueeze(2).to_broadcast([P, n, D]), ALU.mult)

        def enter(layer, half):
            s, t, tiles = self.step(layer, half), self.tokens(half), self.tiles(half)
            if self.normed:
                v.tensor_copy(self.nw[:, half], self.of_layer(self.norms, layer))
            own(v.tensor_copy(self.par[:, half], self.of_layer(self.params, layer)))
            v.sem_inc(self.par_ready, 1)
            yield
            if self.normed:
                v.wait_ge(self.rms_ready, s + 1)
                scaled(tiles, HALF_TILES).then_inc(self.xs_ready, 1)
                yield
            else:
                yield
            for b in range(BLOCKS):
                v.wait_ge(self.tap_ready, BLOCKS * s + b + 1)
                x = self.side_bank(b).rearrange("p (m t) -> p m t", t=SEQ)
                acc = self.conv[:, b, :].rearrange("p (m t) -> p m t", t=SEQ)
                for back in range(1, TAPS):
                    if back > 1:
                        yield
                        own.wait_behind(0)
                    ins = v.scalar_tensor_tensor(out=acc[:, :, back:SEQ], in0=x[:, :, 0:SEQ - back],
                                                 scalar=self.par[:, half, b, TAPS - 1 - back:TAPS - back],
                                                 in1=acc[:, :, back:SEQ], op0=ALU.mult, op1=ALU.add)
                    if back < TAPS - 1:
                        own.mark(ins)
                ins.then_inc(self.conv_ready, 1)
                yield
            v.wait_ge(self.xp_ready, s + 1)
            v.wait_ge(self.dtr_copied, s + 1)
            here = slice(BC_AT, BC_AT + BC)
            products, rest, part = self.side_bank(0, here), self.rest[here, :], self.part[here, :]
            first = self.bc3[here, half, :]
            own.mark(v.tensor_copy(first, products))
            yield
            own.wait_behind(0)
            v.tensor_tensor(rest, products, first, ALU.subtract).then_inc(self.bc_read, 1)
            yield
            v.wait_ge(self.bc_read, s + 1)
            v.tensor_copy(self.bc3[BC:2 * BC, half, :], rest)
            own.mark(v.tensor_copy(part, rest))
            yield
            own.wait_behind(0)
            own.mark(v.tensor_tensor(rest, rest, part, ALU.subtract))
            yield
            own.wait_behind(0)
            v.tensor_copy(self.bc3[0:BC, half, :], rest).then_inc(self.bc3_ready, 1)
            yield
            for b in range(BLOCKS):
                v.wait_ge(self.w1_ready, BLOCKS * s + b + 1)
                own.mark(v.scalar_tensor_tensor(out=self.e[:, b, :], in0=self.w1[:, b, :], scalar=1.0, in1=self.e[:, b, :],
                                                op0=ALU.subtract, op1=ALU.subtract))
                yield
            v.wait_ge(self.bc3_ready, s + 1)
            for b in range(BLOCKS):
                own.wait_behind(0)
                v.wait_ge(self.ln_ready, BLOCKS * s + b + 1)
                own.mark(v.scalar_tensor_tensor(out=self.dt[:, b, t], in0=self.dt[:, b, t], scalar=0.0,
                                                in1=self.log[:, b, :], op0=ALU.max, op1=ALU.add))
                yield
                own.wait_behind(0)
                v.tensor_tensor(self.dt[:, b, t], self.dt[:, b, t], self.e[:, b, :], ALU.subtract).then_inc(self.dt_ready, 1)
                if b < BLOCKS - 1:
                    yield

        def units(layer, half, side):
            s = self.step(layer, half)

            def weigh(unit):
                n, at = unit // BLOCKS, weighed_by_vector(unit)
                v.wait_ge(self.scan_done, UNITS * s + unit + 1)
                v.wait_ge(self.row_copied, BC * s + 2 * n + 2)
                at_least(v, self.hc_used, VECTOR_UNITS * s + at - HC_RING + 1)
                v.tensor_tensor(self.hc[:, at % HC_RING, :], self.hs[:, unit % RING, :], self.c_row[:, n % ROWS, :],
                                ALU.mult).then_inc(self.hc_ready, 1)

            for unit in range(UNITS):
                side.before(unit)
                v.wait_ge(self.da_ready, UNITS * s + unit + 1)
                v.wait_ge(self.bu_ready, UNITS * s + unit + 1)
                if by_pool(unit - RING):
                    at_least(v, self.pool_hc_ready, POOL_UNITS * s + weighed_by_pool(unit - RING) + 1)
                else:
                    at_least(v, self.hc_ready, VECTOR_UNITS * s + weighed_by_vector(unit - RING) + 1)
                v.tensor_tensor_scan(self.hs[:, unit % RING, :],
                                     self.da[:, unit % RING, :, :].rearrange("p m t -> p (m t)"),
                                     self.bu[:, unit % RING, :], 0.0, ALU.mult, ALU.add).then_inc(self.scan_done, 1)
                if unit >= 1 and not by_pool(unit - 1):
                    weigh(unit - 1)
            weigh(UNITS - 1)
            side.finish()

        def leave(layer, half):
            s, t, tiles = self.step(layer, half), self.tokens(half), self.tiles(half)
            v.wait_ge(self.hc_used, VECTOR_UNITS * s + VECTOR_UNITS)
            v.wait_ge(self.pool_hc_used, POOL_UNITS * s + POOL_UNITS)
            for b in range(BLOCKS):
                if b:
                    yield
                last = v.scalar_tensor_tensor(out=self.u[:, b, t], in0=self.u[:, b, t],
                                              scalar=self.par[:, half, b, TAPS + 2:TAPS + 3], in1=k.ps[:, b, :],
                                              op0=ALU.mult, op1=ALU.add)
            last.then_inc(self.y_read, 1)
            yield
            v.wait_ge(self.y_read, s + 1)
            for b in range(BLOCKS):
                if b:
                    yield
                last = v.tensor_tensor(self.u[:, b, t], self.u[:, b, t], self.z[:, b, t], ALU.mult)
            last.then_inc(self.y_ready, 1)
            yield
            v.wait_ge(self.out_ready, s + 1)
            x = self.x if self.normed else k.h
            halves = pairs_of(x[:, tiles, :])
            own(v.tensor_tensor(halves, halves, k.ps[:, SIDE_BANK:SIDE_BANK + 2, 0:2 * D].rearrange("p a (c d) -> p a c d", c=2), ALU.add))
            if self.normed:
                v.sem_inc(self.x_ready, 1)
            yield

        self.steps(own, self.own_vector, "vector", units, enter, leave)
        if self.normed:
            v.wait_ge(self.rms_ready, 2 * (self.layer0 + self.layers) + 2)
            own(scaled(slice(0, TILES), TILES))
            own(v.tensor_tensor(k.xn[:, :, :], k.xn[:, :, :], self.final_w[:, :].unsqueeze(1).to_broadcast([P, TILES, D]), ALU.mult))
            v.tensor_tensor(k.h[:, :, :], k.h[:, :, :], k.xn[:, :, :], ALU.add).then_inc(k.h_ready, 1)
        else:
            v.sem_inc(k.h_ready, 1)


    def pool(self, g, own):
        def weigh(s, unit):
            n, at = unit // BLOCKS, weighed_by_pool(unit)
            g.wait_ge(self.scan_done, UNITS * s + unit + 1)
            g.wait_ge(self.row_copied, BC * s + 2 * n + 2)
            at_least(g, self.pool_hc_used, POOL_UNITS * s + at - POOL_HC_RING + 1)
            g.tensor_tensor(self.pool_hc[:, at % POOL_HC_RING, :], self.hs[:, unit % RING, :], self.c_row[:, n % ROWS, :],
                            ALU.mult).then_inc(self.pool_hc_ready, 1)

        def enter(layer, half):
            s, t = self.step(layer, half), self.tokens(half)
            at_least(g, self.bu_ready, UNITS * (s - 1))
            for b in range(BLOCKS):
                g.wait_ge(self.dt_ready, BLOCKS * s + b + 1)
                last = g.tensor_tensor(self.dtu[:, b, t], self.dt[:, b, t], self.u[:, b, t], ALU.mult)
                if b < BLOCKS - 1:
                    yield
            own(last)

        def units(layer, half, side):
            s = self.step(layer, half)
            for n in range(STATES):
                g.wait_ge(self.row_copied, BC * s + 2 * n + 1)
                for b in range(BLOCKS):
                    unit = BLOCKS * n + b
                    side.before(unit)
                    if unit >= RING and by_pool(unit - RING):
                        weigh(s, unit - RING)
                    at_least(g, self.scan_done, UNITS * s + unit - RING + 1)
                    g.tensor_tensor(self.bu[:, unit % RING, :], self.dtu[:, b, self.tokens(half)], self.b_row[:, n % ROWS, :],
                                    ALU.mult).then_inc(self.bu_ready, 1)
            weigh(s, UNITS - 4)
            side.finish()

        def leave(layer, half):
            return iter(())

        self.steps(own, 2, "pool", units, enter, leave)


class Side:

    def __init__(self, parts, plan):
        self.parts, self.plan = parts, list(plan)

    def before(self, unit):
        while self.plan and self.plan[0] <= unit:
            self.plan.pop(0)
            next(self.parts, None)

    def finish(self):
        for _ in self.parts:
            pass



def softmax_vector(k, v, own, logits, exp_in, sums, max_ready, exp_ready, n=1):
    wide = list(exp_in.shape)
    own(v.tensor_reduce(sums, logits, AX.X, ALU.max))
    v.tensor_tensor(exp_in, logits, sums.unsqueeze(2).to_broadcast(wide), ALU.subtract).then_inc(max_ready, 1)
    v.wait_ge(exp_ready, n)
    own(v.tensor_reduce(sums, exp_in, AX.X, ALU.add))
    own(v.reciprocal(sums, sums))
    own(v.tensor_tensor(exp_in, exp_in, sums.unsqueeze(2).to_broadcast(wide), ALU.mult))


def top_vector(v, own, values, rounds, low, rev, best, hit, first, chosen):
    wide = list(values.shape)
    for r in range(rounds):
        own(v.tensor_reduce(best, values, AX.X, ALU.max))
        own(v.tensor_tensor(hit, values, best.unsqueeze(2).to_broadcast(wide), ALU.is_equal))
        own(v.tensor_tensor(hit, hit, rev.unsqueeze(1).to_broadcast(wide), ALU.mult))
        own(v.tensor_reduce(best, hit, AX.X, ALU.max))
        first_hit = chosen if r == 0 else first
        own(v.tensor_tensor(first_hit, hit, best.unsqueeze(2).to_broadcast(wide), ALU.is_equal))
        if r + 1 < rounds:
            own(v.scalar_tensor_tensor(out=values, in0=first_hit, scalar=low, in1=values, op0=ALU.mult, op1=ALU.add))
        if r > 0:
            own(v.tensor_tensor(chosen, chosen, first, ALU.add))



HIDDEN = 4 * D
CHUNKS = HIDDEN // P


class Experts:
    def __init__(self, k, name, norm, w, experts, top, gelu, keep_xn, tail=None):
        self.k, self.norm, self.w, self.n, self.top = k, norm, w, experts, top
        self.gelu, self.keep_xn, self.tail = gelu, keep_xn, tail
        sb = k.sb
        self.wr = sb(name + "_wr", [DH, 2, experts], F32)
        self.rb = sb(name + "_rb", [P, experts], F32)
        self.rev = sb(name + "_rev", [P, experts], F32)
        self.b1 = sb(name + "_b1", [P, experts // 2, 2 * CHUNKS], F32)
        self.b2 = sb(name + "_b2", [experts, D], F32)
        self.w1 = sb(name + "_w1", [DH, 2, 2, HIDDEN], F32)
        self.w2 = sb(name + "_w2", [P, 2, CHUNKS, D], F32)
        self.probs = sb(name + "_probs", [P, TILES, experts], F32)
        self.values = sb(name + "_values", [P, TILES, experts], F32)
        self.hit = sb(name + "_hit", [P, TILES, experts], F32)
        self.first = sb(name + "_first", [P, TILES, experts], F32)
        self.gates = sb(name + "_gates", [P, TILES, experts], F32)
        self.gates_T = sb(name + "_gates_T", [experts, TOKENS], F32)
        self.best = sb(name + "_best", [P, TILES], F32)
        self.hid = sb(name + "_hid", [P, 3, TOKENS], F32)
        self.y = sb(name + "_y", [P, TILES, D], F32)
        s = lambda x: k.sem("experts_" + x)
        self.before, self.turn, self.consts = k.experts, k.expert_stages, k.expert_consts
        self.consts += 16 * (5 if "router_b" in w else 4)
        k.experts, k.expert_stages, k.expert_consts = self.before + experts, self.turn + 1, self.consts
        self.consts_loaded = s("consts_loaded")
        self.w1_loaded = [s("w1_loaded0"), s("w1_loaded1")]
        self.w2_loaded = [s("w2_loaded0"), s("w2_loaded1")]
        self.route, k.routers = k.routers, k.routers + 1
        self.gating, k.gatings = k.gatings, k.gatings + 1
        self.logits_ready, self.max_ready, self.exp_ready = k.sem("router_logits_ready"), k.sem("router_max_ready"), k.sem("router_exp_ready")
        self.gates_ready, self.gates_T_ready, self.gates_T_copied = k.sem("router_gates_ready"), k.sem("router_gates_T_ready"), k.sem("router_gates_T_copied")
        self.b2_ready = s("b2_ready")
        self.hid_ready, self.gelu_done = s("hid_ready"), s("gelu_done")
        self.expert_ready = s("expert_ready")
        self.y_added = s("y_added")

    def each(self, eng, body):
        with eng.Fori(0, self.n // 2) as two:
            body(two, 0)
            body(two, 1)

    def sync(self, sp):
        w = self.w
        sp.wait_ge(self.k.h_ready, self.norm)
        loads = [(self.wr[:, :, :], w["router_T"].rearrange("(c p) e -> p c e", p=DH)),
                 (self.rev[:, :], w["rev"].to_broadcast([P, self.n])),
                 (self.b1[:, :, :], w["b1"]), (self.b2[:, :], w["b2"])]
        if "router_b" in w:
            loads.append((self.rb[:, :], w["router_b"].to_broadcast([P, self.n])))
        for dst, src in loads:
            sp.dma_start(dst, src).then_inc(self.consts_loaded, 16)

        def load(two, buf):
            sp.dma_start(self.w1[:, buf, :, :], pick_of_two(w["W1"], two, buf).rearrange("(c p) m -> p c m", p=DH)).then_inc(self.w1_loaded[buf], 16)
            sp.dma_start(self.w2[:, buf, :, :], pick_of_two(w["W2"], two, buf).rearrange("(c p) m -> p c m", p=P)).then_inc(self.w2_loaded[buf], 16)

        load(0, 0)
        load(0, 1)
        if self.tail:
            self.tail.sync(sp)
        with sp.Fori(1, self.n // 2) as two:
            for buf in range(2):
                sp.wait_ge(self.expert_ready, self.before + 2 * two + buf - 1)
                load(two, buf)

    def tensor(self, pe, own):
        k = self.k
        norm_tensor(k, pe, self.norm)
        pe.wait_ge(self.consts_loaded, self.consts)
        logits = k.ps[:, 4, 0:TILES * self.n].rearrange("p (j e) -> p j e", e=self.n)
        for j in range(TILES):
            for c in range(2):
                last = pe.matmul(logits[:, j, :], k.xnF[:, c, P * j:P * (j + 1)], self.wr[:, c, :],
                                 start=(c == 0), stop=(c == 1))
        last.then_inc(self.logits_ready, 1)
        pe.wait_ge(self.max_ready, self.route + 1)

        def expert(two, buf):
            e = self.before + 2 * two + buf

            def down(m):
                pe.wait_ge(self.gelu_done, 6 * e + m + 1)
                if m == 0:
                    pe.wait_ge(self.w2_loaded[buf], 8 * self.before + 16 * two + 16)
                    pe.wait_ge(self.y_added, self.turn + e + 1)
                for j in range(TILES):
                    last = pe.matmul(k.tok_psum(4, D)[:, j // 2, j % 2, :], self.hid[:, m % 3, P * j:P * (j + 1)],
                                     self.w2[:, buf, m, :], start=(m == 0 and j % 2 == 0), stop=(m == CHUNKS - 1),
                                     skip_group_check=True)
                return last

            pe.wait_ge(self.w1_loaded[buf], 8 * self.before + 16 * two + 16)
            for m in range(CHUNKS):
                if m >= 2:
                    pe.wait_ge(self.gelu_done, 6 * e + m - 1)
                for c in range(2):
                    for t in range(2):
                        last = pe.matmul(k.pair(m % 2)[:, BANK * t:BANK * (t + 1)], self.w1[:, buf, c, P * m:P * (m + 1)],
                                         k.xnF[:, c, BANK * t:BANK * (t + 1)], start=(c == 0), stop=(c == 1))
                last.then_inc(self.hid_ready, 1)
                if m >= 1:
                    down(m - 1)
            down(CHUNKS - 1).then_inc(self.expert_ready, 1)

        self.each(pe, expert)
        pe.wait_ge(self.gates_ready, self.gating + 1)
        for j in range(TILES):
            last = pe.transpose(k.pair(0, self.n)[:, P * j:P * (j + 1)], self.gates[:, j, :], k.ident[:, :])
        last.then_inc(self.gates_T_ready, 1)
        pe.wait_ge(self.gates_T_copied, self.gating + 1)
        pe.wait_ge(self.y_added, self.before + self.n + self.turn + 1)
        for j in range(TILES):
            last = pe.matmul(k.tok_psum(4, D)[:, j // 2, j % 2, :], self.gates_T[:, P * j:P * (j + 1)], self.b2[:, :],
                             start=True, stop=True)
        last.then_inc(self.b2_ready, 1)
        if self.tail:
            self.tail.tensor(pe, own)

    def scalar(self, a, own):
        k = self.k
        norm_scalar(k, a, self.norm)
        a.wait_ge(self.max_ready, self.route + 1)
        a.activation(self.probs[:, :, :], self.probs[:, :, :], ACT.Exp).then_inc(self.exp_ready, 1)

        def expert(two, buf):
            e = self.before + 2 * two + buf
            for m in range(CHUNKS):
                a.wait_ge(self.hid_ready, 6 * e + m + 1)
                a.activation(self.hid[:, m % 3, :], k.pair(m % 2), self.gelu,
                             bias=column(self.b1, two, CHUNKS * buf + m)).then_inc(self.gelu_done, 1)

        if self.tail:
            self.tail.scalar_scores(a)
        self.each(a, expert)
        a.wait_ge(self.gates_T_ready, self.gating + 1)
        a.copy(self.gates_T[:, :], k.pair(0, self.n)).then_inc(self.gates_T_copied, 1)

    def vector(self, v, own):
        k = self.k
        norm_vector(k, v, own, self.norm)
        y = self.y[:, :, :]
        (v.tensor_copy(y, k.xn[:, :, :]) if self.keep_xn else v.memset(y, 0.0)).then_inc(self.y_added, 1)
        v.wait_ge(self.logits_ready, self.route + 1)
        logits = k.ps[:, 4, 0:TILES * self.n].rearrange("p (j e) -> p j e", e=self.n)
        if "router_b" in self.w:
            v.wait_ge(self.consts_loaded, self.consts)
            own(v.tensor_tensor(self.values[:, :, :], logits, self.rb[:, :].unsqueeze(1).to_broadcast([P, TILES, self.n]), ALU.add))
            logits = self.values[:, :, :]
        softmax_vector(k, v, own, logits, self.probs[:, :, :], self.best[:, :], self.max_ready, self.exp_ready, self.route + 1)
        own(v.tensor_copy(self.values[:, :, :], self.probs[:, :, :]))
        top_vector(v, own, self.values[:, :, :], self.top, -4.0, self.rev[:, :], self.best[:, :], self.hit[:, :, :],
                   self.first[:, :, :], self.gates[:, :, :])
        v.tensor_tensor(self.gates[:, :, :], self.gates[:, :, :], self.probs[:, :, :], ALU.mult).then_inc(self.gates_ready, 1)
        v.wait_ge(self.gates_ready, self.gating + 1)
        if self.tail:
            self.tail.vector_scores(v, own)

        def expert(two, buf):
            e = self.before + 2 * two + buf
            v.wait_ge(self.expert_ready, e + 1)
            v.wait_ge(self.y_added, self.turn + e + 1)
            for j in range(TILES):
                last = v.scalar_tensor_tensor(out=self.y[:, j, :], in0=k.tok_psum(4, D)[:, j // 2, j % 2, :],
                                              scalar=column(self.gates[:, j, :].rearrange("p (e b) -> p e b", b=2), two, buf), in1=self.y[:, j, :],
                                              op0=ALU.mult, op1=ALU.add)
            last.then_inc(self.y_added, 1)

        self.each(v, expert)
        v.wait_ge(self.y_added, self.before + self.n + self.turn + 1)
        v.wait_ge(self.b2_ready, self.turn + 1)
        own(v.tensor_tensor(pairs_of(y), pairs_of(y), k.tok_psum(4, D), ALU.add))
        if self.tail:
            self.tail.vector(v, own)
        else:
            v.tensor_tensor(k.h[:, :, :], k.h[:, :, :], self.y[:, :, :], ALU.add).then_inc(k.h_ready, 1)

    def pool(self, g, own):
        if self.tail:
            self.tail.pool(g, own)


def column(t, i, j):
    s = [slice(x, x + 1) if isinstance(x, int) else bass.ds(x, 1) for x in (i, j)]
    return t[:, s[0], s[1]].rearrange("p a b -> p (a b)")



class GatedExperts:
    ROUTED, GROUPS, TOP_GROUPS, TOP, WIDTH = 8, 4, 2, 2, 96
    ALPHA, LIMIT = 1.702, 7.0
    MASKED = -1e30

    def __init__(self, k, name, norm, w):
        self.k, self.norm, self.w = k, norm, w
        n = self.n = self.ROUTED + 1
        sb, s = (lambda x, shape, t=F32: k.sb(name + "_" + x, shape, t)), (lambda x: k.sem(name + "_" + x))
        self.wr = sb("wr", [DH, 2, self.ROUTED])
        self.gate_b = sb("gate_b", [P, self.ROUTED])
        self.rev8, self.rev4 = sb("rev8", [P, 8]), sb("rev4", [P, 4])
        self.b1, self.b3 = sb("b1", [DH, n, 2]), sb("b3", [DH, n, 2])
        self.b2 = sb("b2", [n, D])
        self.w1, self.w3 = sb("w1", [DH, 2, 2, D]), sb("w3", [DH, 2, 2, D])
        self.w2 = sb("w2", [DH, 2, D])
        self.probs, self.scores = sb("probs", [P, TILES, 8]), sb("scores", [P, TILES, 8])
        self.hit, self.first, self.chosen = sb("hit", [P, TILES, 8]), sb("first", [P, TILES, 8]), sb("chosen", [P, TILES, 8])
        self.group, self.group_first = sb("group", [P, TILES, 4]), sb("group_first", [P, TILES, 4])
        self.group_hit, self.kept = sb("group_hit", [P, TILES, 4]), sb("kept", [P, TILES, 4])
        self.gates = sb("gates", [P, TILES, n])
        self.gates_T = sb("gates_T", [n, TOKENS])
        self.best = sb("best", [P, TILES])
        self.lin = sb("lin", [DH, 2, TOKENS])
        self.xg, self.xl = sb("xg", [DH, TOKENS]), sb("xl", [DH, TOKENS])
        self.sig = sb("sig", [DH, TOKENS])
        self.g = sb("g", [DH, 2, TOKENS])
        self.y = sb("y", [P, TILES, D])
        self.consts_loaded = s("consts_loaded")
        self.weights_loaded = [s("weights_loaded0"), s("weights_loaded1")]
        self.route, k.routers = k.routers, k.routers + 1
        self.gating, k.gatings = k.gatings, k.gatings + 1
        self.logits_ready, self.max_ready, self.exp_ready = k.sem("router_logits_ready"), k.sem("router_max_ready"), k.sem("router_exp_ready")
        self.gates_ready, self.gates_T_ready, self.gates_T_copied = k.sem("router_gates_ready"), k.sem("router_gates_T_ready"), k.sem("router_gates_T_copied")
        self.b2_ready = s("b2_ready")
        self.h1_ready, self.h3_ready = s("h1_ready"), s("h3_ready")
        self.lin_done, self.prod_done = s("lin_done"), s("prod_done")
        self.xg_ready, self.sig_ready, self.g_ready = s("xg_ready"), s("sig_ready"), s("g_ready")
        self.out_ready, self.y_added = s("out_ready"), s("y_added")

    def sync(self, sp):
        k, w = self.k, self.w
        sp.wait_ge(k.h_ready, self.norm)
        loads = [(self.wr[:, :, :], w["router_T"].rearrange("(c p) e -> p c e", p=DH)),
                 (self.gate_b[:, :], w["gate_b"].to_broadcast([P, 8])), (self.rev8[:, :], w["rev8"].to_broadcast([P, 8])),
                 (self.rev4[:, :], w["rev4"].to_broadcast([P, 4])), (self.b1[:, :, :], w["b1"]), (self.b3[:, :, :], w["b3"]),
                 (self.b2[:, :], w["b2"])]
        for dst, src in loads:
            sp.dma_start(dst, src).then_inc(self.consts_loaded, 16)

        def load(row, buf):
            for dst, src in ((self.w1[:, buf], row("W1").rearrange("(c p) m -> p c m", p=DH)),
                             (self.w3[:, buf], row("W3").rearrange("(c p) m -> p c m", p=DH)), (self.w2[:, buf], row("W2"))):
                sp.dma_start(dst, src).then_inc(self.weights_loaded[buf], 16)

        load(lambda x: pick(w[x], 0), 0)
        load(lambda x: pick(w[x], 1), 1)
        with sp.Fori(0, self.n // 2 - 1) as two:
            sp.wait_ge(self.out_ready, 2 * two + 1)
            load(lambda x: pick_of_two(w[x][1:], two, 1), 0)
            sp.wait_ge(self.out_ready, 2 * two + 2)
            load(lambda x: pick_of_two(w[x][3:], two, 0), 1)
        sp.wait_ge(self.out_ready, self.n - 2)
        load(lambda x: pick(w[x], self.n - 1), 0)

    def experts(self, eng, body):
        body(None, 0, 0, 0)
        with eng.Fori(0, self.n // 2) as two:
            body(two, 0, 2 * two + 1, 1)
            body(two, 1, 2 * two + 2, 0)

    def tensor(self, pe, own):
        k = self.k
        norm_tensor(k, pe, self.norm)
        pe.wait_ge(self.consts_loaded, 16 * 7)
        for j in range(TILES):
            for c in range(2):
                last = pe.matmul(k.ps[:, 4, 8 * j:8 * j + 8], k.xnF[:, c, P * j:P * (j + 1)], self.wr[:, c, :],
                                 start=(c == 0), stop=(c == 1))
        last.then_inc(self.logits_ready, 1)
        pe.wait_ge(self.max_ready, self.route + 1)

        def up(w, buf, odd, pair):
            for c in range(2):
                for t in range(2):
                    last = pe.matmul(k.pair(pair, DH)[:, BANK * t:BANK * (t + 1)], w[:, buf, c, DH * odd:DH * (odd + 1)],
                                     k.xnF[:, c, BANK * t:BANK * (t + 1)], start=(c == 0), stop=(c == 1))
            return last

        def down(e, buf):
            pe.wait_ge(self.g_ready, e + 1)
            pe.wait_ge(self.y_added, e + 1)
            for j in range(TILES):
                last = pe.matmul(k.tok_psum(4, D)[:, j // 2, j % 2, :], self.g[:, buf, P * j:P * (j + 1)],
                                 self.w2[:, buf, :], start=True, stop=True)
            last.then_inc(self.out_ready, 1)

        def expert(two, place, e, buf):
            loads = 48 if two is None else 48 * two + (48 if place == 0 else 96)
            pe.wait_ge(self.weights_loaded[buf], loads)
            if two is not None:
                pe.wait_ge(self.lin_done, 2 * e)
            up(self.w1, buf, 0, 0).then_inc(self.h1_ready, 1)
            if two is not None:
                pe.wait_ge(self.prod_done, 2 * e)
            up(self.w3, buf, 0, 1).then_inc(self.h3_ready, 1)
            pe.wait_ge(self.lin_done, 2 * e + 1)
            up(self.w1, buf, 1, 0).then_inc(self.h1_ready, 1)
            if two is not None:
                down(e - 1, 1 - buf)
            pe.wait_ge(self.prod_done, 2 * e + 1)
            up(self.w3, buf, 1, 1).then_inc(self.h3_ready, 1)

        self.experts(pe, expert)
        down(self.n - 1, 0)
        pe.wait_ge(self.prod_done, 2 * self.n)
        pe.wait_ge(self.gates_ready, self.gating + 1)
        for j in range(TILES):
            last = pe.transpose(k.pair(0, self.n)[:, P * j:P * (j + 1)], self.gates[:, j, :], k.ident[:, :])
        last.then_inc(self.gates_T_ready, 1)
        pe.wait_ge(self.gates_T_copied, self.gating + 1)
        pe.wait_ge(self.y_added, self.n + 1)
        for j in range(TILES):
            last = pe.matmul(k.tok_psum(4, D)[:, j // 2, j % 2, :], self.gates_T[:, P * j:P * (j + 1)], self.b2[:, :],
                             start=True, stop=True)
        last.then_inc(self.b2_ready, 1)

    def scalar(self, a, own):
        k = self.k
        norm_scalar(k, a, self.norm)
        a.wait_ge(self.max_ready, self.route + 1)
        a.activation(self.probs[:, :, :], self.probs[:, :, :], ACT.Exp).then_inc(self.exp_ready, 1)

        def bias(two, place, odd):
            if two is None:
                return self.b1[:, 0, odd:odd + 1]
            return column(self.b1[:, 1:, odd].rearrange("p (o b) -> p o b", b=2), two, place)

        def expert(two, place, e, buf):
            for odd in range(2):
                a.wait_ge(self.h1_ready, 2 * e + odd + 1)
                if two is not None:
                    a.wait_ge(self.prod_done, 2 * e + odd - 1)
                a.activation(self.lin[:, odd, :], k.pair(0, DH), ACT.Identity, bias=bias(two, place, odd)).then_inc(self.lin_done, 1)
                if odd == 0:
                    a.wait_ge(self.xg_ready, e + 1)
                    a.activation(self.sig[:, :], self.xg[:, :], ACT.Sigmoid, scale=self.ALPHA).then_inc(self.sig_ready, 1)

        self.experts(a, expert)
        a.wait_ge(self.gates_T_ready, self.gating + 1)
        a.copy(self.gates_T[:, :], k.pair(0, self.n)).then_inc(self.gates_T_copied, 1)

    def vector(self, v, own):
        k = self.k
        norm_vector(k, v, own, self.norm)
        wide = [P, TILES, 8]
        v.wait_ge(self.consts_loaded, 16 * 7)
        v.memset(self.y[:, :, :], 0.0).then_inc(self.y_added, 1)
        v.wait_ge(self.logits_ready, self.route + 1)
        logits = k.ps[:, 4, 0:64].rearrange("p (j e) -> p j e", e=8)
        softmax_vector(k, v, own, logits, self.probs[:, :, :], self.best[:, :], self.max_ready, self.exp_ready, self.route + 1)
        own(v.tensor_tensor(self.scores[:, :, :], self.probs[:, :, :], self.gate_b[:, :].unsqueeze(1).to_broadcast(wide), ALU.add))
        own(v.tensor_reduce(self.group[:, :, :], self.scores[:, :, :].rearrange("p j (g i) -> p j g i", i=2), AX.X, ALU.add))
        top_vector(v, own, self.group[:, :, :], self.TOP_GROUPS, self.MASKED, self.rev4[:, :], self.best[:, :],
                   self.group_hit[:, :, :], self.group_first[:, :, :], self.kept[:, :, :])
        for i in range(2):
            half = self.scores[:, :, :].rearrange("p j (g i) -> p j g i", i=2)[:, :, :, i]
            own(v.tensor_tensor(half, half, self.kept[:, :, :], ALU.mult))
        own(v.tensor_scalar(self.group[:, :, :], self.kept[:, :, :], 1.0, -self.MASKED, ALU.subtract, ALU.mult))
        for i in range(2):
            half = self.scores[:, :, :].rearrange("p j (g i) -> p j g i", i=2)[:, :, :, i]
            own(v.tensor_tensor(half, half, self.group[:, :, :], ALU.add))
        top_vector(v, own, self.scores[:, :, :], self.TOP, self.MASKED, self.rev8[:, :], self.best[:, :],
                   self.hit[:, :, :], self.first[:, :, :], self.chosen[:, :, :])
        v.memset(self.gates[:, :, 8:9], 1.0)
        v.tensor_tensor(self.gates[:, :, 0:8], self.chosen[:, :, :], self.probs[:, :, :], ALU.mult).then_inc(self.gates_ready, 1)
        v.wait_ge(self.gates_ready, self.gating + 1)

        def bias(two, place, odd):
            if two is None:
                return self.b3[:, 0, odd:odd + 1]
            return column(self.b3[:, 1:, odd].rearrange("p (o b) -> p o b", b=2), two, place)

        def gate(two, place, j):
            if two is None:
                return self.gates[:, j, self.n - 1:self.n]
            return column(self.gates[:, j, 0:self.n - 1].rearrange("p (o b) -> p o b", b=2), two, place)

        def add(two, place, e):
            v.wait_ge(self.out_ready, e + 1)
            v.wait_ge(self.y_added, e + 1)
            for j in range(TILES):
                last = v.scalar_tensor_tensor(out=self.y[:, j, :], in0=k.tok_psum(4, D)[:, j // 2, j % 2, :],
                                              scalar=gate(two, place, j), in1=self.y[:, j, :], op0=ALU.mult, op1=ALU.add)
            last.then_inc(self.y_added, 1)

        def expert(two, place, e, buf):
            for odd, out in ((0, self.xg), (1, self.xl)):
                v.wait_ge(self.lin_done, 2 * e + odd + 1)
                v.wait_ge(self.h3_ready, 2 * e + odd + 1)
                v.scalar_tensor_tensor(out=out[:, :], in0=k.pair(1, DH), scalar=bias(two, place, odd), in1=self.lin[:, odd, :],
                                       op0=ALU.add, op1=ALU.mult).then_inc(self.prod_done, 1)
                v.wait_ge(self.prod_done, 2 * e + odd + 1)
                if odd == 0:
                    v.tensor_scalar(self.xg[:, :], self.xg[:, :], self.LIMIT, None, ALU.min).then_inc(self.xg_ready, 1)
                    v.wait_ge(self.xg_ready, e + 1)
            own(v.tensor_scalar(self.xl[:, :], self.xl[:, :], self.LIMIT, -self.LIMIT, ALU.min, ALU.max))
            v.wait_ge(self.sig_ready, e + 1)
            own(v.tensor_tensor(self.xg[:, :], self.xg[:, :], self.sig[:, :], ALU.mult))
            v.scalar_tensor_tensor(out=self.g[:, buf, :], in0=self.xl[:, :], scalar=1.0, in1=self.xg[:, :],
                                   op0=ALU.add, op1=ALU.mult).then_inc(self.g_ready, 1)
            v.wait_ge(self.g_ready, e + 1)
            if two is not None:
                add(two, place, e - 1)

        expert(None, 0, 0, 0)
        with own.loop(self.n // 2, 4) as two:
            expert(two, 0, 2 * two + 1, 1)
            expert(two, 1, 2 * two + 2, 0)
        add(None, 0, self.n - 1)
        v.wait_ge(self.b2_ready, 1)
        v.wait_ge(self.y_added, self.n + 1)
        own(v.tensor_tensor(pairs_of(self.y[:, :, :]), pairs_of(self.y[:, :, :]), k.tok_psum(4, D), ALU.add))
        v.wait_ge(self.y_added, self.n + 1)
        v.tensor_tensor(k.h[:, :, :], k.h[:, :, :], self.y[:, :, :], ALU.add).then_inc(k.h_ready, 1)

    def pool(self, g, own):
        pass



SPAN = SEQ + P


def causal_parts():
    return ((0, 0, slice(0, SEQ)), (1, P, slice(SEQ, SPAN)))


class ErfAttention:
    HEADS, HEAD = 12, 16
    BUFS = 4
    PAD = 32
    COLS = HEAD + 1
    FLOOR = 1e-6
    TURN = 2 ** 0.5 * HEAD ** -0.5
    TINY = 1e-20
    LEAST = 3 * 2.0 ** -24 - 1

    def __init__(self, k, name, norm, w):
        self.k, self.norm, self.w = k, norm, w
        sb, s = (lambda x, shape, t=F32: k.sb(name + "_" + x, shape, t)), (lambda x: k.sem(name + "_" + x))
        H, G = self.HEADS, 2 * self.HEADS
        self.w_qkv, self.w_proj = sb("w_qkv", [DH, 2, 3 * D]), sb("w_proj", [DH, 2, D])
        self.cos, self.sin, self.mask = sb("cos", [P, 2, 8]), sb("sin", [P, 2, 8]), sb("mask", [P, SPAN])
        self.qk = sb("qk", [P, TILES, G, self.PAD])
        self.t1, self.t2 = sb("t1", [P, IMAGES, G, 8]), sb("t2", [P, IMAGES, G, 8])
        self.v = sb("v", [P, TILES, H, self.COLS])
        self.qkT = sb("qkT", [P, 6, TOKENS])
        self.wts = sb("wts", [P, self.BUFS, 2, SPAN])
        self.gelu, self.ratio = sb("gelu", [P, self.BUFS, 2, SPAN]), sb("ratio", [P, self.BUFS, 2, SPAN])
        self.inv = sb("inv", [P, self.BUFS, 2, SPAN])
        self.den = sb("den", [P, TILES, H])
        self.tiny, self.minus_one = sb("tiny", [P, 1]), sb("minus_one", [P, 1])
        self.y = sb("y", [P, TILES, D])
        self.consts_loaded, self.v_ready, self.qk_ready = s("consts_loaded"), s("v_ready"), s("qk_ready")
        self.rotated, self.qk_written, self.v_copied = s("rotated"), s("qk_written"), s("v_copied")
        self.qkT_ready, self.qkT_copied = s("qkT_ready"), s("qkT_copied")
        self.scores_ready, self.abs_done, self.wts_ready = s("scores_ready"), s("abs_done"), s("wts_ready")
        self.consts_filled, self.divided, self.erf_ready = s("consts_filled"), s("divided"), s("erf_ready")
        self.gelu_done, self.ratio_ready = s("gelu_done"), s("ratio_ready")
        self.av_ready, self.y_ready = s("av_ready"), s("y_ready")
        self.yT_ready, self.yT_copied, self.out_ready = s("yT_ready"), s("yT_copied"), s("out_ready")

    def sync(self, sp):
        w = self.w
        sp.wait_ge(self.k.h_ready, self.norm)
        for dst, src in ((self.w_qkv[:, :, :], w["qkv_T"].rearrange("(c p) m -> p c m", p=DH)),
                         (self.w_proj[:, :, :], w["proj_T"].rearrange("(c p) m -> p c m", p=DH)),
                         (self.cos[:, :, :], w["cos"]), (self.sin[:, :, :], w["sin"]), (self.mask[:, :], w["mask"])):
            sp.dma_start(dst, src).then_inc(self.consts_loaded, 16)

    def units(self):
        return [(6 * b + u, b, 2 * u) for b in range(IMAGES) for u in range(6)]

    def tensor(self, pe, own):
        k, H = self.k, self.HEADS
        norm_tensor(k, pe, self.norm)
        pe.wait_ge(self.consts_loaded, 80)
        for j in range(TILES):
            for c in range(2):
                last = pe.matmul(k.tok_psum(4, D)[:, j // 2, j % 2, :], k.xnF[:, c, P * j:P * (j + 1)],
                                 self.w_qkv[:, c, 2 * D:3 * D], start=(c == 0), stop=(c == 1))
        last.then_inc(self.v_ready, 1)
        for half in range(2):
            if half == 1:
                pe.wait_ge(self.rotated, 1)
            for b in range(IMAGES):
                for c in range(2):
                    last = pe.matmul(k.ps[:, b, 0:2 * D], k.xnF[:, c, P * (2 * b + half):P * (2 * b + half + 1)],
                                     self.w_qkv[:, c, 0:2 * D], start=(c == 0), stop=(c == 1))
            last.then_inc(self.qk_ready, 1)
        pe.wait_ge(self.qk_written, 4)
        pe.wait_ge(self.v_copied, 1)
        for g in range(6):
            if g >= 4:
                pe.wait_ge(self.qkT_copied, g - 3)
            for j in range(TILES):
                last = pe.transpose(k.pair(g % 4)[:, P * j:P * (j + 1)],
                                    self.qk[:, j, 4 * g:4 * g + 4, :].rearrange("p h d -> p (h d)"), k.ident[:, :])
            last.then_inc(self.qkT_ready, 1)
        pe.wait_ge(self.qkT_copied, 6)

        def scores(unit, b, head):
            if unit >= 2:
                pe.wait_ge(self.gelu_done, unit - 1)
            for i in range(2):
                rows = slice(self.PAD * ((head + i) % 4), self.PAD * ((head + i) % 4 + 1))
                g = (head + i) // 4
                for t, s0, cols in causal_parts():
                    key = SEQ * b + P * t
                    last = pe.matmul(k.ps[:, 2 * (unit % 2) + i, cols], self.qkT[rows, 3 + g, key:key + P],
                                     self.qkT[rows, g, SEQ * b + s0:SEQ * (b + 1)], start=True, stop=True)
            last.then_inc(self.scores_ready, 1)

        def weigh(unit, b, head):
            pe.wait_ge(self.wts_ready, unit + 1)
            for i in range(2):
                h = head + i
                wt = self.wts[:, unit % self.BUFS, i, :]
                out = k.tok_psum(4, H * self.COLS)[:, b, :, self.COLS * h:self.COLS * (h + 1)]
                pe.matmul(out[:, 0, :], wt[:, 0:P], self.v[:, 2 * b, h, :], start=True, stop=True)
                pe.matmul(out[:, 1, :], wt[:, P:SEQ], self.v[:, 2 * b, h, :], start=True, stop=False)
                last = pe.matmul(out[:, 1, :], wt[:, SEQ:SPAN], self.v[:, 2 * b + 1, h, :], start=False, stop=True)
            last.then_inc(self.av_ready, 1)

        units = self.units()
        scores(*units[0])
        scores(*units[1])
        for n in range(len(units) + 1):
            if n + 2 < len(units):
                scores(*units[n + 2])
            if n >= 1:
                weigh(*units[n - 1])
        pe.wait_ge(self.y_ready, 1)
        transpose_tokens(k, pe, self.y).then_inc(self.yT_ready, 1)
        pe.wait_ge(self.yT_copied, 2)
        for j in range(TILES):
            for c in range(2):
                last = pe.matmul(k.tok_psum(4, D)[:, j // 2, j % 2, :], k.xnF[:, c, P * j:P * (j + 1)],
                                 self.w_proj[:, c, :], start=(c == 0), stop=(c == 1))
        last.then_inc(self.out_ready, 1)

    def scalar(self, a, own):
        k = self.k
        norm_scalar(k, a, self.norm)
        a.wait_ge(self.v_ready, 1)
        for half in range(2):
            last = a.copy(self.v[:, half::2, :, 0:self.HEAD],
                          k.tok_psum(4, D)[:, :, half, :].rearrange("p b (h d) -> p b h d", d=self.HEAD))
        last.then_inc(self.v_copied, 1)
        for g in range(6):
            a.wait_ge(self.qkT_ready, g + 1)
            a.copy(self.qkT[:, g, :], k.pair(g % 4)).then_inc(self.qkT_copied, 1)

        def erf(unit):
            a.wait_ge(self.divided, unit + 1)
            ratio = self.ratio[:, unit % self.BUFS, :, :]
            a.activation(ratio, ratio, ACT.Identity, bias=self.minus_one[:, :], scale=2 / self.TURN).then_inc(self.erf_ready, 1)

        a.wait_ge(self.consts_filled, 1)
        for unit in range(len(self.units())):
            a.wait_ge(self.scores_ready, unit + 1)
            if unit >= self.BUFS:
                a.wait_ge(self.divided, unit - self.BUFS + 1)
            a.activation(self.inv[:, unit % self.BUFS, :, :], k.ps[:, 2 * (unit % 2):2 * (unit % 2) + 2, 0:SPAN], ACT.Abs)
            own(a.activation(self.gelu[:, unit % self.BUFS, :, :], k.ps[:, 2 * (unit % 2):2 * (unit % 2) + 2, 0:SPAN],
                             ACT.Gelu, scale=self.TURN))
            a.activation(self.inv[:, unit % self.BUFS, :, :], self.inv[:, unit % self.BUFS, :, :], ACT.Identity,
                         bias=self.tiny[:, :]).then_inc(self.abs_done, 1)
            a.activation(self.gelu[:, unit % self.BUFS, :, :], self.gelu[:, unit % self.BUFS, :, :], ACT.Abs).then_inc(self.gelu_done, 1)
            if unit >= 1:
                erf(unit - 1)
        erf(len(self.units()) - 1)
        a.wait_ge(self.yT_ready, 1)
        a.copy(k.xnF[:, 0, :], k.pair(0, DH)).then_inc(self.yT_copied, 1)

    def vector(self, v, own):
        k, H, G = self.k, self.HEADS, 2 * self.HEADS
        v.memset(self.qk[:, :, :, self.HEAD:], 0.0)
        v.memset(self.v[:, :, :, self.HEAD:], 1.0)
        v.memset(self.tiny[:, :], self.TINY)
        v.memset(self.minus_one[:, :], -1.0).then_inc(self.consts_filled, 1)
        norm_vector(k, v, own, self.norm)
        v.wait_ge(self.consts_loaded, 80)
        for half in range(2):
            v.wait_ge(self.qk_ready, half + 1)
            x = k.ps[:, 0:IMAGES, 0:2 * D].rearrange("p b (h d e) -> p b h d e", h=G, e=2)
            wide = [P, IMAGES, G, 8]
            for i, (first, second, op) in enumerate(((self.cos, self.sin, ALU.subtract), (self.sin, self.cos, ALU.add))):
                for b in range(IMAGES):
                    v.tensor_tensor(self.t1[:, b], x[:, b, :, :, 0], first[:, half, :].unsqueeze(1).to_broadcast(wide[0:1] + wide[2:]), ALU.mult)
                    last = v.tensor_tensor(self.t2[:, b], x[:, b, :, :, 1], second[:, half, :].unsqueeze(1).to_broadcast(wide[0:1] + wide[2:]), ALU.mult)
                if i == 0:
                    own(last)
                else:
                    last.then_inc(self.rotated, 1)
                    v.wait_ge(self.rotated, half + 1)
                v.tensor_tensor(self.qk[:, half::2, :, 8 * i:8 * i + 8], self.t1[:, :, :, :], self.t2[:, :, :, :],
                                op).then_inc(self.qk_written, 1)
                v.wait_ge(self.qk_written, 2 * half + i + 1)

        def clip(unit):
            ratio = self.ratio[:, unit % self.BUFS, :, :]
            v.wait_ge(self.erf_ready, unit + 1)
            v.tensor_scalar(ratio, ratio, self.LEAST, 1.0, ALU.max, ALU.add).then_inc(self.ratio_ready, 1)

        for unit in range(len(self.units())):
            inv = self.inv[:, unit % self.BUFS, :, :]
            v.wait_ge(self.abs_done, unit + 1)
            own(v.reciprocal(inv, inv))
            v.wait_ge(self.gelu_done, unit + 1)
            if unit >= self.BUFS:
                v.wait_ge(self.wts_ready, unit - self.BUFS + 1)
            v.scalar_tensor_tensor(out=self.ratio[:, unit % self.BUFS, :, :], in0=self.gelu[:, unit % self.BUFS, :, :],
                                   scalar=self.TINY * self.TURN / 2, in1=inv, op0=ALU.add, op1=ALU.mult).then_inc(self.divided, 1)
            if unit >= 1:
                clip(unit - 1)
        clip(len(self.units()) - 1)
        v.wait_ge(self.av_ready, len(self.units()))
        sums = k.tok_psum(4, H * self.COLS).rearrange("p b t (h d) -> p b t h d", d=self.COLS)
        for half in range(2):
            last = v.tensor_scalar(self.den[:, half::2, :], sums[:, :, half, :, self.HEAD], self.FLOOR, None, ALU.max)
        own(last)
        own(v.reciprocal(self.den[:, :, :], self.den[:, :, :]))
        for half in range(2):
            last = v.tensor_tensor(self.y[:, half::2, :].rearrange("p b (h d) -> p b h d", d=self.HEAD),
                                   sums[:, :, half, :, 0:self.HEAD],
                                   self.den[:, half::2, :].unsqueeze(3).to_broadcast([P, IMAGES, H, self.HEAD]), ALU.mult)
        last.then_inc(self.y_ready, 1)
        v.wait_ge(self.yT_ready, 1)
        v.tensor_copy(k.xnF[:, 1, :], k.pair(1, DH)).then_inc(self.yT_copied, 1)
        v.wait_ge(self.out_ready, 1)
        v.tensor_tensor(pairs_of(k.h[:, :, :]), pairs_of(k.h[:, :, :]), k.tok_psum(4, D), ALU.add).then_inc(k.h_ready, 1)

    def pool(self, g, own):
        g.wait_ge(self.consts_loaded, 80)
        for unit in range(len(self.units())):
            g.wait_ge(self.ratio_ready, unit + 1)
            if unit >= self.BUFS:
                g.wait_ge(self.av_ready, unit - self.BUFS + 1)
            g.tensor_tensor(self.wts[:, unit % self.BUFS, :, :], self.ratio[:, unit % self.BUFS, :, :],
                            self.mask[:, :].unsqueeze(1).to_broadcast([P, 2, SPAN]), ALU.mult).then_inc(self.wts_ready, 1)


class Retention:

    def __init__(self, k, name, norm, w):
        self.k, self.norm, self.w = k, norm, w
        sb, s = (lambda x, shape, t=F32: k.sb(name + "_" + x, shape, t)), (lambda x: k.sem(name + "_" + x))
        self.w_qkv, self.qk_b, self.v_b = sb("w_qkv", [DH, 2, 3 * D]), sb("qk_b", [DH, 4]), sb("v_b", [P, D])
        self.mask = sb("mask", [P, SPAN])
        self.qk = sb("qk", [DH, 4, TOKENS])
        self.v = sb("v", [P, TILES, D])
        self.wts = sb("wts", [P, IMAGES, SPAN])
        self.consts_loaded, self.qk_ready, self.qk_copied = s("consts_loaded"), s("qk_ready"), s("qk_copied")
        self.v_ready, self.v_copied = s("v_ready"), s("v_copied")
        self.scores_ready, self.wts_ready, self.out_ready = s("scores_ready"), s("wts_ready"), s("out_ready")

    def sync(self, sp):
        w = self.w
        sp.wait_ge(self.k.h_ready, self.norm)
        for dst, src in ((self.w_qkv[:, :, :], w["qkv"].rearrange("(c p) m -> p c m", p=DH)), (self.qk_b[:, :], w["qk_b"]),
                         (self.v_b[:, :], w["v_b"].to_broadcast([P, D])), (self.mask[:, :], w["mask"])):
            sp.dma_start(dst, src).then_inc(self.consts_loaded, 16)

    def tensor(self, pe, own):
        k = self.k
        norm_tensor(k, pe, self.norm)
        pe.wait_ge(self.consts_loaded, 64)
        for m in range(4):
            for c in range(2):
                for t in range(2):
                    last = pe.matmul(k.pair(m, DH)[:, BANK * t:BANK * (t + 1)], self.w_qkv[:, c, DH * m:DH * (m + 1)],
                                     k.xnF[:, c, BANK * t:BANK * (t + 1)], start=(c == 0), stop=(c == 1))
            last.then_inc(self.qk_ready, 1)
        pe.wait_ge(self.qk_copied, 2)
        for j in range(TILES):
            for c in range(2):
                last = pe.matmul(k.tok_psum(0, D)[:, j // 2, j % 2, :], k.xnF[:, c, P * j:P * (j + 1)],
                                 self.w_qkv[:, c, 2 * D:3 * D], start=(c == 0), stop=(c == 1))
        last.then_inc(self.v_ready, 1)
        pe.wait_ge(self.qk_copied, 4)
        for b in range(IMAGES):
            for t, s0, cols in causal_parts():
                key = SEQ * b + P * t
                for c in range(2):
                    last = pe.matmul(k.ps[:, 4 + b, cols], self.qk[:, 2 + c, key:key + P],
                                     self.qk[:, c, SEQ * b + s0:SEQ * (b + 1)], start=(c == 0), stop=(c == 1))
            last.then_inc(self.scores_ready, 1)
        pe.wait_ge(self.v_copied, 1)
        for b in range(IMAGES):
            pe.wait_ge(self.wts_ready, b + 1)
            out, wt = k.tok_psum(0, D)[:, b], self.wts[:, b, :]
            pe.matmul(out[:, 0, :], wt[:, 0:P], self.v[:, 2 * b, :], start=True, stop=True)
            pe.matmul(out[:, 1, :], wt[:, P:SEQ], self.v[:, 2 * b, :], start=True, stop=False)
            last = pe.matmul(out[:, 1, :], wt[:, SEQ:SPAN], self.v[:, 2 * b + 1, :], start=False, stop=True)
        last.then_inc(self.out_ready, 1)

    def scalar(self, a, own):
        k = self.k
        norm_scalar(k, a, self.norm)
        a.wait_ge(self.consts_loaded, 64)
        for m in range(4):
            a.wait_ge(self.qk_ready, m + 1)
            a.activation(self.qk[:, m, :], k.pair(m, DH), ACT.Identity, bias=self.qk_b[:, m:m + 1]).then_inc(self.qk_copied, 1)

    def vector(self, v, own):
        k = self.k
        norm_vector(k, v, own, self.norm)
        v.wait_ge(self.consts_loaded, 64)
        v.wait_ge(self.v_ready, 1)
        for half in range(2):
            last = v.tensor_tensor(self.v[:, half::2, :], k.tok_psum(0, D)[:, :, half, :],
                                   self.v_b[:, :].unsqueeze(1).to_broadcast([P, IMAGES, D]), ALU.add)
        last.then_inc(self.v_copied, 1)
        for b in range(IMAGES):
            v.wait_ge(self.scores_ready, b + 1)
            v.scalar_tensor_tensor(out=self.wts[:, b, :], in0=k.ps[:, 4 + b, 0:SPAN], scalar=D ** -0.5, in1=self.mask[:, :],
                                   op0=ALU.mult, op1=ALU.mult).then_inc(self.wts_ready, 1)
        v.wait_ge(self.out_ready, 1)
        v.tensor_tensor(pairs_of(k.h[:, :, :]), pairs_of(k.h[:, :, :]), k.tok_psum(0, D), ALU.add).then_inc(k.h_ready, 1)

    def pool(self, g, own):
        pass



class Tokenizer:
    SIDE, LEVELS, GROUP, EMBED = 64, (1, 2, 4), 16, 64
    PLACES = (4096, 1024, 256)
    LENGTHS = (256, 64, 16)
    WIDTHS = (3, 12, 48)

    def __init__(self, k, name, norm, w):
        self.k, self.norm, self.w = k, norm, w
        sb, s = (lambda x, shape, t=F32: k.sb(name + "_" + x, shape, t)), (lambda x: k.sem(name + "_" + x))
        G, E = self.GROUP, self.EMBED
        self.rows = [P, self.LENGTHS[1], self.LENGTHS[2]]
        self.tiles = [2, 1, 1]
        self.raw = [sb("raw%d" % q, [self.rows[q], self.tiles[q], G], I32) for q in range(3)]
        self.pos = [sb("pos%d" % q, [self.rows[q], self.tiles[q], G]) for q in range(3)]
        self.neg = [sb("neg%d" % q, [self.rows[q], self.tiles[q], G]) for q in range(3)]
        self.idx = [sb("idx%d" % q, [self.rows[q], self.tiles[q], G], U32) for q in range(3)]
        self.got = [sb("got%d" % q, [self.rows[q], self.tiles[q], G, IMAGES * self.WIDTHS[q]]) for q in range(3)]
        self.byimage = [sb("byimage%d" % q, [self.rows[q], self.tiles[q], IMAGES, G * self.WIDTHS[q]]) for q in range(3)]
        self.byimage_ready = s("byimage_ready")
        self.gotT = [sb("gotT0", [G * 3, TOKENS]), sb("gotT1", [DH, 2, IMAGES, 64]), sb("gotT2", [DH, 8, IMAGES, 16])]
        self.W = [sb("W0", [G * 3, E]), sb("W1", [DH, 2, E]), sb("W2", [DH, 8, E])]
        self.b, self.fuse, self.fuse_b = sb("b", [E, 3]), sb("fuse", [E, 3, D]), sb("fuse_b", [P, D])
        self.stretch = [None, sb("stretch1", [64, SEQ]), sb("stretch2", [16, SEQ])]
        self.short = [None, sb("short1", [64, IMAGES, E]), sb("short2", [16, IMAGES, E])]
        self.e = sb("e", [E, 3, TOKENS])
        self.consts_loaded, self.idx_loaded, self.idx_ready = s("consts_loaded"), s("idx_loaded"), s("idx_ready")
        self.gathered = [s("gathered0"), s("gathered1"), s("gathered2")]
        self.gotT_ready, self.gotT_copied = s("gotT_ready"), s("gotT_copied")
        self.short_ready, self.short_copied = s("short_ready"), s("short_copied")
        self.e_ready, self.e_copied, self.out_ready = s("e_ready"), s("e_copied"), s("out_ready")

    def sync(self, sp):
        w = self.w
        for q in range(3):
            sp.dma_start(self.raw[q][:, :, :], w["idx%d" % q].rearrange("(t p g) -> p t g", p=self.rows[q], g=self.GROUP)).then_inc(self.idx_loaded, 16)
        for dst, src in ((self.W[0][:, :], w["W0_T"]), (self.W[1][:, :, :], w["W1_T"].rearrange("(c p) m -> p c m", p=DH)),
                         (self.W[2][:, :, :], w["W2_T"].rearrange("(c p) m -> p c m", p=DH)), (self.b[:, :], w["b"]),
                         (self.stretch[1][:, :], w["stretch1"]), (self.stretch[2][:, :], w["stretch2"]),
                         (self.fuse[:, :, :], w["fuse_T"].rearrange("(c p) m -> p c m", p=self.EMBED)),
                         (self.fuse_b[:, :], w["fuse_b"].to_broadcast([P, D]))):
            sp.dma_start(dst, src).then_inc(self.consts_loaded, 16)

    def pool(self, g, own):
        for q in (2, 1, 0):
            g.wait_ge(self.idx_ready, 3 - q)
            for t in range(self.tiles[q]):
                for i in range(self.GROUP):
                    g.indirect_dma_start(out=self.got[q][:, t, i, :], out_offset=None, in_=self.w["patches%d" % q],
                                         in_offset=bass.IndirectOffsetOnAxis(ap=self.idx[q][:, t, i:i + 1], axis=0)).then_inc(self.gathered[q], 16)

    def tensor(self, pe, own):
        k, G = self.k, self.GROUP
        pe.wait_ge(self.consts_loaded, 16 * 8)
        pe.wait_ge(self.byimage_ready, 1)
        for b in range(IMAGES):
            for c in range(8):
                last = pe.transpose(k.ps[0:DH, 4, 64 * c + 16 * b:64 * c + 16 * b + 16],
                                    self.byimage[2][:, 0, b, DH * c:DH * (c + 1)], k.ident[0:16, 0:16])
        last.then_inc(self.gotT_ready, 1)
        pe.wait_ge(self.byimage_ready, 2)
        for b in range(IMAGES):
            for c in range(2):
                last = pe.transpose(k.ps[0:DH, 2, 256 * c + 64 * b:256 * c + 64 * b + 64],
                                    self.byimage[1][:, 0, b, DH * c:DH * (c + 1)], k.ident[0:64, 0:64])
        last.then_inc(self.gotT_ready, 1)
        pe.wait_ge(self.gotT_copied, 1)
        for b in range(IMAGES):
            for c in range(8):
                last = pe.matmul(k.ps[0:16, 5, 64 * b:64 * b + 64], self.gotT[2][:, c, b, :], self.W[2][:, c, :],
                                 start=(c == 0), stop=(c == 7))
        last.then_inc(self.short_ready, 1)
        pe.wait_ge(self.gotT_copied, 2)
        for b in range(IMAGES):
            for c in range(2):
                last = pe.matmul(k.ps[0:64, 3, 64 * b:64 * b + 64], self.gotT[1][:, c, b, :], self.W[1][:, c, :],
                                 start=(c == 0), stop=(c == 1))
        last.then_inc(self.short_ready, 1)
        for n, (q, pair) in enumerate(((2, 2), (1, 1))):
            pe.wait_ge(self.short_copied, n + 1)
            if q == 1:
                pe.wait_ge(self.short_copied, 2)
            for b in range(IMAGES):
                last = pe.matmul(k.pair(pair, 64)[:, SEQ * b:SEQ * (b + 1)], self.short[q][:, b, :], self.stretch[q][:, :],
                                 start=True, stop=True)
            last.then_inc(self.e_ready, 1)

        def fuse(q, first, last):
            for j in range(TILES):
                ins = pe.matmul(k.tok_psum(4, D)[:, j // 2, j % 2, :], self.e[:, q, P * j:P * (j + 1)], self.fuse[:, q, :],
                                start=first and j % 2 == 0, stop=last, skip_group_check=True)
            return ins

        pe.wait_ge(self.e_copied, 2)
        fuse(2, True, False)
        fuse(1, False, False)
        pe.wait_ge(self.byimage_ready, 4)
        for j in range(TILES):
            last = pe.transpose(k.pair(0, 48)[:, P * j:P * (j + 1)], self.byimage[0][:, j % 2, j // 2, :],
                                k.ident[:, :])
        last.then_inc(self.gotT_ready, 1)
        pe.wait_ge(self.gotT_copied, 3)
        for t in range(2):
            last = pe.matmul(k.pair(0, 64)[:, BANK * t:BANK * (t + 1)], self.W[0][:, :], self.gotT[0][:, BANK * t:BANK * (t + 1)],
                             start=True, stop=True)
        last.then_inc(self.e_ready, 1)
        pe.wait_ge(self.e_copied, 3)
        fuse(0, False, True).then_inc(self.out_ready, 1)

    def scalar(self, a, own):
        k = self.k
        a.wait_ge(self.consts_loaded, 16 * 8)
        a.wait_ge(self.gotT_ready, 1)
        a.copy(self.gotT[2][:, :, :, :].rearrange("p c b l -> p (c b l)"), k.ps[0:DH, 4, :]).then_inc(self.gotT_copied, 1)
        a.wait_ge(self.gotT_ready, 2)
        a.copy(self.gotT[1][:, :, :, :].rearrange("p c b l -> p (c b l)"), k.ps[0:DH, 2, :]).then_inc(self.gotT_copied, 1)
        a.wait_ge(self.short_ready, 1)
        a.copy(self.short[2][:, :, :].rearrange("p b f -> p (b f)"), k.ps[0:16, 5, 0:256]).then_inc(self.short_copied, 1)
        a.wait_ge(self.short_ready, 2)
        a.copy(self.short[1][:, :, :].rearrange("p b f -> p (b f)"), k.ps[0:64, 3, 0:256]).then_inc(self.short_copied, 1)
        for n, (q, pair) in enumerate(((2, 2), (1, 1))):
            a.wait_ge(self.e_ready, n + 1)
            a.activation(self.e[:, q, :], k.pair(pair, 64), ACT.Identity, bias=self.b[:, q:q + 1]).then_inc(self.e_copied, 1)
        a.wait_ge(self.gotT_ready, 3)
        a.copy(self.gotT[0][:, :], k.pair(0, 48)).then_inc(self.gotT_copied, 1)
        a.wait_ge(self.e_ready, 3)
        a.activation(self.e[:, 0, :], k.pair(0, 64), ACT.Identity, bias=self.b[:, 0:1]).then_inc(self.e_copied, 1)

    def vector(self, v, own):
        k = self.k
        v.wait_ge(self.idx_loaded, 16 * 3)
        for q in (2, 1, 0):
            raw, pos, neg, n = self.raw[q][:, :, :], self.pos[q][:, :, :], self.neg[q][:, :, :], float(self.PLACES[q])
            own(v.tensor_copy(pos, raw))
            own(v.tensor_scalar(neg, pos, 0.0, n, ALU.is_lt, ALU.mult))
            own(v.tensor_tensor(pos, pos, neg, ALU.add))
            v.tensor_scalar(self.idx[q][:, :, :], pos, 0.0, n - 1, ALU.max, ALU.min).then_inc(self.idx_ready, 1)
        for q in (2, 1, 0):
            v.wait_ge(self.gathered[q], 16 * self.tiles[q] * self.GROUP)
            for t in range(self.tiles[q]):
                v.tensor_copy(self.byimage[q][:, t, :, :].rearrange("p b (g w) -> p b g w", g=self.GROUP),
                              self.got[q][:, t, :, :].rearrange("p g (b w) -> p b g w", b=IMAGES)).then_inc(self.byimage_ready, 1)
        v.wait_ge(self.consts_loaded, 16 * 8)
        v.wait_ge(self.out_ready, 1)
        for half in range(2):
            last = v.tensor_tensor(k.h[:, half::2, :], k.tok_psum(4, D)[:, :, half, :],
                                   self.fuse_b[:, :].unsqueeze(1).to_broadcast([P, IMAGES, D]), ALU.add)
        last.then_inc(k.h_ready, 1)



class Neurons:
    N, RANK, KEY, TOP = 128, 128, 64, 4
    NONE = -1.0
    LISTS = 2 * TILES
    F_AT_ONCE, R_AT_ONCE = 4, 2
    SET = 4

    def __init__(self, k, name, norm, w):
        self.k, self.norm, self.w = k, norm, w
        sb, s = (lambda x, shape, t=F32: k.sb(name + "_" + x, shape, t)), (lambda x: k.sem(name + "_" + x))
        wide = [P, self.LISTS, self.N]
        self.key_w, self.key_b = sb("key_w", [DH, 2, P]), sb("key_b", [P, 1])
        self.emb, self.emb_sq = sb("emb", [P, 2, self.KEY]), sb("emb_sq", [P, 2, self.KEY])
        self.norms = sb("norms", [P, 2])
        self.embT, self.keys = sb("embT", [P, self.N]), sb("keys", [P, TOKENS])
        self.probs = sb("probs", wide)
        self.greatest = sb("greatest", [P, self.LISTS, 8])
        self.values, self.others = (sb(x, [P, self.LISTS, self.N + 8 - self.TOP]) for x in ("values", "others"))
        self.best = sb("best", [P, self.LISTS])
        self.F = sb("F", [DH, 2, 2, self.F_AT_ONCE * self.RANK])
        self.R = sb("R", [P, 2, self.R_AT_ONCE * D])
        self.feat, self.featT = sb("feat", [P, TILES, self.RANK]), sb("featT", [P, TOKENS])
        self.y = sb("y", [P, TILES, D])
        self.consts_loaded = s("consts_loaded")
        self.F_loaded, self.R_loaded = [s("F_loaded0"), s("F_loaded1")], [s("R_loaded0"), s("R_loaded1")]
        self.emb_ms_ready, self.emb_std_ready, self.emb_ready = s("emb_ms_ready"), s("emb_std_ready"), s("emb_ready")
        self.embT_ready, self.embT_copied = s("embT_ready"), s("embT_copied")
        self.keys_ready, self.keys_copied = s("keys_ready"), s("keys_copied")
        self.route, k.routers = k.routers, k.routers + 1
        self.logits_ready, self.max_ready, self.exp_ready = k.sem("router_logits_ready"), k.sem("router_max_ready"), k.sem("router_exp_ready")
        self.F_set, self.R_set = s("F_set"), s("R_set")
        self.F_added, self.R_added = s("F_added"), s("R_added")
        self.feat_ready, self.featT_ready, self.featT_copied = s("feat_ready"), s("featT_ready"), s("featT_copied")

    def sync(self, sp):
        w = self.w
        sp.wait_ge(self.k.h_ready, self.norm)
        for dst, src in ((self.key_w[:, :, :], w["key_w"].rearrange("(c p) m -> p c m", p=DH)), (self.key_b[:, :], w["key_b"]),
                         (self.emb[:, :, :], w["emb"])):
            sp.dma_start(dst, src).then_inc(self.consts_loaded, 16)
        for table, buffers, loaded, done in ((w["F"], self.F, self.F_loaded, self.F_set), (w["R"], self.R, self.R_loaded, self.R_set)):
            def load(two, buf):
                src = pick_of_two(table, two, buf)
                if table is w["F"]:
                    src = src.rearrange("(c p) m -> p c m", p=DH)
                sp.dma_start(buffers[:, buf], src).then_inc(loaded[buf], 16)
            load(0, 0)
            load(0, 1)
            with sp.Fori(1, table.shape[0] // 2) as two:
                for buf in range(2):
                    sp.wait_ge(done, 4 * two + 2 * buf - 2)
                    load(two, buf)

    def tensor(self, pe, own):
        k = self.k
        norm_tensor(k, pe, self.norm)
        pe.wait_ge(self.consts_loaded, 48)
        for c in range(2):
            for t in range(2):
                last = pe.matmul(k.pair(2)[:, BANK * t:BANK * (t + 1)], self.key_w[:, c, :], k.xnF[:, c, BANK * t:BANK * (t + 1)],
                                 start=(c == 0), stop=(c == 1))
        last.then_inc(self.keys_ready, 1)
        pe.wait_ge(self.emb_ready, 1)
        pe.transpose(k.ps[:, 6, 0:P], self.emb[:, :, :].rearrange("p a b -> p (a b)"), k.ident[:, :]).then_inc(self.embT_ready, 1)
        pe.wait_ge(self.keys_copied, 1)
        pe.wait_ge(self.embT_copied, 1)
        for a in range(2):
            rows = slice(self.KEY * a, self.KEY * (a + 1))
            for j in range(TILES):
                last = pe.matmul(k.pair(a)[:, P * j:P * (j + 1)], self.keys[rows, P * j:P * (j + 1)], self.embT[rows, :],
                                 start=True, stop=True)
        last.then_inc(self.logits_ready, 1)
        pe.wait_ge(self.max_ready, self.route + 1)

        def pool_of_maps(groups, loaded, ready, added, lhs, rhs, halves, width):
            with pe.Fori(0, groups // 2) as two:
                for buf in range(2):
                    pe.wait_ge(loaded[buf], 16 * two + 16)
                    for s in range(2):
                        pe.wait_ge(added, 4 * two + 2 * buf + s + 1)
                        for b in range(self.SET):
                            j = self.SET * s + b
                            for c in range(halves):
                                last = pe.matmul(k.ps[:, j, 0:width], lhs(c)[:, P * j:P * (j + 1)], rhs(buf, c),
                                                 start=(c == 0), stop=(c == halves - 1))
                        last.then_inc(ready, 1)

        pool_of_maps(self.N // self.F_AT_ONCE, self.F_loaded, self.F_set, self.F_added,
                     lambda c: k.xnF[:, c, :], lambda buf, c: self.F[:, buf, c, :], 2, self.F_AT_ONCE * self.RANK)
        pe.wait_ge(self.feat_ready, 1)
        for j in range(TILES):
            last = pe.transpose(k.pair(0)[:, P * j:P * (j + 1)], self.feat[:, j, :], k.ident[:, :])
        last.then_inc(self.featT_ready, 1)
        pe.wait_ge(self.featT_copied, 1)
        pool_of_maps(self.N // self.R_AT_ONCE, self.R_loaded, self.R_set, self.R_added,
                     lambda c: self.featT[:, :], lambda buf, c: self.R[:, buf, :], 1, self.R_AT_ONCE * D)

    def scalar(self, a, own):
        k = self.k
        a.wait_ge(self.emb_ms_ready, 1)
        a.activation(self.norms[:, :], self.norms[:, :], ACT.Sqrt).then_inc(self.emb_std_ready, 1)
        norm_scalar(k, a, self.norm)
        a.wait_ge(self.consts_loaded, 48)
        a.wait_ge(self.keys_ready, 1)
        a.activation(self.keys[:, :], k.pair(2), ACT.Identity, bias=self.key_b[:, 0:1]).then_inc(self.keys_copied, 1)
        a.wait_ge(self.embT_ready, 1)
        a.copy(self.embT[:, :], k.ps[:, 6, 0:P]).then_inc(self.embT_copied, 1)
        a.wait_ge(self.max_ready, self.route + 1)
        a.activation(self.probs[:, :, :], self.probs[:, :, :], ACT.Exp).then_inc(self.exp_ready, 1)
        a.wait_ge(self.featT_ready, 1)
        a.copy(self.featT[:, :], k.pair(0)).then_inc(self.featT_copied, 1)

    def vector(self, v, own):
        k = self.k
        v.memset(self.feat[:, :, :], 0.0)
        v.memset(self.y[:, :, :], 0.0)
        v.memset(self.values[:, :, self.N:], self.NONE)
        v.sem_inc(self.F_added, 2)
        v.sem_inc(self.R_added, 2)
        v.wait_ge(self.consts_loaded, 48)
        own(v.tensor_tensor(self.emb_sq[:, :, :], self.emb[:, :, :], self.emb[:, :, :], ALU.mult))
        v.tensor_reduce(self.norms[:, :], self.emb_sq[:, :, :], AX.X, ALU.add).then_inc(self.emb_ms_ready, 1)
        v.wait_ge(self.emb_std_ready, 1)
        own(v.tensor_scalar(self.norms[:, :], self.norms[:, :], 1e-8, None, ALU.add))
        own(v.reciprocal(self.norms[:, :], self.norms[:, :]))
        v.tensor_tensor(self.emb[:, :, :], self.emb[:, :, :], self.norms[:, :].unsqueeze(2).to_broadcast([P, 2, self.KEY]),
                        ALU.mult).then_inc(self.emb_ready, 1)
        norm_vector(k, v, own, self.norm)
        wide = [P, self.LISTS, self.N]
        v.wait_ge(self.logits_ready, self.route + 1)
        logits = k.ps[:, 0:4, :].rearrange("p a b -> p (a b)").rearrange("p (l n) -> p l n", n=self.N)
        softmax_vector(k, v, own, logits, self.probs[:, :, :], self.best[:, :], self.max_ready, self.exp_ready, self.route + 1)
        own(v.tensor_copy(self.values[:, :, 0:self.N], self.probs[:, :, :]))
        for n in range(self.LISTS):
            last = v.max(self.greatest[:, n, :], self.values[:, n, :])
        own(last)
        own(v.memset(self.greatest[:, :, self.TOP:], self.NONE))
        for n in range(self.LISTS):
            last = v.match_replace(self.others[:, n, :], self.greatest[:, n, :], self.values[:, n, :], 0.0)
        own(last)
        w = self.probs
        own(v.tensor_tensor(w[:, :, :], w[:, :, :], self.others[:, :, 0:self.N], ALU.subtract))
        own(v.tensor_reduce(self.best[:, :], w[:, :, :], AX.X, ALU.add))
        own(v.tensor_scalar(self.best[:, :], self.best[:, :], 1e-8, None, ALU.add))
        own(v.reciprocal(self.best[:, :], self.best[:, :]))
        own(v.tensor_tensor(w[:, :, :], w[:, :, :], self.best[:, :].unsqueeze(2).to_broadcast(wide), ALU.mult))

        def add_up(twos, ready, added, out, width, each, row):
            with own.loop(twos, 4 * (each * self.SET - 1)) as two:
                for buf in range(2):
                    for s in range(2):
                        v.wait_ge(ready, 4 * two + 2 * buf + s + 1)
                        v.wait_ge(added, 4 * two + 2 * buf + s + 1)
                        for q in range(each):
                            for j in range(self.SET * s, self.SET * (s + 1)):
                                weights = w[:, row + j, :].rearrange("p (o m) -> p o m", m=2 * each)
                                own.wait_behind(self.SET - 1)
                                ins = v.scalar_tensor_tensor(
                                    out=out[:, j, :], in0=k.ps[:, j, width * q:width * (q + 1)],
                                    scalar=column(weights, two, each * buf + q), in1=out[:, j, :], op0=ALU.mult, op1=ALU.add)
                                if q < each - 1 or j < self.SET * (s + 1) - 1:
                                    own.mark(ins)
                        ins.then_inc(added, 1)
            v.wait_ge(added, 4 * twos + 2)

        add_up(self.N // self.F_AT_ONCE // 2, self.F_set, self.F_added, self.feat, self.RANK, self.F_AT_ONCE, 0)
        v.sem_inc(self.feat_ready, 1)
        add_up(self.N // self.R_AT_ONCE // 2, self.R_set, self.R_added, self.y, D, self.R_AT_ONCE, TILES)
        v.tensor_tensor(k.h[:, :, :], k.h[:, :, :], self.y[:, :, :], ALU.add).then_inc(k.h_ready, 1)

    def pool(self, g, own):
        pass



class Resolvent:
    KEEP = int(512 * (1.0 - 0.6))
    V_MAX, CLAMP, Z_MIN = 3.0, 10.0, -88.0
    ROWS, BACK, SEGMENTS = 36, 32, 16
    STEPS = SEQ // SEGMENTS

    def __init__(self, k, name, w, y):
        self.k, self.w, self.y = k, w, y
        sb, s = (lambda x, shape, t=F32: k.sb(name + "_" + x, shape, t)), (lambda x: k.sem(name + "_" + x))
        self.rows, self.scalars = sb("rows", [P, 5, D]), sb("scalars", [P, 3])
        self.turned = sb("turned", [P, P])
        self.prod = sb("prod", [P, TILES, D])
        self.v, self.z, self.score = sb("v", [P, TILES]), sb("z", [P, TILES]), sb("score", [P, TILES])
        self.above, self.greater, self.mask = sb("above", [P, TILES]), sb("greater", [P, TILES, SEQ]), sb("mask", [P, TILES])
        rows, S, L = self.ROWS, self.SEGMENTS, self.STEPS
        self.d, self.hist = sb("d", [rows, S, L]), sb("hist", [rows, SEQ, 2])
        self.p = sb("p", [rows, L + 2, 2, 2, S])
        self.grown, self.turn = sb("grown", [rows, 2, 2, S]), sb("turn", [rows, 2, 2, S])
        self.size = sb("size", [rows, 2, S])
        self.maps = sb("maps", [rows, S, 2, 2, 4])
        self.starts = sb("starts", [rows, S, 4])
        self.term = sb("term", [rows, 4, 4])
        self.coef = sb("coef", [rows, 2, 4, S])
        self.terms = sb("terms", [rows, 2, L + 1, 4, S])
        self.whole = sb("whole", [rows, 2, L + 1, S])
        self.t1, self.t2 = sb("t1", [rows, 3, L, S]), sb("t2", [rows, 3, L, S])
        self.size2 = sb("size2", [rows, L, S])
        self.back = sb("back", [P, 16])
        self.c = sb("c", [P, 2, 2, IMAGES])
        self.c2 = sb("c2", [P, 2, 2, IMAGES])
        self.cd = sb("cd", [P, 2, IMAGES])
        self.feat = sb("feat", [P, 2, TILES])
        self.mix = sb("mix", [P, TILES, D])
        self.consts_loaded = s("consts_loaded")
        self.z_ready, self.z_exp, self.score_ready, self.scores_spread = s("z_ready"), s("z_exp"), s("score_ready"), s("scores_spread")
        self.v_ready, self.vT_ready, self.hist_ready = s("v_ready"), s("vT_ready"), s("hist_ready")
        self.fwd_ready, self.back_copied, self.back_ready = s("fwd_ready"), s("back_copied"), s("back_ready")

    def sync(self, sp):
        w = self.w
        for dst, src in ((self.rows[:, :, :].rearrange("p r d -> p (r d)"), w["rows"].to_broadcast([P, 5 * D])),
                         (self.scalars[:, :], w["scalars"].to_broadcast([P, 3])),
                         (self.turned[:, :], w["turned"])):
            sp.dma_start(dst, src).then_inc(self.consts_loaded, 16)

    def tensor(self, pe, own):
        k = self.k
        pe.wait_ge(self.score_ready, 1)
        pe.wait_ge(self.consts_loaded, 48)
        for j in range(TILES):
            last = pe.matmul(k.pair(0)[:, P * j:P * (j + 1)], self.score[:, j:j + 1].to_broadcast([P, P]), k.ident[:, :],
                             start=True, stop=True)
        last.then_inc(self.scores_spread, 1)
        pe.wait_ge(self.v_ready, 1)
        for half in range(2):
            pe.matmul(k.ps[0:IMAGES, 2, P * half:P * (half + 1)], self.v[:, half::2], k.ident[:, :], start=True, stop=True)
            last = pe.matmul(k.ps[self.BACK:self.ROWS, 2, P * (1 - half):P * (2 - half)], self.v[:, half::2], self.turned[:, :],
                             start=True, stop=True)
        last.then_inc(self.vT_ready, 1)
        pe.wait_ge(self.hist_ready, 1)
        for part in range(2):
            for half in range(2):
                cols = slice(8 * part + 4 * half, 8 * part + 4 * half + 4)
                turned = slice(8 * part + 4 * (1 - half), 8 * part + 4 * (1 - half) + 4)
                pe.matmul(k.ps[:, 3, cols], self.hist[0:IMAGES, P * half:P * (half + 1), part], k.ident[0:IMAGES, 0:IMAGES],
                          start=True, stop=True)
                last = pe.matmul(k.ps[:, 4, turned], self.hist[self.BACK:self.ROWS, P * half:P * (half + 1), part],
                                 k.ident[self.BACK:self.ROWS, self.BACK:self.ROWS], start=True, stop=True)
        last.then_inc(self.fwd_ready, 1)
        pe.wait_ge(self.back_copied, 1)
        pe.matmul(k.ps[:, 5, 0:16], self.turned[:, :], self.back[:, :], start=True, stop=True).then_inc(self.back_ready, 1)

    def scalar_scores(self, a):
        a.wait_ge(self.z_ready, 1)
        a.activation(self.z[:, :], self.z[:, :], ACT.Exp, scale=-1.0).then_inc(self.z_exp, 1)

    def vector_scores(self, v, own):
        k = self.k
        v.wait_ge(self.consts_loaded, 48)
        for j in range(TILES):
            last = v.tensor_tensor_reduce(self.prod[:, j, :], k.xn[:, j, :], self.rows[:, 1, :], 1.0, 0.0, ALU.mult, ALU.add,
                                          self.z[:, j:j + 1])
        own(last)
        v.tensor_scalar(self.z[:, :], self.z[:, :], self.scalars[:, 1:2], self.Z_MIN, ALU.add, ALU.max).then_inc(self.z_ready, 1)
        v.wait_ge(self.z_exp, 1)
        own(v.tensor_scalar(self.score[:, :], self.z[:, :], 1.0, None, ALU.add))
        v.reciprocal(self.score[:, :], self.score[:, :]).then_inc(self.score_ready, 1)

    def vector(self, v, own):
        k = self.k
        for j in range(TILES):
            last = v.tensor_tensor_reduce(self.prod[:, j, :], self.y[:, j, :], self.rows[:, 0, :], 1.0, 0.0, ALU.mult, ALU.add,
                                          self.v[:, j:j + 1])
        own(last)
        own(v.tensor_scalar(self.v[:, :], self.v[:, :], self.scalars[:, 0:1], None, ALU.add))
        v.tensor_scalar(self.v[:, :], self.v[:, :], -self.V_MAX, self.V_MAX, ALU.max, ALU.min).then_inc(self.v_ready, 1)
        v.wait_ge(self.scores_spread, 1)
        for j in range(TILES):
            b = j // 2
            last = v.tensor_scalar(self.greater[:, j, :], k.pair(0)[:, SEQ * b:SEQ * (b + 1)], self.score[:, j:j + 1], 0.0,
                                   ALU.is_gt, ALU.add, accum_out=self.above[:, j:j + 1])
        own(last)
        own(v.tensor_scalar(self.mask[:, :], self.above[:, :], self.KEEP - 0.5, None, ALU.is_lt))
        self.fractions(v, own)
        v.wait_ge(self.fwd_ready, 1)
        v.tensor_copy(self.back[:, :], k.ps[:, 4, 0:16]).then_inc(self.back_copied, 1)
        by_token = lambda t: t.rearrange("p (part half b) -> p part half b", part=2, half=2)
        own(v.tensor_copy(self.c[:, :, :, :], by_token(k.ps[:, 3, 0:16])))
        v.wait_ge(self.back_ready, 1)
        own(v.tensor_tensor(self.c[:, :, :, :], self.c[:, :, :, :], by_token(k.ps[:, 5, 0:16]), ALU.add))
        half_image = lambda t: t.rearrange("p (b half) -> p half b", half=2)
        v.tensor_tensor(self.c[:, 0], self.c[:, 0], half_image(self.v[:, :]), ALU.subtract)
        own(v.tensor_scalar(self.c[:, 1], self.c[:, 1], 1.0, None, ALU.add))
        own(v.tensor_tensor(self.c2[:, :, :, :], self.c[:, :, :, :], self.c[:, :, :, :], ALU.mult))
        own(v.tensor_tensor(self.cd[:, :, :], self.c2[:, 0], self.c2[:, 1], ALU.add))
        own(v.reciprocal(self.cd[:, :, :], self.cd[:, :, :]))
        v.tensor_tensor(self.c[:, 0], self.c[:, 0], self.cd[:, :, :], ALU.mult)
        own(v.scalar_tensor_tensor(out=self.c[:, 1], in0=self.c[:, 1], scalar=-1.0, in1=self.cd[:, :, :], op0=ALU.mult, op1=ALU.mult))
        for part in range(2):
            last = v.tensor_tensor(half_image(self.feat[:, part, :]), self.c[:, part], half_image(self.mask[:, :]), ALU.mult)
        own(last)
        own(v.tensor_scalar(self.feat[:, :, :], self.feat[:, :, :], -self.CLAMP, self.CLAMP, ALU.max, ALU.min))
        for step in range(2):
            for j in range(TILES):
                if step == 0:
                    last = v.scalar_tensor_tensor(out=self.mix[:, j, :], in0=self.rows[:, 2, :], scalar=self.feat[:, 0, j:j + 1],
                                                  in1=self.rows[:, 4, :], op0=ALU.mult, op1=ALU.add)
                else:
                    last = v.scalar_tensor_tensor(out=self.mix[:, j, :], in0=self.rows[:, 3, :], scalar=self.feat[:, 1, j:j + 1],
                                                  in1=self.mix[:, j, :], op0=ALU.mult, op1=ALU.add)
            own(last)
        own(v.scalar_tensor_tensor(out=self.y[:, :, :], in0=self.mix[:, :, :], scalar=self.scalars[:, 2:3], in1=self.y[:, :, :],
                                   op0=ALU.mult, op1=ALU.add))
        v.tensor_tensor(k.h[:, :, :], k.h[:, :, :], self.y[:, :, :], ALU.add).then_inc(k.h_ready, 1)

    def fractions(self, v, own):
        k, S, L, rows = self.k, self.SEGMENTS, self.STEPS, self.ROWS
        p = self.p
        v.memset(self.d[:, :, :], 0.0)
        v.memset(self.starts[:, :, :], 0.0)
        own(v.memset(p[:, 0:2], 0.0))
        v.memset(self.starts[:, 0, 0:1], 1.0)
        v.memset(p[:, 1, 0, 0, :], 1.0)
        own(v.memset(p[:, 0, 0, 1, :], 1.0))
        v.wait_ge(self.vT_ready, 1)
        for part in (slice(0, IMAGES), slice(self.BACK, self.ROWS)):
            last = v.tensor_copy(self.d[part, :, :].rearrange("p s l -> p (s l)"), k.ps[part, 2, 0:SEQ])
        own(last)
        for t in range(1, L + 1):
            both = lambda x: x.rearrange("p c b s -> p (c b) s")
            v.tensor_tensor(both(self.grown[:, :, :, :]), both(p[:, t]), self.d[:, :, t - 1].unsqueeze(1).to_broadcast([rows, 4, S]), ALU.mult)
            v.tensor_tensor(self.turn[:, 0], p[:, t, 1], p[:, t - 1, 0], ALU.subtract)
            own(v.scalar_tensor_tensor(out=self.turn[:, 1], in0=p[:, t, 0], scalar=-1.0, in1=p[:, t - 1, 1], op0=ALU.mult, op1=ALU.subtract))
            own(v.tensor_tensor(p[:, t + 1], self.grown[:, :, :, :], self.turn[:, :, :, :], ALU.add))
        top = p[:, L + 1, :, 0, :]
        own(v.scalar_tensor_tensor(out=self.size[:, :, :], in0=top, scalar=-1.0, in1=top, op0=ALU.mult, op1=ALU.max))
        own(v.tensor_tensor(self.size[:, 0], self.size[:, 0], self.size[:, 1], ALU.add))
        own(v.reciprocal(self.size[:, 0], self.size[:, 0]))
        wide = self.size[:, 0].unsqueeze(1).to_broadcast([rows, 2, S])
        for which, t in ((0, L + 1), (1, L)):
            real, imaginary = p[:, t, 0], p[:, t, 1]
            to = lambda part, frm: self.maps[:, :, part, which, 2 * frm:2 * frm + 2].rearrange("p s b -> p b s")
            v.tensor_tensor(to(0, 0), real, wide, ALU.mult)
            v.scalar_tensor_tensor(out=to(0, 1), in0=imaginary, scalar=-1.0, in1=wide, op0=ALU.mult, op1=ALU.mult)
            v.tensor_tensor(to(1, 0), imaginary, wide, ALU.mult)
            last = v.tensor_tensor(to(1, 1), real, wide, ALU.mult)
        own(last)
        for s in range(S - 1):
            own(v.tensor_tensor(self.term[:, :, :], self.maps[:, s].rearrange("p a b c -> p (a b) c"),
                                self.starts[:, s, :].unsqueeze(1).to_broadcast([rows, 4, 4]), ALU.mult))
            own(v.tensor_reduce(self.starts[:, s + 1, :], self.term[:, :, :], AX.X, ALU.add))
        real, imaginary = (self.starts[:, :, 2 * c:2 * c + 2].rearrange("p s b -> p b s") for c in range(2))
        v.tensor_copy(self.coef[:, 0, 0:2], real)
        v.tensor_scalar(self.coef[:, 0, 2:4], imaginary, -1.0, None, ALU.mult)
        v.tensor_copy(self.coef[:, 1, 0:2], imaginary)
        own(v.tensor_copy(self.coef[:, 1, 2:4], real))
        for c in range(2):
            last = v.tensor_tensor(self.terms[:, c], p[:, 1:L + 2].rearrange("p t c b s -> p t (c b) s"),
                                   self.coef[:, c].unsqueeze(1).to_broadcast([rows, L + 1, 4, S]), ALU.mult)
        own(last)
        for c in range(2):
            last = v.tensor_reduce(self.whole[:, c], self.terms[:, c].rearrange("p t f s -> p t s f"), AX.X, ALU.add)
        own(last)
        now, before = (self.whole[:, :, 1:L + 1], self.whole[:, :, 0:L])
        for n, (x, y) in enumerate(((now, before), (before, before))):
            v.tensor_tensor(self.t1[:, 2 * n], x[:, 0], y[:, 0], ALU.mult)
            v.tensor_tensor(self.t2[:, 2 * n], x[:, 1], y[:, 1], ALU.mult)
        v.tensor_tensor(self.t1[:, 1], now[:, 1], before[:, 0], ALU.mult)
        own(v.tensor_tensor(self.t2[:, 1], now[:, 0], before[:, 1], ALU.mult))
        v.tensor_tensor(self.t1[:, 0], self.t1[:, 0], self.t2[:, 0], ALU.add)
        v.tensor_tensor(self.t1[:, 1], self.t1[:, 1], self.t2[:, 1], ALU.subtract)
        own(v.tensor_tensor(self.size2[:, :, :], self.t1[:, 2], self.t2[:, 2], ALU.add))
        own(v.reciprocal(self.size2[:, :, :], self.size2[:, :, :]))
        for c in range(2):
            last = v.tensor_tensor(self.hist[:, :, c].rearrange("p (s l) -> p l s", l=L), self.t1[:, c], self.size2[:, :, :], ALU.mult)
        last.then_inc(self.hist_ready, 1)

    def pool(self, g, own):
        pass



def build(nc, a, out):
    with ExitStack() as ctx:
        k = Chip(nc, ctx)
        stages = []
        for n, stage in enumerate(STAGES):
            with ExitStack() as k.stage_memory:
                stages.append(stage(k, a, n))
        out_stored = k.sem("out_stored")

        def start(eng, stage):
            if stage.norm > 0:
                eng.wait_ge(k.h_ready, stage.norm)
        block = ctx.enter_context(nc.Block())

        @block.sync
        def _(sp):
            sp.dma_start(k.ident[:, :], a["ident"]).then_inc(k.ident_loaded, 16)
            for stage in stages:
                stage.sync(sp)
            sp.wait_ge(k.h_ready, len(stages))
            sp.dma_start(out.rearrange("(j p) d -> p j d", p=P), k.h[:, :, :]).then_inc(out_stored, 16)
            sp.wait_ge(out_stored, 16)

        @block.tensor
        def _(pe):
            own = Own(pe, k.tensor_own)
            pe.wait_ge(k.ident_loaded, 16)
            for stage in stages:
                start(pe, stage)
                stage.tensor(pe, own)

        @block.scalar
        def _(act):
            own = Own(act, k.scalar_own)
            for stage in stages:
                start(act, stage)
                stage.scalar(act, own)

        @block.vector
        def _(dve):
            own = Own(dve, k.vector_own)
            for stage in stages:
                start(dve, stage)
                stage.vector(dve, own)

        @block.gpsimd
        def _(pool):
            own = Own(pool, k.pool_own)
            for stage in stages:
                start(pool, stage)
                stage.pool(pool, own)


def mamba_0(k, a, n):
    return Mamba(k, "l0", n, {x: a["m0_" + x] for x in ("in_T", "x_T", "dt_T", "out_T", "params", "norm_w", "final_w")}
                    | {"sel": a["row_sel"]}, 16, 48)


def mamba_1(k, a, n):
    return Mamba(k, "l1", n, {x: a["m1_" + x] for x in ("in_T", "x_T", "dt_T", "out_T", "params")} | {"sel": a["row_sel"]},
                 1, 12)


def experts_0(k, a, n):
    return Experts(k, "l0f", n, {x: a["e0_" + x] for x in ("router_T", "W1", "b1", "W2", "b2")} | {"rev": a["rev16"]},
                   16, 2, ACT.Gelu, True)


def experts_1(k, a, n):
    return GatedExperts(k, "l1f", n, {x: a["e1_" + x] for x in ("router_T", "gate_b", "W1", "W3", "W2", "b1", "b3", "b2")}
                        | {"rev8": a["rev8"], "rev4": a["rev4"]})


def attention_2(k, a, n):
    return ErfAttention(k, "l2a", n, {x: a["a2_" + x] for x in ("qkv_T", "proj_T", "cos", "sin", "mask")})


def attention_3(k, a, n):
    return Retention(k, "l3a", n, {x: a["a3_" + x] for x in ("qkv", "qk_b", "v_b", "mask")})


def neurons_2(k, a, n):
    return Neurons(k, "l2f", n, {x: a["n2_" + x] for x in ("key_w", "key_b", "emb", "F", "R")})


def tokenizer(k, a, n):
    return Tokenizer(k, "tok", n, {x: a["t_" + x] for x in ("patches0", "patches1", "patches2", "idx0", "idx1", "idx2", "W0_T", "W1_T",
                                                            "W2_T", "b", "stretch1", "stretch2", "fuse_T", "fuse_b")})


def experts_3(k, a, n):
    stage = Experts(k, "l3f", n, {x: a["e3_" + x] for x in ("router_T", "router_b", "W1", "b1", "W2", "b2")} | {"rev": a["rev8"]},
                    8, 1, ACT.Gelu_apprx_tanh, False)
    stage.tail = Resolvent(k, "bk", {x: a["r3_" + x] for x in ("rows", "scalars", "turned")}, stage.y)
    return stage


STAGES = (tokenizer, mamba_0, experts_0, mamba_1, experts_1, attention_2, neurons_2, attention_3, experts_3)



def stretch(short, long):
    at = np.clip((np.arange(long, dtype=np.float32) + np.float32(0.5)) * np.float32(short / long) - np.float32(0.5), 0, short - 1)
    low = np.floor(at).astype(np.int32)
    high = np.minimum(low + 1, short - 1)
    w = (at - low).astype(np.float32)
    m = np.zeros((short, long), np.float32)
    m[low, np.arange(long)] += 1 - w
    m[high, np.arange(long)] += w
    return m


def laid_out(x):
    a = {}
    c = np.ascontiguousarray
    a["ident"] = np.eye(P, dtype=np.float32)
    a["row_sel"] = c(np.tile(np.eye(BC, dtype=np.float32), (3, 1)))

    def mamba(p, in_w, conv_w, conv_b, dt_low, b_c, dt_w, dt_b, a_log, d, out_w):
        a[p + "in_T"] = c(in_w.transpose(0, 2, 1))
        a[p + "x_T"] = c(np.concatenate([dt_low, np.zeros((len(dt_low), BC_AT - dt_low.shape[1], INNER), np.float32), b_c], axis=1).transpose(0, 2, 1))
        a[p + "dt_T"] = c(dt_w.transpose(0, 2, 1))
        a[p + "out_T"] = c(out_w.transpose(0, 2, 1))
        a[p + "params"] = c(np.concatenate([conv_w[:, :, 0, :], conv_b[:, :, None], dt_b[:, :, None], d[:, :, None], a_log], axis=2))

    rank = 48
    mamba("m0_", x["L0_attn_in_proj_w"], x["L0_attn_conv_w"], x["L0_attn_conv_b"], x["L0_attn_x_proj_w"][:, :rank],
          x["L0_attn_x_proj_w"][:, rank:], x["L0_attn_dt_proj_w"], x["L0_attn_dt_proj_b"], x["L0_attn_A_log"],
          x["L0_attn_D"], x["L0_attn_out_proj_w"])
    a["m0_norm_w"] = c(x["L0_attn_norm_w"].reshape(-1, 2, DH).transpose(2, 0, 1))
    a["m0_final_w"] = x["L0_attn_final_norm_w"].reshape(1, D)
    mamba("m1_", *[x["L1_attn_" + y][None] for y in ("in_proj_w", "conv_w", "conv_b", "x_dt_w")],
          np.concatenate([x["L1_attn_x_b_w"], x["L1_attn_x_c_w"]], axis=0)[None],
          *[x["L1_attn_" + y][None] for y in ("dt_w", "dt_b", "A_log", "D_param", "out_proj_w")])

    for e in (4, 8, 16):
        a["rev%d" % e] = np.arange(e, 0, -1, dtype=np.float32).reshape(1, e)
    for p, q, router in (("e0_", "L0_ffn_", x["L0_ffn_Wr"].T), ("e3_", "L3_ffn_", x["L3_ffn_Wg"])):
        a[p + "router_T"] = c(router)
        a[p + "W1"], a[p + "W2"], a[p + "b2"] = x[q + "W1"], x[q + "W2"], x[q + "b2"]
        a[p + "b1"] = c(x[q + "b1"].reshape(-1, 2 * CHUNKS, P).transpose(2, 0, 1))

    parted = lambda w: np.concatenate([w[..., ::2], w[..., 1::2]], axis=-1)
    q = "L1_ffn_"
    with_shared = lambda y, z: np.concatenate([x[q + y], x[q + z][None]], axis=0)
    a["e1_router_T"], a["e1_gate_b"] = c(x[q + "gate_w"].T), x[q + "gate_b"].reshape(1, -1)
    a["e1_W1"], a["e1_W3"] = c(parted(with_shared("W1", "Ws1"))), c(parted(with_shared("W3", "Ws3")))
    a["e1_W2"], a["e1_b2"] = with_shared("W2", "Ws2"), with_shared("B2", "Bs2")
    for y, z, t in (("b1", "B1", "Bs1"), ("b3", "B3", "Bs3")):
        a["e1_" + y] = c(with_shared(z, t).reshape(-1, DH, 2).transpose(1, 0, 2))

    a["a2_qkv_T"] = c(np.concatenate([x["L2_attn_W" + y].T for y in "qkv"], axis=1))
    a["a2_proj_T"] = c(x["L2_attn_Wproj"].T)
    half = 8
    freq = np.float32(1.0) / np.float32(10000.0) ** (np.arange(half, dtype=np.float32) / np.float32(half))
    angle = (np.arange(SEQ, dtype=np.float32)[:, None] * freq[None, :]).astype(np.float32)
    by_tile = lambda t: c(t.reshape(2, P, -1).transpose(1, 0, 2).astype(np.float32))
    a["a2_cos"], a["a2_sin"] = by_tile(np.cos(angle)), by_tile(np.sin(angle))
    query, key = np.arange(SEQ)[None, :], np.arange(SEQ)[:, None]
    spans = lambda t: c(np.concatenate([t[0:P], t[P:, P:]], axis=1).astype(np.float32))
    a["a2_mask"] = spans(query >= key)
    decay = np.float32(0.99) ** np.maximum(query - key, 0).astype(np.float32)
    a["a3_mask"] = spans(np.where(query >= key, decay, np.float32(0)))
    a["a3_qkv"] = x["L3_attn_W_qkv"]
    a["a3_qk_b"] = c(x["L3_attn_b_qkv"][:2 * D].reshape(4, DH).T)
    a["a3_v_b"] = x["L3_attn_b_qkv"][2 * D:].reshape(1, D)

    q = "L2_ffn_"
    a["n2_key_w"] = c(np.concatenate([x[q + "W_fk"], x[q + "W_rk"]], axis=1))
    a["n2_key_b"] = np.concatenate([x[q + "b_fk"], x[q + "b_rk"]]).reshape(-1, 1)
    a["n2_emb"] = c(np.stack([x[q + "emb_fk"], x[q + "emb_rk"]], axis=1))
    beside = lambda t, m: c(t.reshape(-1, m, *t.shape[1:]).transpose(0, 2, 1, 3).reshape(t.shape[0] // m, t.shape[1], -1))
    a["n2_F"], a["n2_R"] = beside(x[q + "f_know"], Neurons.F_AT_ONCE), beside(x[q + "r_know"], Neurons.R_AT_ONCE)

    images = x["x"]
    for q, p in enumerate(Tokenizer.LEVELS):
        side = Tokenizer.SIDE // p
        a["t_patches%d" % q] = c(images.reshape(IMAGES, 3, side, p, side, p).transpose(2, 4, 0, 3, 5, 1).reshape(side * side, -1))
        a["t_idx%d" % q] = x["L0_tok_idx%d" % q]
        a["t_W%d_T" % q] = c(x["L0_tok_W%d" % q].T)
        if q:
            a["t_stretch%d" % q] = stretch(Tokenizer.LENGTHS[q], SEQ)
    a["t_b"] = c(np.stack([x["L0_tok_b%d" % q] for q in range(3)], axis=1))
    a["t_fuse_T"], a["t_fuse_b"] = c(x["L0_tok_Wf"].T), x["L0_tok_bf"].reshape(1, D)
    q = "L3_ffn_"
    a["e3_router_b"] = x[q + "bg"].reshape(1, -1)
    a["r3_rows"] = np.concatenate([x[q + "Wv"], x[q + "Wm"], x[q + "Wo"].reshape(-1), x[q + "bo"]]).reshape(1, -1)
    a["r3_scalars"] = np.stack([x[q + "bv"], x[q + "bm"], x[q + "bk_scale"]]).reshape(1, 3)
    a["r3_turned"] = c(np.eye(P, dtype=np.float32)[:, ::-1])
    return a


def kernel(**inputs):
    import concourse.bacc as bacc
    from concourse.bass_utils import run_bass_kernel_spmd

    x = {name: np.asarray(value) for name, value in inputs.items()}
    arrays = laid_out(x)
    nc = bacc.Bacc("TRN2", target_bir_lowering=False, num_devices=1)
    feeds, aps = {}, {}
    for name, value in arrays.items():
        value = np.ascontiguousarray(value)
        feeds["in_" + name] = value
        aps[name] = nc.dram_tensor("in_" + name, value.shape, mybir.dt.from_np(value.dtype), kind="ExternalInput").ap()
    out = nc.dram_tensor("out_0_dram", (TOKENS, D), F32, kind="ExternalOutput").ap()
    build(nc, aps, out)
    r = run_bass_kernel_spmd(nc, [feeds], core_ids=[0])
    return r.results[0]["out_0_dram"].reshape(IMAGES, SEQ, D)
```
